# Optimizing a Trainium2 kernel written in Bass

```python
import numpy as np
import jax
import jax.numpy as jnp

def _softmax(x, axis=-1):
    return jax.nn.softmax(x, axis=axis)

def _gelu(x):
    return jax.nn.gelu(x, approximate=True)

def _silu(x):
    return jax.nn.silu(x)

def _sigmoid(x):
    return jax.nn.sigmoid(x)

def _layernorm(x, axis=-1, eps=1e-05):
    m = jnp.mean(x, axis=axis, keepdims=True)
    v = jnp.var(x, axis=axis, keepdims=True)
    return (x - m) / jnp.sqrt(v + eps)

def _scatter_add(tgt, idx, src, axis=0):
    return tgt.at[idx].add(src)

def _segment_sum(src, seg, n):
    return jax.ops.segment_sum(src, seg, n)
kernel_name = 'mk_conv_attn_hybrid_d4_conv_nchw256_r2_ca5b5f'

def setup_inputs(seed: int=0):
    np.random.seed(seed)
    _w = jnp.asarray

    def _rec_inputs():
        import jax
        import jax.numpy as jnp
        _gk = jax.random.key(seed)
        x = 7.22e-05 + 1 * jax.random.normal(jax.random.fold_in(_gk, 1), (8, 128, 32, 32), jnp.float32)
        return x
    x = _rec_inputs()

    def _L0_conv_setup():
        import jax, jax.numpy as jnp
        import numpy as np
        C = 128
        CQ = C // 2
        key = jax.random.key(seed)
        ks = jax.random.split(key, 8)
        B, H, W = (8, 32, 32)
        x = jax.random.normal(ks[0], (B, C, H, W), dtype=jnp.float32)
        s = 0.02
        Wq = jax.random.normal(ks[1], (CQ, C), dtype=jnp.float32) * s
        bq = jax.random.normal(ks[2], (CQ,), dtype=jnp.float32) * s
        Wk = jax.random.normal(ks[3], (CQ, C), dtype=jnp.float32) * s
        bk = jax.random.normal(ks[4], (CQ,), dtype=jnp.float32) * s
        Wv = jax.random.normal(ks[5], (C, C), dtype=jnp.float32) * s
        bv = jax.random.normal(ks[6], (C,), dtype=jnp.float32) * s
        gamma = jax.random.normal(ks[7], (1,), dtype=jnp.float32) * 0.5
        return {'x': x, 'Wq': Wq, 'bq': bq, 'Wk': Wk, 'bk': bk, 'Wv': Wv, 'bv': bv, 'gamma': gamma}
    _L0_conv_all = _L0_conv_setup()
    _L0_conv_in = {k: v for k, v in _L0_conv_all.items() if k in ('Wq', 'bq', 'Wk', 'bk', 'Wv', 'bv', 'gamma')}
    del _L0_conv_all

    def _L1_conv_setup():
        import jax, jax.numpy as jnp
        import numpy as np
        NC = 32
        T = 5
        EPS = 1e-05

        def _iternorm_whiten(X):
            B, C, H, W = X.shape
            g = C // NC
            xv = jnp.transpose(X, (1, 0, 2, 3)).reshape(g, NC, -1)
            m = xv.shape[-1]
            mean = xv.mean(-1, keepdims=True)
            xc = xv - mean
            I = jnp.eye(NC, dtype=X.dtype)
            Sigma = EPS * I + jnp.einsum('gdm,gem->gde', xc, xc) / m
            rTr = 1.0 / jnp.trace(Sigma, axis1=1, axis2=2)[:, None, None]
            Sn = Sigma * rTr
            P = jnp.broadcast_to(I, (g, NC, NC))
            for _ in range(T):
                P3 = P @ P @ P
                P = 1.5 * P - 0.5 * (P3 @ Sn)
            wm = P * jnp.sqrt(rTr)
            xn = wm @ xc
            Xn = jnp.transpose(xn.reshape(C, B, H, W), (1, 0, 2, 3))
            return Xn
        key = jax.random.key(seed)
        x = jax.random.normal(key, (32, 128, 56, 56), dtype=jnp.float32)
        weight = jnp.ones((1, 128, 1, 1), dtype=jnp.float32)
        bias = jnp.zeros((1, 128, 1, 1), dtype=jnp.float32)
        return {'x': x, 'weight': weight, 'bias': bias}
    _L1_conv_all = _L1_conv_setup()
    _L1_conv_in = {k: v for k, v in _L1_conv_all.items() if k in ('weight', 'bias')}
    del _L1_conv_all

    def _L2_attn_setup():
        import jax, jax.numpy as jnp
        import numpy as np
        EPS = 1e-05

        def _layernorm(x, weight, bias):
            mean = jnp.mean(x, axis=-1, keepdims=True)
            std = jnp.std(x, axis=-1, keepdims=True, ddof=1)
            out = (x - mean) / (std + EPS)
            return weight * out + bias
        key = jax.random.key(seed)
        B, N, C = (4, 16384, 128)
        H, hc = (8, C // 8)
        kx, = jax.random.split(key, 1)
        x = jax.random.normal(kx, (B, N, C), dtype=jnp.float32)
        return {'x': x, 'kln_weight': jnp.ones((H, 1, hc), dtype=jnp.float32), 'kln_bias': jnp.zeros((H, 1, hc), dtype=jnp.float32), 'vln_weight': jnp.ones((H, 1, hc), dtype=jnp.float32), 'vln_bias': jnp.zeros((H, 1, hc), dtype=jnp.float32)}
    _L2_attn_all = _L2_attn_setup()
    _L2_attn_in = {k: v for k, v in _L2_attn_all.items() if k in ('kln_weight', 'kln_bias', 'vln_weight', 'vln_bias')}
    del _L2_attn_all

    def _L2_ffn_setup():
        import jax, jax.numpy as jnp
        import numpy as np
        TOP_K = 2
        LN_EPS = 1e-05
        key = jax.random.key(seed)
        ks = jax.random.split(key, 8)
        B, S, D, E, H = (16, 512, 128, 8, 512)
        x = jax.random.normal(ks[0], (B, S, D), dtype=jnp.float32)
        Wr = jax.random.normal(ks[1], (D, E), dtype=jnp.float32) * 0.1
        br = jnp.zeros((E,), dtype=jnp.float32)
        ln_g = jnp.ones((E, D), dtype=jnp.float32)
        ln_b = jnp.zeros((E, D), dtype=jnp.float32)
        W1 = jax.random.normal(ks[2], (E, D, H), dtype=jnp.float32) * (1.0 / np.sqrt(D))
        b1 = jnp.zeros((E, H), dtype=jnp.float32)
        W2 = jax.random.normal(ks[3], (E, H, D), dtype=jnp.float32) * (1.0 / np.sqrt(H))
        b2 = jnp.zeros((E, D), dtype=jnp.float32)
        return {'x': x, 'Wr': Wr, 'br': br, 'ln_g': ln_g, 'ln_b': ln_b, 'W1': W1, 'b1': b1, 'W2': W2, 'b2': b2}
    _L2_ffn_all = _L2_ffn_setup()
    _L2_ffn_in = {k: v for k, v in _L2_ffn_all.items() if k in ('Wr', 'br', 'ln_g', 'ln_b', 'W1', 'b1', 'W2', 'b2')}
    del _L2_ffn_all

    def _L3_attn_setup():
        import jax, jax.numpy as jnp
        import numpy as np
        INPUT_DIM = 128
        OUTPUT_DIM = 128
        HEAD_DIM = 32
        N_HEADS = INPUT_DIM // HEAD_DIM
        WINDOW = 32
        BLOCK_TYPE = 'SW'

        def _generate_mask(w, p, padding_size, shift, block_type):
            mask = np.zeros((w, p, p), dtype=bool)
            if block_type == 'W':
                s = p - padding_size
                mask[-1, :s, s:] = True
                mask[-1, s:, :s] = True
            elif padding_size + shift <= p:
                s = p - padding_size - shift
                mask[-1, :s, s:] = True
                mask[-1, s:s + padding_size, :s] = True
                mask[-1, s:s + padding_size, s + padding_size:] = True
                mask[-1, s + padding_size:, :s + padding_size] = True
            else:
                t = p - shift
                s = p - (padding_size - t)
                mask[-1, :t, t:] = True
                mask[-1, t:, :t] = True
                mask[-2, :s, s:] = True
                mask[-2, s:, :s] = True
            return mask
        key = jax.random.key(seed)
        ks = jax.random.split(key, 6)
        x = jax.random.normal(ks[0], (8, 8192, INPUT_DIM), dtype=jnp.float32)
        w_qkv = jax.random.normal(ks[1], (3 * INPUT_DIM, INPUT_DIM), dtype=jnp.float32) * 0.02
        b_qkv = jnp.zeros((3 * INPUT_DIM,), dtype=jnp.float32)
        rel_pos = jax.random.normal(ks[2], (N_HEADS, 2 * WINDOW - 1), dtype=jnp.float32) * 0.02
        w_out = jax.random.normal(ks[3], (OUTPUT_DIM, INPUT_DIM), dtype=jnp.float32) * 0.02
        b_out = jnp.zeros((OUTPUT_DIM,), dtype=jnp.float32)
        return {'x': x, 'w_qkv': w_qkv, 'b_qkv': b_qkv, 'rel_pos': rel_pos, 'w_out': w_out, 'b_out': b_out}
    _L3_attn_all = _L3_attn_setup()
    _L3_attn_in = {k: v for k, v in _L3_attn_all.items() if k in ('w_qkv', 'b_qkv', 'rel_pos', 'w_out', 'b_out')}
    del _L3_attn_all

    def _L3_ffn_setup():
        import jax, jax.numpy as jnp
        import numpy as np
        N_EXPERTS = 8
        TOP_K = 2
        key = jax.random.key(seed)
        ks = jax.random.split(key, 5)
        B, T, C, E, H = (8, 1024, 128, 8, 341)
        scale = 1.0 / np.sqrt(C)
        return {'x': jax.random.normal(ks[0], (B, T, C), dtype=jnp.float32), 'router_w': jax.random.normal(ks[1], (E, C), dtype=jnp.float32) * scale, 'w1': jax.random.normal(ks[2], (E, H, C), dtype=jnp.float32) * scale, 'w2': jax.random.normal(ks[3], (E, C, H), dtype=jnp.float32) * (1.0 / np.sqrt(H)), 'w3': jax.random.normal(ks[4], (E, H, C), dtype=jnp.float32) * scale}
    _L3_ffn_all = _L3_ffn_setup()
    _L3_ffn_in = {k: v for k, v in _L3_ffn_all.items() if k in ('router_w', 'w1', 'w2', 'w3')}
    del _L3_ffn_all
    return {'x': x, 'L0_conv_Wq': _L0_conv_in['Wq'], 'L0_conv_bq': _L0_conv_in['bq'], 'L0_conv_Wk': _L0_conv_in['Wk'], 'L0_conv_bk': _L0_conv_in['bk'], 'L0_conv_Wv': _L0_conv_in['Wv'], 'L0_conv_bv': _L0_conv_in['bv'], 'L0_conv_gamma': _L0_conv_in['gamma'], 'L1_conv_weight': _L1_conv_in['weight'], 'L1_conv_bias': _L1_conv_in['bias'], 'L2_attn_kln_weight': _L2_attn_in['kln_weight'], 'L2_attn_kln_bias': _L2_attn_in['kln_bias'], 'L2_attn_vln_weight': _L2_attn_in['vln_weight'], 'L2_attn_vln_bias': _L2_attn_in['vln_bias'], 'L2_ffn_Wr': _L2_ffn_in['Wr'], 'L2_ffn_br': _L2_ffn_in['br'], 'L2_ffn_ln_g': _L2_ffn_in['ln_g'], 'L2_ffn_ln_b': _L2_ffn_in['ln_b'], 'L2_ffn_W1': _L2_ffn_in['W1'], 'L2_ffn_b1': _L2_ffn_in['b1'], 'L2_ffn_W2': _L2_ffn_in['W2'], 'L2_ffn_b2': _L2_ffn_in['b2'], 'L3_attn_w_qkv': _L3_attn_in['w_qkv'], 'L3_attn_b_qkv': _L3_attn_in['b_qkv'], 'L3_attn_rel_pos': _L3_attn_in['rel_pos'], 'L3_attn_w_out': _L3_attn_in['w_out'], 'L3_attn_b_out': _L3_attn_in['b_out'], 'L3_ffn_router_w': _L3_ffn_in['router_w'], 'L3_ffn_w1': _L3_ffn_in['w1'], 'L3_ffn_w2': _L3_ffn_in['w2'], 'L3_ffn_w3': _L3_ffn_in['w3']}

def reference(x, L0_conv_Wq, L0_conv_bq, L0_conv_Wk, L0_conv_bk, L0_conv_Wv, L0_conv_bv, L0_conv_gamma, L1_conv_weight, L1_conv_bias, L2_attn_kln_weight, L2_attn_kln_bias, L2_attn_vln_weight, L2_attn_vln_bias, L2_ffn_Wr, L2_ffn_br, L2_ffn_ln_g, L2_ffn_ln_b, L2_ffn_W1, L2_ffn_b1, L2_ffn_W2, L2_ffn_b2, L3_attn_w_qkv, L3_attn_b_qkv, L3_attn_rel_pos, L3_attn_w_out, L3_attn_b_out, L3_ffn_router_w, L3_ffn_w1, L3_ffn_w2, L3_ffn_w3):
    import jax
    import jax.numpy as jnp

    def _L0_conv_ref(x, Wq, bq, Wk, bk, Wv, bv, gamma):
        import jax, jax.numpy as jnp
        import numpy as np
        C = 128
        CQ = C // 2
        B, Ch, H, W = x.shape
        N = H * W
        xf = x.reshape(B, Ch, N)
        q = jnp.einsum('oc,bcn->bon', Wq, xf) + bq[None, :, None]
        k = jnp.einsum('oc,bcn->bon', Wk, xf) + bk[None, :, None]
        v = jnp.einsum('oc,bcn->bon', Wv, xf) + bv[None, :, None]
        scores = jnp.einsum('bcm,bcn->bmn', q, k)
        attn = jax.nn.softmax(scores, axis=1)
        out = jnp.einsum('bcn,bmn->bcm', v, attn)
        return gamma * out.reshape(B, Ch, H, W) + x

    def _L1_conv_ref(x, weight, bias):
        import jax, jax.numpy as jnp
        import numpy as np
        NC = 32
        T = 5
        EPS = 1e-05

        def _iternorm_whiten(X):
            B, C, H, W = X.shape
            g = C // NC
            xv = jnp.transpose(X, (1, 0, 2, 3)).reshape(g, NC, -1)
            m = xv.shape[-1]
            mean = xv.mean(-1, keepdims=True)
            xc = xv - mean
            I = jnp.eye(NC, dtype=X.dtype)
            Sigma = EPS * I + jnp.einsum('gdm,gem->gde', xc, xc) / m
            rTr = 1.0 / jnp.trace(Sigma, axis1=1, axis2=2)[:, None, None]
            Sn = Sigma * rTr
            P = jnp.broadcast_to(I, (g, NC, NC))
            for _ in range(T):
                P3 = P @ P @ P
                P = 1.5 * P - 0.5 * (P3 @ Sn)
            wm = P * jnp.sqrt(rTr)
            xn = wm @ xc
            Xn = jnp.transpose(xn.reshape(C, B, H, W), (1, 0, 2, 3))
            return Xn
        return _iternorm_whiten(x) * weight + bias

    def _L2_attn_ref(x, kln_weight, kln_bias, vln_weight, vln_bias):
        import jax, jax.numpy as jnp
        import numpy as np
        EPS = 1e-05

        def _layernorm(x, weight, bias):
            mean = jnp.mean(x, axis=-1, keepdims=True)
            std = jnp.std(x, axis=-1, keepdims=True, ddof=1)
            out = (x - mean) / (std + EPS)
            return weight * out + bias
        B, N, C = x.shape
        H = kln_weight.shape[0]
        hc = C // H
        qkv = x.reshape(B, N, H, hc).transpose(0, 2, 1, 3)
        q = qkv
        k = _layernorm(qkv, kln_weight, kln_bias)
        v = _layernorm(qkv, vln_weight, vln_bias)
        kv = jnp.einsum('bhnd,bhne->bhde', k, v) / N
        out = jnp.einsum('bhnd,bhde->bhne', q, kv)
        out = out.transpose(0, 2, 1, 3).reshape(B, N, C)
        return out + x

    def _L2_ffn_ref(x, Wr, br, ln_g, ln_b, W1, b1, W2, b2):
        import jax, jax.numpy as jnp
        import numpy as np
        TOP_K = 2
        LN_EPS = 1e-05
        B, S, D = x.shape
        N = B * S
        xt = x.reshape(N, D)
        logits = xt @ Wr + br
        probs = jax.nn.softmax(logits, axis=-1)
        top_p, top_idx = jax.lax.top_k(probs, TOP_K)
        weights = top_p / top_p.sum(axis=-1, keepdims=True)
        mu = xt.mean(axis=-1, keepdims=True)
        var = ((xt - mu) ** 2).mean(axis=-1, keepdims=True)
        xn = (xt - mu) * jax.lax.rsqrt(var + LN_EPS)
        xe = xn[None, :, :] * ln_g[:, None, :] + ln_b[:, None, :]
        h = jax.nn.gelu(jnp.einsum('end,edh->enh', xe, W1) + b1[:, None, :], approximate=False)
        y = jnp.einsum('enh,ehd->end', h, W2) + b2[:, None, :]
        y_tok = jnp.transpose(y, (1, 0, 2))
        sel = jnp.take_along_axis(y_tok, top_idx[:, :, None], axis=1)
        out = (weights[:, :, None] * sel).sum(axis=1)
        return out.reshape(B, S, D)

    def _L3_attn_ref(x, w_qkv, b_qkv, rel_pos, w_out, b_out):
        import jax, jax.numpy as jnp
        import numpy as np
        INPUT_DIM = 128
        OUTPUT_DIM = 128
        HEAD_DIM = 32
        N_HEADS = INPUT_DIM // HEAD_DIM
        WINDOW = 32
        BLOCK_TYPE = 'SW'

        def _generate_mask(w, p, padding_size, shift, block_type):
            mask = np.zeros((w, p, p), dtype=bool)
            if block_type == 'W':
                s = p - padding_size
                mask[-1, :s, s:] = True
                mask[-1, s:, :s] = True
            elif padding_size + shift <= p:
                s = p - padding_size - shift
                mask[-1, :s, s:] = True
                mask[-1, s:s + padding_size, :s] = True
                mask[-1, s:s + padding_size, s + padding_size:] = True
                mask[-1, s + padding_size:, :s + padding_size] = True
            else:
                t = p - shift
                s = p - (padding_size - t)
                mask[-1, :t, t:] = True
                mask[-1, t:, :t] = True
                mask[-2, :s, s:] = True
                mask[-2, s:, :s] = True
            return mask
        b, n, c = x.shape
        p = WINDOW
        pad = -n % p
        if pad:
            x = jnp.pad(x, ((0, 0), (0, pad), (0, 0)))
        shift = p // 2
        if BLOCK_TYPE != 'W':
            x = jnp.roll(x, -shift, axis=1)
        w = x.shape[1] // p
        xw = x.reshape(b, w, p, c)
        qkv = xw @ w_qkv.T + b_qkv
        qkv = qkv.reshape(b, w, p, 3, N_HEADS, HEAD_DIM)
        q, k, v = (qkv[..., 0, :, :], qkv[..., 1, :, :], qkv[..., 2, :, :])
        scale = HEAD_DIM ** (-0.5)
        sim = jnp.einsum('bwphd,bwqhd->bhwpq', q, k) * scale
        idx = np.arange(p)[:, None] - np.arange(p)[None, :] + p - 1
        sim = sim + rel_pos[:, idx][None, :, None]
        mask = jnp.asarray(_generate_mask(w, p, pad, shift, BLOCK_TYPE))
        sim = jnp.where(mask[None, None], -jnp.inf, sim)
        probs = jax.nn.softmax(sim, axis=-1)
        out = jnp.einsum('bhwpq,bwqhd->bwphd', probs, v)
        out = out.reshape(b, w, p, N_HEADS * HEAD_DIM)
        out = out @ w_out.T + b_out
        out = out.reshape(b, w * p, OUTPUT_DIM)
        if BLOCK_TYPE != 'W':
            out = jnp.roll(out, shift, axis=1)
        return out[:, :n]

    def _L3_ffn_ref(x, router_w, w1, w2, w3):
        import jax, jax.numpy as jnp
        import numpy as np
        N_EXPERTS = 8
        TOP_K = 2
        B, T, C = x.shape
        flat = x.reshape(-1, C)
        logits = flat @ router_w.T
        probs = jax.nn.softmax(logits, axis=-1)
        topk_probs, topk_idx = jax.lax.top_k(probs, TOP_K)
        topk_probs = topk_probs / (jnp.sum(topk_probs, axis=-1, keepdims=True) + 1e-09)
        onehot = jax.nn.one_hot(topk_idx, N_EXPERTS, dtype=flat.dtype)
        gates = jnp.einsum('nk,nke->ne', topk_probs, onehot)
        h1 = jnp.einsum('nc,ehc->neh', flat, w1)
        h3 = jnp.einsum('nc,ehc->neh', flat, w3)
        h = jax.nn.silu(h1) * h3
        y = jnp.einsum('neh,ech->nec', h, w2)
        out = jnp.einsum('ne,nec->nc', gates, y)
        return out.reshape(B, T, C)

    def _gn(v, G=32, eps=1e-05):
        B_, C_, H_, W_ = v.shape
        g = v.reshape(B_, G, C_ // G, H_, W_)
        m = jnp.mean(g, axis=(2, 3, 4), keepdims=True)
        s = jnp.var(g, axis=(2, 3, 4), keepdims=True)
        return ((g - m) / jnp.sqrt(s + eps)).reshape(v.shape)

    def _ln_c(v, eps=1e-06):
        m = jnp.mean(v, axis=1, keepdims=True)
        s = jnp.var(v, axis=1, keepdims=True)
        return (v - m) / jnp.sqrt(s + eps)

    def _ln_t(v, eps=1e-05):
        m = jnp.mean(v, axis=-1, keepdims=True)
        s = jnp.var(v, axis=-1, keepdims=True)
        return (v - m) / jnp.sqrt(s + eps)

    def _to_tokens(v):
        B_, C_, H_, W_ = v.shape
        return v.reshape(B_, C_, H_ * W_).transpose(0, 2, 1)

    def _from_tokens(t, like):
        B_, C_, H_, W_ = like.shape
        return t.transpose(0, 2, 1).reshape(B_, C_, H_, W_)
    x = _L0_conv_ref(x, L0_conv_Wq, L0_conv_bq, L0_conv_Wk, L0_conv_bk, L0_conv_Wv, L0_conv_bv, L0_conv_gamma)
    x = _L1_conv_ref(x, L1_conv_weight, L1_conv_bias)
    t = _to_tokens(x)
    t = t + _L2_attn_ref(_ln_t(t), L2_attn_kln_weight, L2_attn_kln_bias, L2_attn_vln_weight, L2_attn_vln_bias)
    t = t + _L2_ffn_ref(_ln_t(t), L2_ffn_Wr, L2_ffn_br, L2_ffn_ln_g, L2_ffn_ln_b, L2_ffn_W1, L2_ffn_b1, L2_ffn_W2, L2_ffn_b2)
    t = t + _L3_attn_ref(_ln_t(t), L3_attn_w_qkv, L3_attn_b_qkv, L3_attn_rel_pos, L3_attn_w_out, L3_attn_b_out)
    t = t + _L3_ffn_ref(_ln_t(t), L3_ffn_router_w, L3_ffn_w1, L3_ffn_w2, L3_ffn_w3)
    x = _from_tokens(t, x)
    return x

_drawn_inputs = setup_inputs


def setup_inputs(seed=0):
    import zlib

    import numpy as np

    out = dict(_drawn_inputs(seed))
    spreads = {'L1_conv_weight': (1.0, 0.2),
     'L1_conv_bias': (0.0, 0.1),
     'L2_attn_kln_weight': (1.0, 0.2),
     'L2_attn_kln_bias': (0.0, 0.1),
     'L2_attn_vln_weight': (1.0, 0.2),
     'L2_attn_vln_bias': (0.0, 0.1),
     'L2_ffn_br': (0.0, 0.1),
     'L2_ffn_ln_g': (1.0, 0.2),
     'L2_ffn_ln_b': (0.0, 0.348),
     'L2_ffn_b1': (0.0, 0.358),
     'L2_ffn_b2': (0.0, 0.1),
     'L3_attn_b_qkv': (0.0, 0.669),
     'L3_attn_b_out': (0.0, 0.1)}
    factors = {'L0_conv_Wq': 8.0,
     'L0_conv_bq': 64.0,
     'L0_conv_Wk': 8.0,
     'L0_conv_bk': 8.0,
     'L0_conv_Wv': 8.0,
     'L0_conv_bv': 22.867,
     'L3_attn_w_qkv': 8.0,
     'L3_attn_rel_pos': 8.0,
     'L3_attn_w_out': 4.866}
    for name, (base, spread) in spreads.items():
        noise = np.random.default_rng([zlib.crc32(name.encode()), seed]).standard_normal(out[name].shape)
        drawn = base * np.exp(spread * noise) if base else spread * noise
        out[name] = jnp.asarray(drawn.astype(out[name].dtype))
    for name, factor in factors.items():
        out[name] = (out[name] * factor).astype(out[name].dtype)
    return out
```

```python
from contextlib import ExitStack

import concourse.bass as bass
from concourse import mybir

ALU = mybir.AluOpType
ACT = mybir.ActivationFunctionType
AX = mybir.AxisListType
F32 = mybir.dt.float32
BF16 = mybir.dt.bfloat16
I32 = mybir.dt.int32

P = 128
B, C, N = 8, 128, 1024
NT = N // P
TT = B * NT
CQ = C // 2
HALF = 512


class Tools:

    def __init__(self, nc, ctx):
        self.nc, self.ctx = nc, ctx

    def sbuf(self, name, shape, dtype=F32):
        return self.ctx.enter_context(self.nc.sbuf_tensor(name, shape, dtype))

    def psum(self, name, shape, dtype=F32):
        return self.ctx.enter_context(self.nc.psum_tensor(name, shape, dtype))

    def sem(self, name):
        return self.ctx.enter_context(self.nc.semaphore(name))


class ClearedTools(Tools):

    def __init__(self, nc, ctx):
        super().__init__(nc, ctx)
        self.sems = []
        ctx.callback(self.clear)

    def clear(self):
        self.nc.clear_and_free_semaphores(self.sems)
        self.nc.all_engine_barrier()

    def sem(self, name):
        self.sems.append(self.nc.alloc_semaphore(name))
        return self.sems[-1]


class Steps:

    def __init__(self, engine, sem):
        self.engine, self.sem, self.n, self.base, self.per = engine, sem, 0, 0, None

    def round(self, i):
        if self.per is None and self.n:
            self.per = self.n
        if self.per is not None:
            assert self.n == self.per
            self.base = i * self.per
        self.n = 0

    def did(self, instruction):
        instruction.then_inc(self.sem, 1)
        self.n += 1

    def settle(self):
        self.engine.wait_ge(self.sem, self.base + self.n)

    def then(self, instruction):
        self.did(instruction)
        self.settle()


def row_to_all(ap, parts=P):
    return ap.partition_broadcast(parts)


def make_identity(pool, steps, tile):
    steps.then(pool.memset(tile, 0.0))
    steps.then(pool.affine_select(out=tile, in_=tile, compare_op=ALU.not_equal, fill=1.0, base=0,
                                  pattern=[[-1, P]], channel_multiplier=1))



def conv_attention(nc, ins, ident, feats, stats, sorted_rows):
    x = ins["x"].rearrange("b c h w -> b c (h w)")
    with ExitStack() as ctx:
        t = ClearedTools(nc, ctx)
        xin = [t.sbuf(f"xin{i}", [P, N]) for i in range(2)]
        wrow = [t.sbuf(f"wrow{i}", [P, C]) for i in range(3)]
        wT = [t.sbuf(f"wT{i}", [P, P]) for i in range(3)]
        bq = t.sbuf("bq", [P, 1])
        bk = t.sbuf("bk", [P, 1])
        bv = t.sbuf("bv", [P, C])
        gamma = t.sbuf("gamma", [P, 1])
        q = [t.sbuf(f"q{i}", [P, N]) for i in range(2)]
        k = [t.sbuf(f"k{i}", [P, N]) for i in range(2)]
        v = [t.sbuf(f"v{i}", [P, NT, C]) for i in range(2)]
        probs = [t.sbuf(f"probs{i}", [P, N]) for i in range(2)]
        vs = [t.sbuf(f"vs{i}", [P, C]) for i in range(2)]
        nmax = [t.sbuf(f"nmax{i}", [P, 1]) for i in range(2)]
        zsum = [t.sbuf(f"zsum{i}", [P, 1]) for i in range(2)]
        rz = [t.sbuf(f"rz{i}", [P, 1]) for i in range(2)]
        score = [t.psum(f"score{i}", [P, N]) for i in range(2)]
        out = t.psum("attended", [P, N])
        proj = [t.psum(f"proj{i}", [P, HALF]) for i in range(2)]

        weights_loaded = t.sem("weights_loaded")
        x_loaded = [t.sem(f"x_loaded{i}") for i in range(2)]
        weights_turned = t.sem("weights_turned")
        weights_ready = t.sem("weights_ready")
        proj_ready = t.sem("proj_ready")
        qk_taken = t.sem("qk_taken")
        v_taken = t.sem("v_taken")
        score_ready = t.sem("score_ready")
        max_ready = t.sem("max_ready")
        exp_done = t.sem("exp_done")
        vs_ready = t.sem("vs_ready")
        av_done = t.sem("av_done")
        feats_ready = t.sem("feats_ready")
        rz_ready = t.sem("rz_ready")
        stats_ready = t.sem("stats_ready")
        zeros = t.sbuf("zeros", [P, 8 * C])
        zeroed = t.sem("zeroed")
        cleared = t.sem("cleared")
        block = ctx.enter_context(nc.Block())

        @block.sync
        def _(sp):
            for w, name in ((0, "L0_conv_Wq"), (1, "L0_conv_Wk")):
                for r in range(2):
                    sp.dma_start(wrow[w][CQ * r:CQ * r + CQ, :], ins[name]).then_inc(weights_loaded, 16)
            sp.dma_start(wrow[2][:, :], ins["L0_conv_Wv"]).then_inc(weights_loaded, 16)
            for i in range(2):
                sp.dma_start(xin[i][:, :], x[i]).then_inc(x_loaded[i], 16)
            for tile, name in ((bq, "L0_conv_bq"), (bk, "L0_conv_bk")):
                for r in range(2):
                    sp.dma_start(tile[CQ * r:CQ * r + CQ, :],
                                 ins[name].rearrange("(c a) -> c a", a=1)).then_inc(weights_loaded, 16)
            sp.dma_start(bv[:, :], row_to_all(ins["L0_conv_bv"])).then_inc(weights_loaded, 16)
            sp.dma_start(gamma[:, :], row_to_all(ins["L0_conv_gamma"])).then_inc(weights_loaded, 16)
            for b in range(2, B):
                sp.wait_ge(feats_ready, b - 1)
                sp.dma_start(xin[b % 2][:, :], x[b]).then_inc(x_loaded[b % 2], 16)


        @block.gpsimd
        def _(pool):
            pool.memset(zeros[:, :], 0.0).then_inc(zeroed, 1)
            pool.wait_ge(zeroed, 1)
            for rows in sorted_rows:
                for at in range(0, SLOTS, 8 * P):
                    pool.dma_start(rows[at:at + 8 * P, :].rearrange("(p k) c -> p (k c)", p=P),
                                   zeros[:, :]).then_inc(cleared, 16)
            pool.wait_ge(cleared, 16 * len(sorted_rows) * (SLOTS // (8 * P)))

        @block.tensor
        def _(pe):
            pe.wait_ge(weights_loaded, 160 + 16)
            for i in range(3):
                turned = pe.transpose(proj[0][:, P * i:P * i + P], wrow[i][:, :], ident[:, :])
            turned.then_inc(weights_turned, 1)
            pe.wait_ge(weights_ready, 1)

            def project(b, par, item, first):
                if item == 0:
                    pe.wait_ge(x_loaded[par], (b - par) * 8 + 16)
                if item < 2:
                    if not first:
                        pe.wait_ge(v_taken, b * 2 - 1 + item)
                else:
                    pe.wait_ge(qk_taken, b * 4 + item - 1)
                bank = proj[item % 2]
                if item < 4:
                    w = wT[item // 2]
                    pe.matmul(bank[:, :], w[:, :], xin[par][:, HALF * (item % 2):HALF * (item % 2) + HALF],
                              start=True, stop=True).then_inc(proj_ready, 1)
                else:
                    for j in range(4):
                        at = P * (4 * (item - 4) + j)
                        done = pe.matmul(bank[:, P * j:P * j + P], xin[par][:, at:at + P], wT[2][:, :],
                                         start=True, stop=True)
                    done.then_inc(proj_ready, 1)

            def scores(b, par, n):
                if n == 0:
                    pe.wait_ge(qk_taken, b * 4 + 4)
                if not (isinstance(b, int) and b * NT + n < 2):
                    pe.wait_ge(exp_done, b * NT + n - 1)
                rows = slice(CQ * (n % 2), CQ * (n % 2) + CQ)
                for h in range(2):
                    done = pe.matmul(score[n % 2][:, HALF * h:HALF * h + HALF], k[par][rows, P * n:P * n + P],
                                     q[par][rows, HALF * h:HALF * h + HALF], start=True, stop=True)
                done.then_inc(score_ready, 1)

            def attend(b, n):
                pe.wait_ge(vs_ready, b * NT + n + 1)
                if n == 0 and not (isinstance(b, int) and b == 0):
                    pe.wait_ge(feats_ready, b)
                for h in range(2):
                    done = pe.matmul(out[:, HALF * h:HALF * h + HALF], vs[n % 2][:, :],
                                     probs[n % 2][:, HALF * h:HALF * h + HALF],
                                     start=(n == 0), stop=(n == NT - 1))
                done.then_inc(av_done, 1)

            def batch(b, par, first=False, last=False):
                for n in range(NT):
                    scores(b, par, n)
                    if n >= 2:
                        attend(b, n - 2)
                    elif not first:
                        attend(b - 1, NT + n - 2)
                    for item in {2: (0, 1), 3: (2, 3), 4: (4,), 5: (5,)}.get(n, ()) if not last else ():
                        project(b + 1, 1 - par, item, False)

            for item in range(6):
                project(0, 0, item, True)
            batch(0, 0, first=True)
            batch(1, 1)
            with pe.Fori(2, B - 3, 2) as b:
                batch(b, 0)
                batch(b + 1, 1)
            batch(B - 2, 0)
            batch(B - 1, 1, last=True)
            attend(B - 1, NT - 2)
            attend(B - 1, NT - 1)

        @block.vector
        def _(dve):
            dve.wait_ge(weights_turned, 1)
            for i in range(3):
                done = dve.tensor_copy(wT[i][:, :], proj[0][:, P * i:P * i + P])
            done.then_inc(weights_ready, 1)

            def take_values(b, par, h):
                dve.wait_ge(proj_ready, b * 6 + 5 + h)
                dve.tensor_tensor(v[par][:, 4 * h:4 * h + 4, :],
                                  proj[h][:, :].rearrange("p (a c) -> p a c", a=4),
                                  bv[:, :].unsqueeze(1).to_broadcast([P, 4, C]), ALU.add).then_inc(v_taken, 1)

            def row_max(b, n):
                dve.wait_ge(score_ready, b * NT + n + 1)
                dve.tensor_reduce(nmax[n % 2][:, :], score[n % 2][:, :], AX.X, ALU.max,
                                  negate=True).then_inc(max_ready, 1)

            def scale_values(b, par, n):
                dve.wait_ge(exp_done, b * NT + n + 1)
                if n % 4 == 0:
                    dve.wait_ge(v_taken, b * 2 + 1 + n // 4)
                dve.reciprocal(rz[n % 2][:, :], zsum[n % 2][:, :]).then_inc(rz_ready, 1)
                dve.wait_ge(rz_ready, b * NT + n + 1)
                dve.tensor_scalar(vs[n % 2][:, :], v[par][:, n, :], rz[n % 2][:, 0:1], None,
                                  ALU.mult).then_inc(vs_ready, 1)

            def finish(b, par):
                dve.wait_ge(av_done, b * NT + NT)
                dve.scalar_tensor_tensor(out=feats[:, bass.ds(b, 1), :].rearrange("p a n -> p (a n)"),
                                         in0=out[:, :], scalar=gamma[:, 0:1], in1=xin[par][:, :],
                                         op0=ALU.mult, op1=ALU.add).then_inc(feats_ready, 1)
                dve.wait_ge(feats_ready, b + 1)
                for h in range(2):
                    dve.bn_stats(stats[:, bass.ds(b * 2 + h, 1), :].rearrange("p a s -> p (a s)"),
                                 feats[:, bass.ds(b, 1), HALF * h:HALF * h + HALF].rearrange("p a n -> p (a n)"),
                                 ).then_inc(stats_ready, 1)

            def batch(b, par, first=False, last=False):
                for n in range(NT):
                    row_max(b, n)
                    if n >= 1:
                        scale_values(b, par, n - 1)
                    elif not first:
                        scale_values(b - 1, 1 - par, NT - 1)
                    if n == 1 and not first:
                        finish(b - 1, 1 - par)
                    if n in (5, 6) and not last:
                        take_values(b + 1, 1 - par, n - 5)

            take_values(0, 0, 0)
            take_values(0, 0, 1)
            batch(0, 0, first=True)
            batch(1, 1)
            with dve.Fori(2, B - 3, 2) as b:
                batch(b, 0)
                batch(b + 1, 1)
            batch(B - 2, 0)
            batch(B - 1, 1, last=True)
            scale_values(B - 1, 1, NT - 1)
            finish(B - 1, 1)

        @block.scalar
        def _(act):
            act.wait_ge(weights_loaded, 176)

            def take_projection(b, par, item):
                into, bias = ((q, bq), (k, bk))[item // 2]
                at = slice(HALF * (item % 2), HALF * (item % 2) + HALF)
                act.wait_ge(proj_ready, b * 6 + item + 1)
                act.activation(into[par][:, at], proj[item % 2][:, :], ACT.Identity,
                               bias=bias[:, 0:1]).then_inc(qk_taken, 1)

            def exponent(b, n):
                act.wait_ge(max_ready, b * NT + n + 1)
                if not (isinstance(b, int) and b * NT + n < 2):
                    act.wait_ge(av_done, b * NT + n - 1)
                act.activation(probs[n % 2][:, :], score[n % 2][:, :], ACT.Exp, bias=nmax[n % 2][:, 0:1],
                               accum_out=zsum[n % 2][:, 0:1]).then_inc(exp_done, 1)

            def batch(b, par, first=False, last=False):
                for n in range(NT):
                    exponent(b, n)
                    for item in {2: (0, 1), 3: (2, 3)}.get(n, ()) if not last else ():
                        take_projection(b + 1, 1 - par, item)

            for item in range(4):
                take_projection(0, 0, item)
            batch(0, 0, first=True)
            batch(1, 1)
            with act.Fori(2, B - 3, 2) as b:
                batch(b, 0)
                batch(b + 1, 1)
            batch(B - 2, 0)
            batch(B - 1, 1, last=True)



GROUP = 32
WHITEN_STEPS = 5
WHITEN_EPS = 1e-05


def whiten(nc, ins, ident, feats, stats, tokens):
    with ExitStack() as ctx:
        t = Tools(nc, ctx)
        centred = [t.sbuf(f"centred{i}", [P, N]) for i in range(2)]
        turned = [t.sbuf(f"turned{i}", [P, NT, C]) for i in range(2)]
        mean = t.sbuf("mean", [P, 2])
        negmean = t.sbuf("negmean", [P, 1])
        blocks = t.sbuf("blocks", [P, P])
        sigma = t.sbuf("sigma", [P, P])
        scratch = t.sbuf("scratch", [P, P])
        diag = t.sbuf("diag", [P, 1])
        rtrace = t.sbuf("rtrace", [P, 1])
        root = t.sbuf("root", [P, 1])
        power = [t.sbuf(f"power{i}", [P, P]) for i in range(3)]
        weight = t.sbuf("weight", [P, C])
        bias = t.sbuf("bias", [P, C])
        mix = t.sbuf("mix", [P, P])
        turn = [[t.psum(f"turn{i}{h}", [P, HALF]) for h in range(2)] for i in range(2)]
        cov = t.psum("cov", [P, HALF])
        small = t.psum("small", [P, HALF])

        params_loaded = t.sem("params_loaded")
        blocks_ready = t.sem("blocks_ready")
        centred_ready = t.sem("centred_ready")
        turn_ready = t.sem("turn_ready")
        turned_low = t.sem("turned_low")
        turned_high = t.sem("turned_high")
        cov_done = t.sem("cov_done")
        dve_steps = t.sem("dve_steps")
        pool_steps = t.sem("pool_steps")
        operand_ready = t.sem("operand_ready")
        product_ready = t.sem("product_ready")
        root_ready = t.sem("root_ready")
        root_asked = t.sem("root_asked")
        recentred = t.sem("recentred")
        mixed = t.sem("mixed")
        mixed_taken = t.sem("mixed_taken")
        block = ctx.enter_context(nc.Block())
        small_products = 1 + 3 * (WHITEN_STEPS - 1)

        @block.sync
        def _(sp):
            sp.dma_start(weight[:, :], row_to_all(ins["L1_conv_weight"].rearrange("a c h w -> (a c h w)"))
                         ).then_inc(params_loaded, 16)
            sp.dma_start(bias[:, :], row_to_all(ins["L1_conv_bias"].rearrange("a c h w -> (a c h w)"))
                         ).then_inc(params_loaded, 16)

        @block.gpsimd
        def _(pool):
            steps = Steps(pool, pool_steps)
            steps.then(pool.memset(blocks[:, :], 1.0))
            grid = blocks[:, :].rearrange("p (g c) -> p g c", g=P // GROUP)
            steps.then(pool.affine_select(out=grid, in_=grid, compare_op=ALU.is_ge, fill=0.0, base=0,
                                          pattern=[[-GROUP, P // GROUP], [0, GROUP]], channel_multiplier=1))
            pool.affine_select(out=grid, in_=grid, compare_op=ALU.is_ge, fill=0.0, base=GROUP - 1,
                               pattern=[[GROUP, P // GROUP], [0, GROUP]],
                               channel_multiplier=-1).then_inc(blocks_ready, 1)

        @block.tensor
        def _(pe):
            def turn_batch(b, par, first):
                pe.wait_ge(centred_ready, b + 1)
                if not first:
                    pe.wait_ge(turned_low, b - 1)
                    pe.wait_ge(turned_high, b - 1)
                for h in range(2):
                    for j in range(4):
                        at = P * (4 * h + j)
                        done = pe.transpose(turn[par][h][:, P * j:P * j + P], centred[par][:, at:at + P],
                                            ident[:, :])
                    done.then_inc(turn_ready, 1)

            def covariance(b, par, start, stop):
                pe.wait_ge(turned_low, b + 1)
                pe.wait_ge(turned_high, b + 1)
                for j in range(NT):
                    done = pe.matmul(cov[:, 0:P], turned[par][:, j, :], turned[par][:, j, :],
                                     start=(start and j == 0), stop=(stop and j == NT - 1),
                                     skip_group_check=True)
                done.then_inc(cov_done, 1)

            turn_batch(0, 0, True)
            turn_batch(1, 1, True)
            covariance(0, 0, True, False)
            with pe.Fori(1, B - 2, 2) as b:
                turn_batch(b + 1, 0, False)
                covariance(b, 1, False, False)
                turn_batch(b + 2, 1, False)
                covariance(b + 1, 0, False, False)
            covariance(B - 1, 1, False, True)

            for i in range(small_products):
                pe.wait_ge(operand_ready, i + 1)
                if i == 0:
                    pe.matmul(small[:, 0:1], blocks[:, :], diag[:, :], start=True, stop=True
                              ).then_inc(product_ready, 1)
                else:
                    left, right = ((power[0], power[0]), (power[1], power[0]), (power[2], sigma))[(i - 1) % 3]
                    pe.matmul(small[:, 0:P], left[:, :], right[:, :], start=True, stop=True
                              ).then_inc(product_ready, 1)
            pe.wait_ge(operand_ready, small_products + 1)

            def mix_batch(b, par, first):
                pe.wait_ge(recentred, b + 1)
                if not first:
                    pe.wait_ge(mixed_taken, b * 2 - 2)
                for h in range(2):
                    for j in range(4):
                        at = P * (4 * h + j)
                        done = pe.matmul(turn[par][h][:, P * j:P * j + P], centred[par][:, at:at + P],
                                         mix[:, :], start=True, stop=True)
                    done.then_inc(mixed, 1)

            mix_batch(0, 0, True)
            mix_batch(1, 1, True)
            with pe.Fori(2, B - 1, 2) as b:
                mix_batch(b, 0, False)
                mix_batch(b + 1, 1, False)

        @block.scalar
        def _(act):
            def take(b, par):
                act.wait_ge(turn_ready, b * 2 + 2)
                act.activation(turned[par][:, 4:8, :], turn[par][1][:, :].rearrange("p (a c) -> p a c", a=4),
                               ACT.Copy).then_inc(turned_high, 1)

            take(0, 0)
            take(1, 1)
            with act.Fori(2, B - 1, 2) as b:
                for par in range(2):
                    act.wait_ge(cov_done, b + par - 1)
                    take(b + par, par)
            act.wait_ge(root_asked, 1)
            act.activation(root[:, :], rtrace[:, :], ACT.Sqrt).then_inc(root_ready, 1)

        @block.vector
        def _(dve):
            steps = Steps(dve, dve_steps)
            steps.then(dve.bn_aggr(mean[:, :], stats[:, :, :].rearrange("p a s -> p (a s)")))
            steps.then(dve.tensor_scalar(negmean[:, :], mean[:, 0:1], -1.0, None, ALU.mult))

            def centre(b, par, signal):
                dve.tensor_scalar(centred[par][:, :], feats[:, bass.ds(b, 1), :].rearrange("p a n -> p (a n)"),
                                  negmean[:, 0:1], None, ALU.add).then_inc(signal, 1)

            def take(b, par, first):
                dve.wait_ge(turn_ready, b * 2 + 1)
                if not first:
                    dve.wait_ge(cov_done, b - 1)
                dve.tensor_copy(turned[par][:, 0:4, :], turn[par][0][:, :].rearrange("p (a c) -> p a c", a=4)
                                ).then_inc(turned_low, 1)

            centre(0, 0, centred_ready)
            centre(1, 1, centred_ready)
            take(0, 0, True)
            take(1, 1, True)
            with dve.Fori(2, B - 1, 2) as b:
                for par in range(2):
                    dve.wait_ge(turn_ready, (b + par) * 2 - 2)
                    centre(b + par, par, centred_ready)
                for par in range(2):
                    take(b + par, par, False)

            dve.wait_ge(cov_done, B)
            dve.wait_ge(blocks_ready, 1)
            steps.then(dve.scalar_tensor_tensor(out=sigma[:, :], in0=cov[:, 0:P], scalar=1.0 / (B * N),
                                                in1=blocks[:, :], op0=ALU.mult, op1=ALU.mult))
            steps.then(dve.scalar_tensor_tensor(out=sigma[:, :], in0=ident[:, :], scalar=WHITEN_EPS,
                                                in1=sigma[:, :], op0=ALU.mult, op1=ALU.add))
            steps.then(dve.tensor_tensor(scratch[:, :], sigma[:, :], ident[:, :], ALU.mult))
            dve.tensor_reduce(diag[:, :], scratch[:, :], AX.X, ALU.add).then_inc(operand_ready, 1)
            dve.wait_ge(product_ready, 1)
            steps.then(dve.reciprocal(rtrace[:, :], small[:, 0:1]))
            dve.tensor_scalar(sigma[:, :], sigma[:, :], rtrace[:, 0:1], None, ALU.mult).then_inc(root_asked, 1)
            dve.wait_ge(root_asked, 1)
            steps.then(dve.tensor_scalar(scratch[:, :], sigma[:, :], -0.5, None, ALU.mult))
            dve.scalar_tensor_tensor(out=power[0][:, :], in0=ident[:, :], scalar=1.5, in1=scratch[:, :],
                                     op0=ALU.mult, op1=ALU.add).then_inc(operand_ready, 1)
            n = 1
            for _ in range(WHITEN_STEPS - 1):
                for into in (1, 2):
                    n += 1
                    dve.wait_ge(product_ready, n)
                    dve.tensor_copy(power[into][:, :], small[:, 0:P]).then_inc(operand_ready, 1)
                n += 1
                steps.then(dve.tensor_scalar(scratch[:, :], power[0][:, :], 1.5, None, ALU.mult))
                dve.wait_ge(product_ready, n)
                dve.scalar_tensor_tensor(out=power[0][:, :], in0=small[:, 0:P], scalar=-0.5, in1=scratch[:, :],
                                         op0=ALU.mult, op1=ALU.add).then_inc(operand_ready, 1)
            dve.wait_ge(root_ready, 1)
            dve.wait_ge(params_loaded, 32)
            dve.wait_ge(operand_ready, n + 1)
            dve.scalar_tensor_tensor(out=mix[:, :], in0=power[0][:, :], scalar=root[:, 0:1], in1=weight[:, :],
                                     op0=ALU.mult, op1=ALU.mult).then_inc(operand_ready, 1)

            def give_tokens(b, par):
                for h in range(2):
                    dve.wait_ge(mixed, b * 2 + h + 1)
                    dve.tensor_tensor(tokens[:, bass.ds(b * NT + 4 * h, 4), :],
                                      turn[par][h][:, :].rearrange("p (a c) -> p a c", a=4),
                                      bias[:, :].unsqueeze(1).to_broadcast([P, 4, C]), ALU.add
                                      ).then_inc(mixed_taken, 1)

            centre(0, 0, recentred)
            centre(1, 1, recentred)
            with dve.Fori(0, B - 3, 2) as b:
                for par in range(2):
                    give_tokens(b + par, par)
                    centre(b + par + 2, par, recentred)
            give_tokens(B - 2, 0)
            give_tokens(B - 1, 1)



def store_images(nc, ident, tokens, out):
    image = out.rearrange("b c h w -> b c (h w)")
    with ExitStack() as ctx:
        t = Tools(nc, ctx)
        rows = [t.sbuf(f"rows{i}", [P, NT, C]) for i in range(2)]
        plane = [t.sbuf(f"plane{i}", [P, N]) for i in range(2)]
        turn = [t.psum(f"oturn{i}", [P, N]) for i in range(2)]
        rows_ready = t.sem("rows_ready")
        turned = t.sem("oturned")
        plane_ready = t.sem("plane_ready")
        stored = [t.sem(f"stored{i}") for i in range(2)]
        block = ctx.enter_context(nc.Block())

        @block.vector
        def _(dve):
            def stage(b, par):
                dve.tensor_copy(rows[par][:, :, :], tokens[:, bass.ds(b * NT, NT), :]).then_inc(rows_ready, 1)
            stage(0, 0)
            stage(1, 1)
            with dve.Fori(2, B - 1, 2) as b:
                for par in range(2):
                    dve.wait_ge(turned, b + par - 1)
                    stage(b + par, par)

        @block.tensor
        def _(pe):
            def turn_batch(b, par, first):
                pe.wait_ge(rows_ready, b + 1)
                if not first:
                    pe.wait_ge(plane_ready, b - 1)
                for j in range(NT):
                    done = pe.transpose(turn[par][:, P * j:P * j + P], rows[par][:, j, :], ident[:, :])
                done.then_inc(turned, 1)
            turn_batch(0, 0, True)
            turn_batch(1, 1, True)
            with pe.Fori(2, B - 1, 2) as b:
                for par in range(2):
                    turn_batch(b + par, par, False)

        @block.scalar
        def _(act):
            def take(b, par, first):
                act.wait_ge(turned, b + 1)
                if not first:
                    act.wait_ge(stored[par], (b - par) * 8)
                act.activation(plane[par][:, :], turn[par][:, :], ACT.Copy).then_inc(plane_ready, 1)
            take(0, 0, True)
            take(1, 1, True)
            with act.Fori(2, B - 1, 2) as b:
                for par in range(2):
                    take(b + par, par, False)

        @block.sync
        def _(sp):
            for b in range(B):
                sp.wait_ge(plane_ready, b + 1)
                sp.dma_start(image[b], plane[b % 2][:, :]).then_inc(stored[b % 2], 16)
            for par in range(2):
                sp.wait_ge(stored[par], 16 * B // 2)



HEADS2 = 8
HC = C // HEADS2
TOKEN_EPS = 1e-05
HEAD_EPS = 1e-05


def linear_attention(nc, ins, ident, tokens):
    with ExitStack() as ctx:
        t = Tools(nc, ctx)
        names = ["kln_weight", "kln_bias", "vln_weight", "vln_bias"]
        column = t.sbuf("lcolumn", [P, 2])
        rows = t.sbuf("lrows", [P, 2, C])
        blocks = t.sbuf("lblocks", [P, C])
        ones = t.sbuf("lones", [P, P])
        factor = [t.sbuf(f"lfactor{i}", [P, C]) for i in range(4)]
        head_sum = [t.sbuf(f"head_sum{i}", [P, NT * HEADS2]) for i in range(2)]
        offset = [t.sbuf(f"offset{i}", [P, N]) for i in range(2)]
        square = [t.sbuf(f"square{i}", [P, N]) for i in range(2)]
        bn = [t.sbuf(f"lbn{i}", [P, NT, 6]) for i in range(2)]
        mv = [t.sbuf(f"lmv{i}", [P, NT, 2]) for i in range(2)]
        var = [t.sbuf(f"lvar{i}", [P, NT * HEADS2 + NT]) for i in range(2)]
        std = [t.sbuf(f"lstd{i}", [P, NT * HEADS2 + NT]) for i in range(2)]
        rstd = [t.sbuf(f"lrstd{i}", [P, NT]) for i in range(2)]
        scale = [t.sbuf(f"lscale{i}", [P, NT * HEADS2]) for i in range(2)]
        z = [t.sbuf(f"z{i}", [P, NT, C + 1]) for i in range(2)]
        u = [t.sbuf(f"lu{i}", [P, NT, C]) for i in range(2)]
        uT = [t.sbuf(f"luT{i}", [P, N]) for i in range(2)]
        sums = [t.sbuf(f"lsums{i}", [P, 1]) for i in range(2)]
        kv = [t.sbuf(f"kv{i}", [P, C]) for i in range(2)]
        turn = [t.psum(f"lturn{h}", [P, HALF]) for h in range(2)]
        gram = [t.psum(f"gram{i}", [P, HALF]) for i in range(2)]
        result = [t.psum(f"lresult{h}", [P, HALF]) for h in range(2)]
        GS = slice(256, 256 + C)

        params_loaded = t.sem("lparams_loaded")
        blocks_ready = t.sem("lblocks_ready")
        pool_steps = t.sem("lpool_steps")
        setup_steps = t.sem("lsetup_steps")
        front_steps = t.sem("lfront_steps")
        back_steps = t.sem("lback_steps")
        offset_ready = t.sem("offset_ready")
        square_ready = t.sem("square_ready")
        var_ready = t.sem("lvar_ready")
        std_ready = t.sem("lstd_ready")
        z_ready = t.sem("z_ready")
        u_ready = t.sem("lu_ready")
        turn_ready = t.sem("lturn_ready")
        uT_ready = t.sem("luT_ready")
        gram_ready = t.sem("gram_ready")
        kv_ready = t.sem("kv_ready")
        result_ready = t.sem("lresult_ready")
        added = t.sem("ladded")
        block = ctx.enter_context(nc.Block())

        @block.sync
        def _(sp):
            for i in range(2):
                sp.dma_start(column[:, i:i + 1], ins["L2_attn_" + names[i]].rearrange("h a d -> (h d) a")
                             ).then_inc(params_loaded, 16)
                sp.dma_start(rows[:, i, :], row_to_all(ins["L2_attn_" + names[2 + i]].rearrange("h a d -> (h a d)"))
                             ).then_inc(params_loaded, 16)

        @block.gpsimd
        def _(pool):
            steps = Steps(pool, pool_steps)
            steps.did(pool.memset(ones[:, :], 1.0))
            for i in range(2):
                steps.did(pool.memset(z[i][:, :, C:C + 1], 1.0))
            steps.then(pool.memset(blocks[:, :], 1.0))
            grid = blocks[:, :].rearrange("p (g c) -> p g c", g=HEADS2)
            steps.then(pool.affine_select(out=grid, in_=grid, compare_op=ALU.is_ge, fill=0.0, base=0,
                                          pattern=[[-HC, HEADS2], [0, HC]], channel_multiplier=1))
            pool.affine_select(out=grid, in_=grid, compare_op=ALU.is_ge, fill=0.0, base=HC - 1,
                               pattern=[[HC, HEADS2], [0, HC]], channel_multiplier=-1).then_inc(blocks_ready, 1)

        @block.vector
        def _(dve):
            steps = Steps(dve, setup_steps)
            dve.wait_ge(params_loaded, 64)
            dve.wait_ge(blocks_ready, 1)
            for i, (col, row, over) in enumerate(((0, 0, 1.0 / N), (0, 1, 1.0 / N), (1, 0, 1.0 / N), (1, 1, 1.0))):
                steps.then(dve.tensor_scalar(factor[i][:, :], rows[:, row, :], column[:, col:col + 1], over,
                                             ALU.mult, ALU.mult))
                steps.then(dve.tensor_tensor(factor[i][:, :], factor[i][:, :], blocks[:, :], ALU.mult))
            steps.then(dve.tensor_tensor(factor[3][:, :], factor[3][:, :], ident[:, :], ALU.add))

            front = Steps(dve, front_steps)
            back = Steps(dve, back_steps)

            def front_half(b, par):
                front.round(b)
                batch = tokens[:, bass.ds(b * NT, NT), :].rearrange("p j (h d) -> p (j h) d", h=HEADS2)
                front.did(dve.tensor_reduce(head_sum[par][:, :], batch, AX.X, ALU.add))
                for j in range(NT):
                    front.did(dve.bn_stats(bn[par][:, j, :], tokens[:, bass.ds(b * NT + j, 1), :]
                                           .rearrange("p a c -> p (a c)")))
                front.settle()
                front.did(dve.tensor_scalar(head_sum[par][:, :], head_sum[par][:, :], 1.0 / HC, None, ALU.mult))
                for j in range(NT):
                    front.did(dve.bn_aggr(mv[par][:, j, :], bn[par][:, j, :]))
                front.settle()
                dve.tensor_tensor(offset[par][:, :].rearrange("p (g d) -> p g d", d=HC), batch,
                                  head_sum[par][:, :].unsqueeze(2).to_broadcast([P, NT * HEADS2, HC]),
                                  ALU.subtract).then_inc(offset_ready, 1)
                front.did(dve.tensor_scalar(var[par][:, NT * HEADS2:], mv[par][:, :, 1], TOKEN_EPS, None, ALU.add))
                dve.wait_ge(square_ready, b + 1)
                front.then(dve.tensor_reduce(head_sum[par][:, :], square[par][:, :].rearrange("p (g d) -> p g d", d=HC),
                                             AX.X, ALU.add))
                dve.tensor_scalar(var[par][:, 0:NT * HEADS2], head_sum[par][:, :], 1.0 / (HC - 1), None,
                                  ALU.mult).then_inc(var_ready, 1)

            def front_rest(b, par):
                dve.wait_ge(std_ready, b + 1)
                front.then(dve.reciprocal(rstd[par][:, :], std[par][:, NT * HEADS2:]))
                for j in range(NT):
                    done = dve.tensor_scalar(u[par][:, j, :], tokens[:, bass.ds(b * NT + j, 1), :]
                                             .rearrange("p a c -> p (a c)"), mv[par][:, j, 0:1],
                                             rstd[par][:, j:j + 1], ALU.subtract, ALU.mult)
                done.then_inc(u_ready, 1)
                scales = scale[par][:, :].rearrange("p (j h) -> p j h", h=HEADS2)
                spread = rstd[par][:, :].unsqueeze(2).to_broadcast([P, NT, HEADS2])
                front.then(dve.tensor_tensor(scales, std[par][:, 0:NT * HEADS2].rearrange("p (j h) -> p j h", h=HEADS2),
                                             spread, ALU.mult))
                front.then(dve.tensor_scalar(scale[par][:, :], scale[par][:, :], HEAD_EPS, None, ALU.add))
                front.then(dve.reciprocal(scale[par][:, :], scale[par][:, :]))
                front.then(dve.tensor_tensor(scales, scales, spread, ALU.mult))
                dve.tensor_tensor(z[par][:, :, 0:C].rearrange("p j (h d) -> p j h d", h=HEADS2),
                                  offset[par][:, :].rearrange("p (j h d) -> p j h d", j=NT, h=HEADS2),
                                  scales.unsqueeze(3).to_broadcast([P, NT, HEADS2, HC]), ALU.mult
                                  ).then_inc(z_ready, 1)

            def combine(b, par):
                back.round(b)
                dve.wait_ge(gram_ready, b + 1)
                back.did(dve.tensor_copy(sums[par][:, :], gram[par][:, C:C + 1]))
                back.then(dve.tensor_tensor(kv[par][:, :], gram[par][:, 0:C], factor[0][:, :], ALU.mult))
                back.then(dve.scalar_tensor_tensor(out=kv[par][:, :], in0=factor[1][:, :], scalar=sums[par][:, 0:1],
                                                   in1=kv[par][:, :], op0=ALU.mult, op1=ALU.add))
                back.then(dve.tensor_tensor(u[par][:, 0, :], gram[par][:, GS], factor[2][:, :], ALU.mult))
                back.then(dve.tensor_tensor(kv[par][:, :], kv[par][:, :], u[par][:, 0, :], ALU.add))
                dve.tensor_tensor(kv[par][:, :], kv[par][:, :], factor[3][:, :], ALU.add).then_inc(kv_ready, 1)

            def add(b, par):
                dve.wait_ge(result_ready, b + 1)
                for h in range(2):
                    rows4 = tokens[:, bass.ds(b * NT + 4 * h, 4), :]
                    done = dve.tensor_tensor(rows4, rows4, result[h][:, :].rearrange("p (a c) -> p a c", a=4), ALU.add)
                done.then_inc(added, 1)

            def batch(b, par, first=False):
                front_half(b, par)
                if not first:
                    combine(b - 1, 1 - par)
                front_rest(b, par)
                if not first:
                    add(b - 1, 1 - par)

            batch(0, 0, first=True)
            batch(1, 1)
            with dve.Fori(2, B - 1, 2) as b:
                batch(b, 0)
                batch(b + 1, 1)
            combine(B - 1, 1)
            add(B - 1, 1)

        @block.scalar
        def _(act):
            def batch(b, par):
                act.wait_ge(offset_ready, b + 1)
                act.activation(square[par][:, :], offset[par][:, :], ACT.Square).then_inc(square_ready, 1)
                act.wait_ge(var_ready, b + 1)
                act.activation(std[par][:, :], var[par][:, :], ACT.Sqrt).then_inc(std_ready, 1)
                act.wait_ge(turn_ready, b + 1)
                for h in range(2):
                    done = act.activation(uT[par][:, HALF * h:HALF * h + HALF], turn[h][:, :], ACT.Copy)
                done.then_inc(uT_ready, 1)

            batch(0, 0)
            batch(1, 1)
            with act.Fori(2, B - 1, 2) as b:
                batch(b, 0)
                batch(b + 1, 1)

        @block.tensor
        def _(pe):
            pe.wait_ge(pool_steps, 4)

            def batch(b, par, first=False):
                pe.wait_ge(u_ready, b + 1)
                if not first:
                    pe.wait_ge(uT_ready, b)
                for j in range(NT):
                    done = pe.transpose(turn[j // 4][:, P * (j % 4):P * (j % 4) + P], u[par][:, j, :], ident[:, :])
                done.then_inc(turn_ready, 1)
                pe.wait_ge(z_ready, b + 1)
                for j in range(NT):
                    pe.matmul(gram[par][:, 0:C + 1], z[par][:, j, 0:C], z[par][:, j, :],
                              start=(j == 0), stop=(j == NT - 1))
                for j in range(NT):
                    done = pe.matmul(gram[par][:, GS], ones[:, :], z[par][:, j, 0:C],
                                     start=(j == 0), stop=(j == NT - 1))
                done.then_inc(gram_ready, 1)

            def give(b, par, first=False):
                pe.wait_ge(kv_ready, b + 1)
                pe.wait_ge(uT_ready, b + 1)
                if not first:
                    pe.wait_ge(added, b)
                for j in range(NT):
                    done = pe.matmul(result[j // 4][:, P * (j % 4):P * (j % 4) + P], uT[par][:, P * j:P * j + P],
                                     kv[par][:, :], start=True, stop=True)
                done.then_inc(result_ready, 1)

            batch(0, 0, first=True)
            give(0, 0, first=True)
            batch(1, 1)
            with pe.Fori(1, B - 2, 2) as b:
                give(b, 1)
                batch(b + 1, 0)
                give(b + 1, 0)
                batch(b + 2, 1)
            give(B - 1, 1)



E = 8
GROUPS = 4
GT = TT // GROUPS
QUADS = -(-(2 * GT + E - 1) // 4)
GS_TILES = 4 * QUADS
SLOT_TILES = GROUPS * GS_TILES
SLOTS = GS_TILES * P
UNIT = 4
UNITS = GT // UNIT
BIG = 3.0e38
ROUND = 1.5 * 2.0 ** 23


class Expert:

    def __init__(self, kind, width):
        self.gelu = kind == "gelu"
        self.width = width
        self.chunks = [(k, min(P, width - k)) for k in range(0, width, P)]


def route(nc, kind, router, rbias, ident, tokens, normed, masks, gates, places, owner, tag):
    with ExitStack() as ctx:
        t = Tools(nc, ctx)
        bn = [t.sbuf(f"{tag}bn{i}", [P, NT, 6]) for i in range(2)]
        mv = [t.sbuf(f"{tag}mv{i}", [P, NT, 2]) for i in range(2)]
        var = [t.sbuf(f"{tag}var{i}", [P, NT]) for i in range(2)]
        std = [t.sbuf(f"{tag}std{i}", [P, NT]) for i in range(2)]
        rstd = [t.sbuf(f"{tag}rstd{i}", [P, NT]) for i in range(2)]
        std2 = [t.sbuf(f"{tag}std2{i}", [P, NT]) for i in range(2)]
        u = [t.sbuf(f"{tag}u{i}", [P, NT, C]) for i in range(2)]
        uT = [t.sbuf(f"{tag}uT{i}", [P, N]) for i in range(2)]
        logits = t.sbuf(f"{tag}logits", [P, TT, E])
        work = t.sbuf(f"{tag}work", [P, TT, E])
        best = [t.sbuf(f"{tag}best{i}", [P, TT]) for i in range(2)]
        first = t.sbuf(f"{tag}first", [P, TT])
        rank = t.sbuf(f"{tag}rank", [P, E])
        rank_i = t.sbuf(f"{tag}rank_i", [P, E], I32)
        chosen = t.sbuf(f"{tag}chosen", [P, GROUPS, E, GT], BF16)
        upper = t.sbuf(f"{tag}upper", [P, P], BF16)
        ones = t.sbuf(f"{tag}ones", [P, P], BF16)
        ones_row = t.sbuf(f"{tag}ones_row", [P, GROUPS * E * GT])
        count = t.sbuf(f"{tag}count", [P, GROUPS * E, GT])
        before = t.sbuf(f"{tag}before", [P, GROUPS * E, GT])
        total = t.sbuf(f"{tag}total", [P, GROUPS, E])
        running = t.sbuf(f"{tag}running", [P, GROUPS, E])
        padded = t.sbuf(f"{tag}padded", [P, GROUPS, E])
        ends = t.sbuf(f"{tag}ends", [P, GROUPS, E])
        shift = t.sbuf(f"{tag}shift", [P, GROUPS, E])
        slot_i = t.sbuf(f"{tag}slot_i", [1, GS_TILES], I32)
        slot_f = t.sbuf(f"{tag}slot_f", [1, GS_TILES])
        passed = t.sbuf(f"{tag}passed", [1, GS_TILES, E])
        owner_f = t.sbuf(f"{tag}owner_f", [1, SLOT_TILES])
        slot_no = t.sbuf(f"{tag}slot_no", [P, TT, 2])
        part_i = [t.sbuf(f"{tag}part{i}", [P, TT, 2], I32) for i in range(2)]
        turn = [[t.psum(f"{tag}turn{i}{h}", [P, HALF]) for h in range(2)] for i in range(2)]
        score = [t.psum(f"{tag}score{i}", [P, HALF]) for i in range(2)]
        ahead = t.psum(f"{tag}ahead", [P, HALF])
        totals = t.psum(f"{tag}totals", [P, HALF])

        constants = t.sem(f"{tag}constants")
        pool_steps = t.sem(f"{tag}pool_steps")
        front_steps = t.sem(f"{tag}front_steps")
        steps_sem = t.sem(f"{tag}steps")
        var_ready = t.sem(f"{tag}var_ready")
        std_ready = t.sem(f"{tag}std_ready")
        u_ready = t.sem(f"{tag}u_ready")
        copied = t.sem(f"{tag}copied")
        turn_ready = t.sem(f"{tag}turn_ready")
        uT_ready = t.sem(f"{tag}uT_ready")
        score_ready = t.sem(f"{tag}score_ready")
        score_taken = t.sem(f"{tag}score_taken")
        exp_asked = t.sem(f"{tag}exp_asked")
        exp_done = t.sem(f"{tag}exp_done")
        chosen_ready = t.sem(f"{tag}chosen_ready")
        counted = t.sem(f"{tag}counted")
        norms = 2 if kind.gelu else 1
        block = ctx.enter_context(nc.Block())

        @block.gpsimd
        def _(pool):
            steps = Steps(pool, pool_steps)
            steps.did(pool.iota(rank_i[:, :], [[-1, E]], base=E, channel_multiplier=0))
            steps.did(pool.iota(slot_i[:, :], [[P, GS_TILES]], base=0, channel_multiplier=0))
            steps.did(pool.memset(ones[:, :], 1.0))
            steps.did(pool.memset(ones_row[:, :], 1.0))
            steps.then(pool.memset(upper[:, :], 1.0))
            steps.did(pool.tensor_copy(rank[:, :], rank_i[:, :]))
            steps.did(pool.tensor_copy(slot_f[:, :], slot_i[:, :]))
            steps.then(pool.affine_select(out=upper[:, :], in_=upper[:, :], compare_op=ALU.is_gt, fill=0.0, base=0,
                                          pattern=[[1, P]], channel_multiplier=-1))
            pool.memset(owner_f[:, :], 0.0).then_inc(constants, 1)

            def keep(b, par):
                pool.wait_ge(u_ready, b + 1)
                pool.tensor_copy(normed[:, bass.ds(b * NT, NT), :], u[par][:, :, :]).then_inc(copied, 1)
            keep(0, 0)
            keep(1, 1)
            with pool.Fori(2, B - 1, 2) as b:
                keep(b, 0)
                keep(b + 1, 1)

        @block.tensor
        def _(pe):
            def turn_batch(b, par, first=False):
                pe.wait_ge(u_ready, b + 1)
                if not first:
                    pe.wait_ge(uT_ready, b - 1)
                for j in range(NT):
                    done = pe.transpose(turn[par][j // 4][:, P * (j % 4):P * (j % 4) + P], u[par][:, j, :], ident[:, :])
                done.then_inc(turn_ready, 1)

            def score_batch(b, par, first=False):
                pe.wait_ge(uT_ready, b + 1)
                if not first:
                    pe.wait_ge(score_taken, b - 1)
                for j in range(NT):
                    done = pe.matmul(score[par][:, E * j:E * j + E], uT[par][:, P * j:P * j + P], router[:, :],
                                     start=True, stop=True)
                done.then_inc(score_ready, 1)

            turn_batch(0, 0, first=True)
            turn_batch(1, 1, first=True)
            score_batch(0, 0, first=True)
            turn_batch(2, 0)
            score_batch(1, 1, first=True)
            with pe.Fori(2, B - 3, 2) as b:
                for par in range(2):
                    turn_batch(b + par + 1, 1 - par)
                    score_batch(b + par, par)
            turn_batch(B - 1, 1)
            score_batch(B - 2, 0)
            score_batch(B - 1, 1)
            pe.wait_ge(constants, 1)
            pe.wait_ge(chosen_ready, 1)
            flat = chosen[:, :, :, :].rearrange("p g e t -> p (g e t)")
            pe.matmul(ahead[:, :], upper[:, :], flat, start=True, stop=True).then_inc(counted, 1)
            pe.matmul(totals[:, :], ones[:, :], flat, start=True, stop=True).then_inc(counted, 1)

        @block.scalar
        def _(act):
            def batch(b, par, first=False):
                act.wait_ge(var_ready, b * norms + 1)
                act.activation(std[par][:, :], var[par][:, :], ACT.Sqrt).then_inc(std_ready, 1)
                if kind.gelu:
                    act.wait_ge(var_ready, b * norms + 2)
                    act.activation(std2[par][:, :], var[par][:, :], ACT.Sqrt).then_inc(std_ready, 1)
                act.wait_ge(turn_ready, b + 1)
                for h in range(2):
                    done = act.activation(uT[par][:, HALF * h:HALF * h + HALF], turn[par][h][:, :], ACT.Copy)
                done.then_inc(uT_ready, 1)
            batch(0, 0, True)
            batch(1, 1, True)
            with act.Fori(2, B - 1, 2) as b:
                for par in range(2):
                    act.wait_ge(score_ready, b + par - 1)
                    batch(b + par, par)
            act.wait_ge(exp_asked, 1)
            act.activation(work[:, :, :], work[:, :, :], ACT.Exp).then_inc(exp_done, 1)
            act.activation(best[1][:, :], best[1][:, :], ACT.Exp).then_inc(exp_done, 1)

        @block.vector
        def _(dve):
            front = Steps(dve, front_steps)

            def normalise(b, par, first=False):
                front.round(b)
                for j in range(NT):
                    front.did(dve.bn_stats(bn[par][:, j, :], tokens[:, bass.ds(b * NT + j, 1), :]
                                           .rearrange("p a c -> p (a c)")))
                if not first:
                    dve.wait_ge(copied, b - 1)
                    dve.wait_ge(turn_ready, b - 1)
                front.settle()
                front.did(dve.tensor_copy(rstd[par][:, 0:1], bn[par][:, 0, 0:1]))
                for j in range(NT):
                    front.did(dve.bn_aggr(mv[par][:, j, :], bn[par][:, j, :]))
                front.settle()
                dve.tensor_scalar(var[par][:, :], mv[par][:, :, 1], TOKEN_EPS, None, ALU.add).then_inc(var_ready, 1)
                dve.wait_ge(std_ready, b * norms + 1)
                front.then(dve.reciprocal(rstd[par][:, :], std[par][:, :]))
                if kind.gelu:
                    front.then(dve.tensor_tensor(var[par][:, :], rstd[par][:, :], rstd[par][:, :], ALU.mult))
                    front.then(dve.tensor_tensor(var[par][:, :], var[par][:, :], mv[par][:, :, 1], ALU.mult))
                    dve.tensor_scalar(var[par][:, :], var[par][:, :], TOKEN_EPS, None, ALU.add).then_inc(var_ready, 1)
                    dve.wait_ge(std_ready, b * norms + 2)
                    front.then(dve.reciprocal(var[par][:, :], std2[par][:, :]))
                    front.then(dve.tensor_tensor(rstd[par][:, :], rstd[par][:, :], var[par][:, :], ALU.mult))
                for j in range(NT):
                    done = dve.tensor_scalar(u[par][:, j, :], tokens[:, bass.ds(b * NT + j, 1), :]
                                             .rearrange("p a c -> p (a c)"), mv[par][:, j, 0:1],
                                             rstd[par][:, j:j + 1], ALU.subtract, ALU.mult)
                done.then_inc(u_ready, 1)

            def take_scores(b, par):
                dve.wait_ge(score_ready, b + 1)
                rows = logits[:, bass.ds(b * NT, NT), :]
                given = score[par][:, 0:NT * E].rearrange("p (j e) -> p j e", e=E)
                if kind.gelu:
                    dve.tensor_tensor(rows, given, std2[par][:, :].unsqueeze(2).to_broadcast([P, NT, E]),
                                      ALU.mult).then_inc(score_taken, 1)
                else:
                    dve.tensor_copy(rows, given).then_inc(score_taken, 1)

            normalise(0, 0, first=True)
            normalise(1, 1, first=True)
            with dve.Fori(2, B - 1, 2) as b:
                for par in range(2):
                    take_scores(b + par - 2, par)
                    normalise(b + par, par)
            take_scores(B - 2, 0)
            take_scores(B - 1, 1)

            steps = Steps(dve, steps_sem)
            dve.wait_ge(score_taken, B)
            dve.wait_ge(constants, 1)
            over_e = [P, TT, E]
            if kind.gelu:
                steps.then(dve.tensor_tensor(logits[:, :, :], logits[:, :, :],
                                             rbias[:, :].unsqueeze(1).to_broadcast(over_e), ALU.add))
            ranks = rank[:, :].unsqueeze(1).to_broadcast(over_e)
            for r in range(2):
                steps.then(dve.tensor_reduce(best[r][:, :], logits[:, :, :] if r == 0 else work[:, :, :],
                                             AX.X, ALU.max))
                steps.then(dve.tensor_tensor(masks[r][:, :, :], logits[:, :, :] if r == 0 else work[:, :, :],
                                             best[r][:, :].unsqueeze(2).to_broadcast(over_e), ALU.is_ge))
                steps.then(dve.tensor_tensor(masks[r][:, :, :], masks[r][:, :, :], ranks, ALU.mult))
                steps.then(dve.tensor_reduce(first[:, :], masks[r][:, :, :], AX.X, ALU.max))
                steps.then(dve.tensor_tensor(masks[r][:, :, :], masks[r][:, :, :],
                                             first[:, :].unsqueeze(2).to_broadcast(over_e), ALU.is_equal))
                if r == 0:
                    steps.then(dve.scalar_tensor_tensor(out=work[:, :, :], in0=masks[0][:, :, :], scalar=-BIG,
                                                        in1=logits[:, :, :], op0=ALU.mult, op1=ALU.add))
            dve.tensor_tensor(chosen[:, :, :, :].rearrange("p g e t -> p g t e"),
                              masks[0][:, :, :].rearrange("p (g t) e -> p g t e", g=GROUPS),
                              masks[1][:, :, :].rearrange("p (g t) e -> p g t e", g=GROUPS),
                              ALU.add).then_inc(chosen_ready, 1)

            steps.did(dve.tensor_tensor(work[:, :, :], logits[:, :, :],
                                        best[0][:, :].unsqueeze(2).to_broadcast(over_e), ALU.subtract))
            dve.tensor_tensor(best[1][:, :], best[1][:, :], best[0][:, :], ALU.subtract).then_inc(exp_asked, 1)
            dve.wait_ge(exp_done, 2)
            if kind.gelu:
                steps.then(dve.tensor_scalar(best[0][:, :], best[1][:, :], 1.0, None, ALU.add))
            else:
                steps.then(dve.tensor_reduce(first[:, :], work[:, :, :], AX.X, ALU.add))
                steps.then(dve.scalar_tensor_tensor(out=best[0][:, :], in0=first[:, :], scalar=1e-09,
                                                    in1=best[1][:, :], op0=ALU.mult, op1=ALU.add))
                steps.then(dve.tensor_scalar(best[0][:, :], best[0][:, :], 1.0, None, ALU.add))
            steps.then(dve.reciprocal(best[0][:, :], best[0][:, :]))
            steps.did(dve.tensor_copy(gates[:, :, 0], best[0][:, :]))
            steps.did(dve.tensor_tensor(gates[:, :, 1], best[1][:, :], best[0][:, :], ALU.mult))

            dve.wait_ge(counted, 2)
            flat = lambda x: x[:, :, :].rearrange("p a b -> p (a b)")
            steps.then(dve.tensor_copy(flat(count), totals[:, :]))
            steps.did(dve.tensor_tensor_scan(flat(before), ones_row[:, :], flat(count), 0.0, ALU.mult, ALU.add))
            steps.then(dve.tensor_reduce(flat(total), count[:, :, :], AX.X, ALU.add))
            steps.did(dve.tensor_tensor_scan(flat(running), ones_row[:, 0:GROUPS * E], flat(total), 0.0,
                                             ALU.mult, ALU.add))
            steps.then(dve.tensor_scalar(flat(padded), flat(total), (P - 1) / 2.0, 1.0 / P, ALU.add, ALU.mult))
            steps.then(dve.tensor_scalar(flat(padded), flat(padded), ROUND, None, ALU.add))
            steps.then(dve.tensor_scalar(flat(padded), flat(padded), -ROUND, float(P), ALU.add, ALU.mult))
            for g in range(GROUPS):
                steps.did(dve.tensor_tensor_scan(ends[:, g, :], ones_row[:, 0:E], padded[:, g, :], 0.0,
                                                 ALU.mult, ALU.add))
            steps.settle()
            steps.did(dve.tensor_tensor(flat(shift), flat(ends), flat(padded), ALU.subtract))
            steps.did(dve.tensor_tensor(flat(total), flat(running), flat(total), ALU.subtract))
            steps.then(dve.tensor_tensor(flat(before), flat(before), flat(count), ALU.subtract))
            steps.did(dve.tensor_tensor(flat(shift), flat(shift), flat(total), ALU.subtract))
            steps.then(dve.tensor_tensor(flat(before), flat(before), ahead[:, :], ALU.add))
            steps.then(dve.tensor_tensor(before[:, :, :], before[:, :, :],
                                         flat(shift).unsqueeze(2).to_broadcast([P, GROUPS * E, GT]), ALU.add))
            for r in range(2):
                steps.then(dve.tensor_tensor(work[:, :, :].rearrange("p (g t) e -> p g t e", g=GROUPS),
                                             masks[r][:, :, :].rearrange("p (g t) e -> p g t e", g=GROUPS),
                                             before[:, :, :].rearrange("p (g e) t -> p g t e", g=GROUPS), ALU.mult))
                steps.then(dve.tensor_reduce(slot_no[:, :, r], work[:, :, :], AX.X, ALU.add))
            steps.then(dve.tensor_copy(flat(part_i[0]), flat(slot_no)))
            steps.did(dve.tensor_scalar(flat(places), flat(part_i[0]), -4 * P, None, ALU.bitwise_and))
            steps.did(dve.tensor_scalar(flat(part_i[1]), flat(part_i[0]), P - 1, 2, ALU.bitwise_and,
                                        ALU.logical_shift_left))
            steps.settle()
            steps.then(dve.tensor_scalar(flat(part_i[0]), flat(part_i[0]), 7, 3, ALU.logical_shift_right,
                                         ALU.bitwise_and))
            steps.then(dve.tensor_tensor(flat(places), flat(places), flat(part_i[1]), ALU.bitwise_or))
            steps.then(dve.tensor_tensor(flat(places), flat(places), flat(part_i[0]), ALU.bitwise_or))
            for g in range(GROUPS):
                steps.then(dve.tensor_tensor(passed[:, :, :], ends[0:1, g, :].unsqueeze(1).to_broadcast([1, GS_TILES, E]),
                                             slot_f[:, :].unsqueeze(2).to_broadcast([1, GS_TILES, E]), ALU.is_le))
                steps.then(dve.tensor_reduce(owner_f[:, GS_TILES * g:GS_TILES * g + GS_TILES], passed[:, :, :],
                                             AX.X, ALU.add))
            steps.then(dve.tensor_scalar(owner_f[:, :], owner_f[:, :], float(E - 1), None, ALU.min))
            steps.then(dve.tensor_copy(owner[:, :], owner_f[:, :]))


def run_experts(nc, kind, w_up, w_gate, w_down, up_bias, down_bias, ident, tokens, normed, gates, places,
                owner, sorted_rows, sorted_results, tag):
    row_quads = [x.rearrange("(q p k) c -> q p (k c)", p=P, k=4) for x in sorted_rows]
    result_quads = [x.rearrange("(q p k) c -> q p (k c)", p=P, k=4) for x in sorted_results]
    W = kind.width
    chunks = kind.chunks
    with ExitStack() as ctx:
        t = Tools(nc, ctx)
        send = [t.sbuf(f"{tag}send{i}", [P, UNIT, C]) for i in range(2)]
        send_at = [t.sbuf(f"{tag}send_at{i}", [P, UNIT, 2], I32) for i in range(2)]
        fetch = [t.sbuf(f"{tag}fetch{i}", [P, UNIT, 2, C]) for i in range(2)]
        fetch_at = [t.sbuf(f"{tag}fetch_at{i}", [P, UNIT, 2], I32) for i in range(2)]
        xq = [t.sbuf(f"{tag}xq{i}", [P, 4, C]) for i in range(2)]
        yq = [t.sbuf(f"{tag}yq{i}", [P, 4, C]) for i in range(2)]
        xT = [t.sbuf(f"{tag}xT{i}", [P, P]) for i in range(2)]
        summed = [t.sbuf(f"{tag}summed{i}", [P, W]) for i in range(2)]
        hidden = [t.sbuf(f"{tag}hidden{i}", [P, W]) for i in range(2)]
        hT = [t.sbuf(f"{tag}hT{i}", [P, len(chunks), P]) for i in range(2)]
        up = [t.psum(f"{tag}up{i}", [P, HALF]) for i in range(2)]
        gate = None if kind.gelu else [t.psum(f"{tag}gate{i}", [P, HALF]) for i in range(2)]
        hturn = [t.psum(f"{tag}hturn{i}", [P, HALF]) for i in range(2)]
        xturn = t.psum(f"{tag}xturn", [P, HALF])
        down = t.psum(f"{tag}down", [P, HALF])

        staged = t.sem(f"{tag}staged")
        indexed = t.sem(f"{tag}indexed")
        sent = [t.sem(f"{tag}sent{i}") for i in range(2)]
        fetched = [t.sem(f"{tag}fetched{i}") for i in range(2)]
        fetch_used = t.sem(f"{tag}fetch_used")
        x_loaded = [t.sem(f"{tag}x_loaded{i}") for i in range(2)]
        y_stored = [t.sem(f"{tag}y_stored{i}") for i in range(2)]
        x_turned = t.sem(f"{tag}x_turned")
        xT_ready = t.sem(f"{tag}xT_ready")
        up_done = t.sem(f"{tag}up_done")
        up_taken = t.sem(f"{tag}up_taken")
        hidden_ready = t.sem(f"{tag}hidden_ready")
        h_turned = t.sem(f"{tag}h_turned")
        hT_ready = t.sem(f"{tag}hT_ready")
        down_done = t.sem(f"{tag}down_done")
        y_ready = t.sem(f"{tag}y_ready")
        adding = t.sem(f"{tag}adding")
        silu_ready = t.sem(f"{tag}silu_ready")
        block = ctx.enter_context(nc.Block())
        last = SLOT_TILES - 1

        def known(s, least):
            return not isinstance(s, int) or s >= least

        @block.gpsimd
        def _(pool):
            sent_goal = [pool.alloc_register(f"{tag}sent_goal{i}") for i in range(2)]
            used_goal = [pool.alloc_register(f"{tag}used_goal{i}") for i in range(2)]
            staged_goal = pool.alloc_register(f"{tag}staged_goal")
            indexed_goal = pool.alloc_register(f"{tag}indexed_goal")
            for i in range(2):
                pool.reg_mov(sent_goal[i], 2 * UNIT * 16)
                pool.reg_mov(used_goal[i], 1 + i)
            pool.reg_mov(staged_goal, 2)
            pool.reg_mov(indexed_goal, 1)

            def send_unit(g, n, par):
                if known(n, 2):
                    pool.wait_ge(sent[par], sent_goal[par])
                    pool.reg_add(sent_goal[par], sent_goal[par], 2 * UNIT * 16)
                pool.tensor_copy(send[par][:, :, :], normed[:, bass.ds(n * UNIT, UNIT), :]).then_inc(staged, 1)
                pool.tensor_copy(send_at[par][:, :, :], places[:, bass.ds(n * UNIT, UNIT), :]).then_inc(staged, 1)
                pool.wait_ge(staged, staged_goal)
                pool.reg_add(staged_goal, staged_goal, 2)
                for i in range(UNIT):
                    for r in range(2):
                        pool.indirect_dma_start(
                            out=sorted_rows[g], out_offset=bass.IndirectOffsetOnAxis(ap=send_at[par][:, i, r:r + 1], axis=0),
                            in_=send[par][:, i, :], in_offset=None).then_inc(sent[par], 16)

            def fetch_unit(g, n, par):
                if known(n, 2):
                    pool.wait_ge(fetch_used, used_goal[par])
                    pool.reg_add(used_goal[par], used_goal[par], 2)
                pool.tensor_copy(fetch_at[par][:, :, :], places[:, bass.ds(n * UNIT, UNIT), :]).then_inc(indexed, 1)
                pool.wait_ge(indexed, indexed_goal)
                pool.reg_add(indexed_goal, indexed_goal, 1)
                for i in range(UNIT):
                    for r in range(2):
                        pool.indirect_dma_start(
                            out=fetch[par][:, i, r, :], out_offset=None, in_=sorted_results[g],
                            in_offset=bass.IndirectOffsetOnAxis(ap=fetch_at[par][:, i, r:r + 1], axis=0)
                            ).then_inc(fetched[par], 16)

            def over_units(g, unit):
                start = g * UNITS
                if g == 0:
                    unit(g, 0, 0)
                    unit(g, 1, 1)
                    start = 2
                if start < (g + 1) * UNITS:
                    with pool.Fori(start, (g + 1) * UNITS - 1, 2) as n:
                        unit(g, n, 0)
                        unit(g, n + 1, 1)

            def fetch_group(g):
                for par in range(2):
                    pool.wait_ge(y_stored[par], 16 * (g + 1) * QUADS // 2)
                over_units(g, fetch_unit)

            over_units(0, send_unit)
            for g in range(1, GROUPS):
                over_units(g, send_unit)
                fetch_group(g - 1)
            fetch_group(GROUPS - 1)

        @block.sync
        def _(sp):
            def load(g, q, par):
                if known(q, 2) or g > 0:
                    sp.wait_ge(x_turned, q * 4 + (g * GS_TILES - 4))
                sp.dma_start(xq[par][:, :, :], row_quads[g][bass.ds(q, 1), :, :].rearrange("a p (k c) -> p (a k) c", k=4)
                             ).then_inc(x_loaded[par], 16)

            def store(g, q, par):
                sp.wait_ge(y_ready, q * 4 + (g * GS_TILES + 4))
                sp.dma_start(result_quads[g][bass.ds(q, 1), :, :].rearrange("a p (k c) -> p (a k) c", k=4),
                             yq[par][:, :, :]).then_inc(y_stored[par], 16)

            for g in range(GROUPS):
                for par in range(2):
                    sp.wait_ge(sent[par], (g + 1) * (UNITS // 2) * 2 * UNIT * 16)
                for par in range(2):
                    load(g, par, par)
                    if g > 0:
                        store(g - 1, QUADS - 2 + par, par)
                with sp.Fori(2, QUADS - 1, 2) as q:
                    for par in range(2):
                        load(g, q + par, par)
                        store(g, q + par - 2, par)
            store(GROUPS - 1, QUADS - 2, 0)
            store(GROUPS - 1, QUADS - 1, 1)
            for par in range(2):
                sp.wait_ge(y_stored[par], 16 * GROUPS * QUADS // 2)

        @block.tensor
        def _(pe):
            def turn_x(s, k, qpar):
                if k == 0:
                    pe.wait_ge(x_loaded[qpar], (s - 4 * qpar) * 2 + 16)
                if known(s, 1):
                    pe.wait_ge(xT_ready, s)
                pe.transpose(xturn[:, 0:P], xq[qpar][:, k, :], ident[:, :]).then_inc(x_turned, 1)

            def go_up(s, par):
                e = pe.value_load(owner[0:1, bass.ds(s, 1)], min_val=0, max_val=E - 1)
                pe.wait_ge(xT_ready, s + 1)
                if known(s, 2):
                    pe.wait_ge(up_taken if kind.gelu else hidden_ready, s - 1)
                done = pe.matmul(up[par][:, 0:W], xT[par][:, :], w_up[:, bass.ds(e, 1), :].rearrange("p a h -> p (a h)"),
                                 start=True, stop=True)
                if not kind.gelu:
                    done = pe.matmul(gate[par][:, 0:W], xT[par][:, :],
                                     w_gate[:, bass.ds(e, 1), :].rearrange("p a h -> p (a h)"), start=True, stop=True)
                done.then_inc(up_done, 1)

            def turn_hidden(s, par):
                pe.wait_ge(hidden_ready, s + 1)
                if known(s, 2):
                    pe.wait_ge(hT_ready, s - 1)
                for i, (at, width) in enumerate(chunks):
                    done = pe.transpose(hturn[par][0:width, P * i:P * i + P], hidden[par][:, at:at + width], ident[:, :])
                done.then_inc(h_turned, 1)

            def go_down(s, par):
                e = pe.value_load(owner[0:1, bass.ds(s, 1)], min_val=0, max_val=E - 1)
                pe.wait_ge(hT_ready, s + 1)
                if known(s, 1):
                    pe.wait_ge(y_ready, s)
                for i, (at, width) in enumerate(chunks):
                    done = pe.matmul(down[:, 0:C], hT[par][0:width, i, :],
                                     w_down[0:width, bass.ds(e, 1), i, :].rearrange("p a c -> p (a c)"),
                                     start=(i == 0), stop=(i == len(chunks) - 1))
                done.then_inc(down_done, 1)

            def step(s, k, qpar, ending=False):
                if not (ending and k == 3):
                    turn_x(s + 1, (k + 1) % 4, qpar if k < 3 else 1 - qpar)
                go_up(s, k % 2)
                if known(s, 2):
                    go_down(s - 2, k % 2)
                if known(s, 1):
                    turn_hidden(s - 1, 1 - k % 2)

            turn_x(0, 0, 0)
            for k in range(4):
                step(k, k, 0)
            with pe.Fori(4, SLOT_TILES - 7, 8) as s:
                for k in range(8):
                    step(s + k, k % 4, 1 if k < 4 else 0)
            for k in range(4):
                step(SLOT_TILES - 4 + k, k, 1, ending=True)
            go_down(last - 1, 0)
            turn_hidden(last, 1)
            go_down(last, 1)

        @block.scalar
        def _(act):
            def take_hidden(s, par):
                act.wait_ge(h_turned, s + 1)
                if known(s, 2):
                    act.wait_ge(down_done, s - 1)
                full = sum(width == P for _, width in chunks)
                done = act.activation(hT[par][:, 0:full, :], hturn[par][:, 0:P * full].rearrange("p (k m) -> p k m", m=P),
                                      ACT.Copy)
                if full < len(chunks):
                    width = chunks[full][1]
                    done = act.activation(hT[par][0:width, full, :], hturn[par][0:width, P * full:P * full + P], ACT.Copy)
                done.then_inc(hT_ready, 1)

            def step(s, k):
                par = k % 2
                if kind.gelu:
                    act.wait_ge(up_taken, s + 1)
                    if known(s, 2):
                        act.wait_ge(h_turned, s - 1)
                    act.activation(hidden[par][:, :], summed[par][:, :], ACT.Gelu).then_inc(hidden_ready, 1)
                else:
                    act.wait_ge(up_done, s + 1)
                    if known(s, 2):
                        act.wait_ge(hidden_ready, s - 1)
                    act.activation(summed[par][:, :], up[par][:, 0:W], ACT.Silu).then_inc(silu_ready, 1)
                if known(s, 1):
                    take_hidden(s - 1, 1 - par)

            for k in range(4):
                step(k, k)
            with act.Fori(4, SLOT_TILES - 3, 4) as s:
                for k in range(4):
                    step(s + k, k)
            take_hidden(last, 1)

        @block.vector
        def _(dve):
            def take_x(s, par):
                dve.wait_ge(x_turned, s + 1)
                if known(s, 2):
                    dve.wait_ge(up_done, s - 1)
                dve.tensor_copy(xT[par][:, :], xturn[:, 0:P]).then_inc(xT_ready, 1)

            def take_up(s, par):
                if kind.gelu:
                    e = dve.value_load(owner[0:1, bass.ds(s, 1)], min_val=0, max_val=E - 1)
                    dve.wait_ge(up_done, s + 1)
                    if known(s, 2):
                        dve.wait_ge(hidden_ready, s - 1)
                    dve.tensor_tensor(summed[par][:, :], up[par][:, 0:W],
                                      up_bias[:, bass.ds(e, 1), :].rearrange("p a h -> p (a h)"), ALU.add
                                      ).then_inc(up_taken, 1)
                else:
                    dve.wait_ge(silu_ready, s + 1)
                    if known(s, 2):
                        dve.wait_ge(h_turned, s - 1)
                    dve.tensor_tensor(hidden[par][:, :], summed[par][:, :], gate[par][:, 0:W], ALU.mult
                                      ).then_inc(hidden_ready, 1)

            def take_down(s, k, qpar):
                if kind.gelu:
                    e = dve.value_load(owner[0:1, bass.ds(s, 1)], min_val=0, max_val=E - 1)
                if k == 0 and known(s, 8):
                    dve.wait_ge(y_stored[qpar], (s - 4 * qpar) * 2)
                dve.wait_ge(down_done, s + 1)
                if kind.gelu:
                    dve.tensor_tensor(yq[qpar][:, k, :], down[:, 0:C],
                                      down_bias[:, bass.ds(e, 1), :].rearrange("p a c -> p (a c)"), ALU.add
                                      ).then_inc(y_ready, 1)
                else:
                    dve.tensor_copy(yq[qpar][:, k, :], down[:, 0:C]).then_inc(y_ready, 1)

            def step(s, k, qpar, ending=False):
                if not (ending and k == 3):
                    take_x(s + 1, 1 - k % 2)
                if known(s, 2):
                    take_down(s - 2, (k + 2) % 4, qpar if k >= 2 else 1 - qpar)
                take_up(s, k % 2)

            def add_unit(n, par):
                dve.wait_ge(fetched[par], (n - par) * (UNIT * 16) + 2 * UNIT * 16)
                for r in range(2):
                    for i in range(UNIT):
                        row = tokens[:, bass.ds(n * UNIT + i, 1), :].rearrange("p a c -> p (a c)")
                        done = dve.scalar_tensor_tensor(
                            out=row, in0=fetch[par][:, i, r, :],
                            scalar=gates[:, bass.ds(n * UNIT + i, 1), r:r + 1].rearrange("p a b -> p (a b)"),
                            in1=row, op0=ALU.mult, op1=ALU.add)
                        if r == 0:
                            done.then_inc(adding, 1)
                    if r == 0:
                        dve.wait_ge(adding, (n + 1) * UNIT)
                done.then_inc(fetch_used, 1)

            take_x(0, 0)
            for k in range(4):
                step(k, k, 0)
            for k in range(4):
                step(4 + k, k, 1)
            with dve.Fori(8, GS_TILES - 7, 8) as s:
                for k in range(8):
                    step(s + k, k % 4, 0 if k < 4 else 1)
            for g in range(1, GROUPS):
                start = g * GS_TILES
                with dve.Fori(0, UNITS - 1, 2) as n:
                    for k in range(8):
                        step(n * 4 + (start + k), k % 4, 0 if k < 4 else 1)
                        if k % 4 == 3:
                            add_unit(n + ((g - 1) * UNITS + k // 4), k // 4)
                end = (g + 1) * GS_TILES
                final = end - 8 if g == GROUPS - 1 else end
                with dve.Fori(start + 4 * UNITS, final - 7, 8) as s:
                    for k in range(8):
                        step(s + k, k % 4, 0 if k < 4 else 1)
            for k in range(8):
                step(SLOT_TILES - 8 + k, k % 4, k // 4, ending=(k // 4 == 1))
            take_down(last - 1, 2, 1)
            take_down(last, 3, 1)
            with dve.Fori((GROUPS - 1) * UNITS, GROUPS * UNITS - 1, 2) as n:
                add_unit(n, 0)
                add_unit(n + 1, 1)


def experts_gelu(nc, ins, ident, tokens, sorted_rows, sorted_results):
    kind = Expert("gelu", 512)
    W = kind.width
    with ExitStack() as ctx:
        t = Tools(nc, ctx)
        normed = t.sbuf("g_normed", [P, TT, C])
        gates = t.sbuf("g_gates", [P, TT, 2])
        places = t.sbuf("g_places", [P, TT, 2], I32)
        owner = t.sbuf("g_owner", [1, SLOT_TILES], I32)
        w_up = t.sbuf("g_w_up", [P, E, W])
        w_down = t.sbuf("g_w_down", [P, E, W // P, C])
        up_bias = t.sbuf("g_up_bias", [P, E, W])
        down_bias = t.sbuf("g_down_bias", [P, E, C])
        router = t.sbuf("g_router", [P, E])
        rbias = t.sbuf("g_rbias", [P, E])
        with ExitStack() as setup:
            t = Tools(nc, setup)
            scale = t.sbuf("g_scale", [P, E])
            shift = t.sbuf("g_shift", [P, E])
            extra = [t.psum(f"g_extra{i}", [P, HALF]) for i in range(2)]
            loaded = t.sem("g_loaded")
            added = t.sem("g_added")
            extra_ready = t.sem("g_extra_ready")
            block = setup.enter_context(nc.Block())

            @block.sync
            def _(sp):
                sp.dma_start(w_up[:, :, :], ins["L2_ffn_W1"].rearrange("e c h -> c e h")).then_inc(loaded, 16)
                sp.dma_start(up_bias[:, :, :], row_to_all(ins["L2_ffn_b1"])).then_inc(loaded, 16)
                sp.dma_start(scale[:, :], ins["L2_ffn_ln_g"].rearrange("e c -> c e"), allow_slow_non_contiguous=True).then_inc(loaded, 16)
                sp.dma_start(shift[:, :], ins["L2_ffn_ln_b"].rearrange("e c -> c e"), allow_slow_non_contiguous=True).then_inc(loaded, 16)
                sp.dma_start(router[:, :], ins["L2_ffn_Wr"]).then_inc(loaded, 16)
                sp.dma_start(rbias[:, :], row_to_all(ins["L2_ffn_br"])).then_inc(loaded, 16)
                sp.dma_start(down_bias[:, :, :], row_to_all(ins["L2_ffn_b2"])).then_inc(loaded, 16)
                sp.dma_start(w_down[:, :, :, :].rearrange("p e k c -> p (e k) c"),
                             ins["L2_ffn_W2"].rearrange("e (k p) c -> p (e k) c", p=P)).then_inc(loaded, 16)
                sp.wait_ge(loaded, 128)

            @block.tensor
            def _(pe):
                pe.wait_ge(loaded, 128)
                for e in range(E):
                    if e >= 2:
                        pe.wait_ge(added, e - 1)
                    pe.matmul(extra[e % 2][:, :], shift[:, e:e + 1].to_broadcast([P, P]), w_up[:, e, :],
                              start=True, stop=True).then_inc(extra_ready, 1)

            @block.vector
            def _(dve):
                for e in range(E):
                    dve.wait_ge(extra_ready, e + 1)
                    dve.tensor_tensor(up_bias[:, e, :], up_bias[:, e, :], extra[e % 2][:, :], ALU.add
                                      ).then_inc(added, 1)
                    dve.tensor_scalar(w_up[:, e, :], w_up[:, e, :], scale[:, e:e + 1], None, ALU.mult)

        with ExitStack() as routing:
            masks = [Tools(nc, routing).sbuf(f"g_mask{i}", [P, TT, E]) for i in range(2)]
            route(nc, kind, router, rbias, ident, tokens, normed, masks, gates, places, owner, "gr_")
        run_experts(nc, kind, w_up, None, w_down, up_bias, down_bias, ident, tokens, normed, gates, places,
                    owner, sorted_rows, sorted_results, "gx_")



WINDOW = 32
SHIFT = WINDOW // 2
HEADS3 = 4
HD = C // HEADS3
CW = HALF // WINDOW
MASKED = -1.0e30


def window_attention(nc, ins, ident, tokens):
    with ExitStack() as ctx:
        t = Tools(nc, ctx)
        rows = t.sbuf("w_rows", [P, 4, C])
        wT = t.sbuf("w_wT", [P, 4, C])
        qbias = t.sbuf("w_qbias", [P, 3])
        obias = t.sbuf("w_obias", [P, C])
        toeplitz = t.sbuf("w_toeplitz", [P, WINDOW])
        bias = t.sbuf("w_bias", [P, WINDOW])
        last_bias = t.sbuf("w_last_bias", [P, CW, WINDOW])
        bn = t.sbuf("w_bn", [P, NT, 6])
        mv = t.sbuf("w_mv", [P, NT, 2])
        var = t.sbuf("w_var", [P, NT])
        std = t.sbuf("w_std", [P, NT])
        rstd = t.sbuf("w_rstd", [P, NT])
        u = t.sbuf("w_u", [P, NT, C])
        uT = [t.sbuf(f"w_uT{i}", [P, N + SHIFT]) for i in range(2)]
        qs = [t.sbuf(f"w_qs{i}", [P, CW, HEADS3, WINDOW]) for i in range(2)]
        kT = [t.sbuf(f"w_kT{i}", [P, HALF]) for i in range(2)]
        vs = [t.sbuf(f"w_vs{i}", [P, CW, HEADS3, HD]) for i in range(4)]
        logit = [t.sbuf(f"w_logit{i}", [P, CW, WINDOW]) for i in range(2)]
        top = [t.sbuf(f"w_top{i}", [P, CW]) for i in range(2)]
        prob = [t.sbuf(f"w_prob{i}", [P, CW, WINDOW]) for i in range(2)]
        total = [t.sbuf(f"w_total{i}", [P, CW]) for i in range(2)]
        pT = [t.sbuf(f"w_pT{i}", [P, HALF]) for i in range(2)]
        oT = [t.sbuf(f"w_oT{i}", [P, SHIFT + N]) for i in range(2)]
        turn = [t.psum(f"w_turn{i}", [P, HALF]) for i in range(2)]
        proj = [t.psum(f"w_proj{i}", [P, HALF]) for i in range(3)]
        score = t.psum("w_score", [P, HALF])
        mixed = t.psum("w_mixed", [P, HALF])
        result = t.psum("w_result", [P, HALF])

        loaded = t.sem("w_loaded")
        turned = t.sem("w_turned")
        weights_ready = t.sem("w_weights_ready")
        pool_steps = t.sem("w_pool_steps")
        masks_ready = t.sem("w_masks_ready")
        setup = t.sem("w_setup")
        table_ready = t.sem("w_table_ready")
        front_steps = t.sem("w_front_steps")
        var_ready = t.sem("w_var_ready")
        std_ready = t.sem("w_std_ready")
        u_ready = t.sem("w_u_ready")
        turn_ready = t.sem("w_turn_ready")
        uT_ready = t.sem("w_uT_ready")
        prepared = t.sem("w_prepared")
        result_ready = t.sem("w_result_ready")
        result_taken = t.sem("w_result_taken")
        proj_ready = t.sem("w_proj_ready")
        q_taken = t.sem("w_q_taken")
        k_taken = t.sem("w_k_taken")
        v_taken = t.sem("w_v_taken")
        score_ready = t.sem("w_score_ready")
        score_taken = t.sem("w_score_taken")
        pre_steps = t.sem("w_pre_steps")
        shifted = t.sem("w_shifted")
        exp_done = t.sem("w_exp_done")
        post_steps = t.sem("w_post_steps")
        pT_ready = t.sem("w_pT_ready")
        mixed_ready = t.sem("w_mixed_ready")
        mixed_taken = t.sem("w_mixed_taken")
        block = ctx.enter_context(nc.Block())
        loads = 8 + HEADS3

        def batches(engine, step, turn_first):
            turn_first()
            for b in range(2):
                for h in range(2):
                    step(b, h, b)
            with engine.Fori(2, B - 3, 2) as b:
                for par in range(2):
                    for h in range(2):
                        step(b + par, h, par)
            for b in (B - 2, B - 1):
                for h in range(2):
                    step(b, h, b % 2)

        def known(x, least):
            return not isinstance(x, int) or x >= least

        @block.sync
        def _(sp):
            for i in range(3):
                sp.dma_start(rows[:, i, :], ins["L3_attn_w_qkv"][P * i:P * i + P, :]).then_inc(loaded, 16)
                sp.dma_start(qbias[:, i:i + 1], ins["L3_attn_b_qkv"][P * i:P * i + P].rearrange("(c a) -> c a", a=1)
                             ).then_inc(loaded, 16)
            sp.dma_start(rows[:, 3, :], ins["L3_attn_w_out"]).then_inc(loaded, 16)
            sp.dma_start(obias[:, :], row_to_all(ins["L3_attn_b_out"])).then_inc(loaded, 16)
            rel = ins["L3_attn_rel_pos"]
            for h in range(HEADS3):
                windows = bass.AP(tensor=rel.tensor, offset=h * (2 * WINDOW - 1), ap=[[1, WINDOW], [1, WINDOW]])
                sp.dma_start(toeplitz[WINDOW * h:WINDOW * h + WINDOW, :], windows).then_inc(loaded, 16)

        @block.gpsimd
        def _(pool):
            steps = Steps(pool, pool_steps)
            for x in (*qs, *vs):
                steps.did(pool.memset(x[:, :, :, :], 0.0))
            pool.wait_ge(table_ready, 1)
            steps.then(pool.tensor_copy(last_bias[:, :, :], bias[:, :].unsqueeze(1).to_broadcast([P, CW, WINDOW])))
            for h in range(HEADS3):
                part = slice(WINDOW * h, WINDOW * h + WINDOW)
                steps.did(pool.affine_select(out=last_bias[part, CW - 1, SHIFT:], in_=last_bias[part, CW - 1, SHIFT:],
                                             compare_op=ALU.is_ge, fill=MASKED, base=-SHIFT,
                                             pattern=[[0, WINDOW - SHIFT]], channel_multiplier=1))
                steps.did(pool.affine_select(out=last_bias[part, CW - 1, 0:SHIFT], in_=last_bias[part, CW - 1, 0:SHIFT],
                                             compare_op=ALU.is_ge, fill=MASKED, base=SHIFT - 1,
                                             pattern=[[0, SHIFT]], channel_multiplier=-1))
            steps.settle()
            pool.memset(std[:, :], 1.0).then_inc(masks_ready, 1)

            def prepare(b):
                pool.wait_ge(u_ready, b + 1)
                batch = tokens[:, bass.ds(b * NT, NT), :]
                pool.tensor_tensor(batch, batch, obias[:, :].unsqueeze(1).to_broadcast([P, NT, C]), ALU.add
                                   ).then_inc(prepared, 1)
            pool.wait_ge(loaded, 16 * loads)
            with pool.Fori(0, B) as b:
                prepare(b)

        @block.tensor
        def _(pe):
            pe.wait_ge(loaded, 16 * loads)
            for i in range(4):
                done = pe.transpose(turn[0][:, P * i:P * i + P], rows[:, i, :], ident[:, :])
            done.then_inc(turned, 1)
            pe.wait_ge(weights_ready, 1)
            pe.wait_ge(pool_steps, 6)

            def turn_batch(b):
                pe.wait_ge(u_ready, b + 1)
                if known(b, 1):
                    pe.wait_ge(uT_ready, b)
                for j in range(NT):
                    done = pe.transpose(turn[j // 4][:, P * (j % 4):P * (j % 4) + P], u[:, j, :], ident[:, :])
                done.then_inc(turn_ready, 1)

            def project(b, h, par):
                pe.wait_ge(uT_ready, b + 1)
                for i, taken in enumerate((q_taken, k_taken, v_taken)):
                    if known(b, 1) or h == 1:
                        pe.wait_ge(taken, b * 2 + h)
                    at = SHIFT + HALF * h
                    pe.matmul(proj[i][:, :], wT[:, i, :], uT[par][:, at:at + HALF], start=True, stop=True
                              ).then_inc(proj_ready, 1)

            def scores(b, h):
                pe.wait_ge(q_taken, b * 2 + h + 1)
                pe.wait_ge(k_taken, b * 2 + h + 1)
                if known(b, 1) or h == 1:
                    pe.wait_ge(score_taken, b * 2 + h)
                for w in range(CW):
                    done = pe.matmul(score[:, WINDOW * w:WINDOW * w + WINDOW],
                                     qs[h][:, w, :, :].rearrange("p h q -> p (h q)"),
                                     kT[h][:, WINDOW * w:WINDOW * w + WINDOW], start=True, stop=True)
                done.then_inc(score_ready, 1)

            def mix(b, h, par):
                pe.wait_ge(v_taken, b * 2 + h + 1)
                pe.wait_ge(pT_ready, b * 2 + h + 1)
                if known(b, 1) or h == 1:
                    pe.wait_ge(mixed_taken, b * 2 + h)
                for w in range(CW):
                    done = pe.matmul(mixed[:, WINDOW * w:WINDOW * w + WINDOW],
                                     vs[2 * par + h][:, w, :, :].rearrange("p h d -> p (h d)"),
                                     pT[h][:, WINDOW * w:WINDOW * w + WINDOW], start=True, stop=True)
                done.then_inc(mixed_ready, 1)

            def give(b, par):
                pe.wait_ge(mixed_taken, b * 2 + 2)
                for half in range(2):
                    if known(b, 1) or half == 1:
                        pe.wait_ge(result_taken, b * 2 + half)
                    for j in range(4):
                        at = P * (4 * half + j)
                        done = pe.matmul(result[:, P * j:P * j + P], oT[par][:, at:at + P], wT[:, 3, :],
                                         start=True, stop=True)
                    done.then_inc(result_ready, 1)

            def step(b, h, par):
                project(b, h, par)
                if h == 0 and known(b, 2):
                    give(b - 2, par)
                if h == 1:
                    scores(b, 0)
                elif known(b, 1):
                    scores(b - 1, 1)
                if known(b, 1):
                    mix(b - 1, h, 1 - par)
                if h == 0 and not (isinstance(b, int) and b == B - 1):
                    turn_batch(b + 1)

            batches(pe, step, lambda: turn_batch(0))
            give(B - 2, 0)
            scores(B - 1, 1)
            mix(B - 1, 0, 1)
            mix(B - 1, 1, 1)
            give(B - 1, 1)

        @block.scalar
        def _(act):
            act.wait_ge(masks_ready, 1)

            def take_turned(b, par):
                act.wait_ge(turn_ready, b + 1)
                for h in range(2):
                    act.activation(uT[par][:, HALF * h:HALF * h + HALF], turn[h][:, :], ACT.Copy)
                act.activation(uT[par][:, N:N + SHIFT], turn[0][:, 0:SHIFT], ACT.Copy).then_inc(uT_ready, 1)

            def root(b):
                act.wait_ge(var_ready, b + 1)
                act.activation(std[:, :], var[:, :], ACT.Sqrt).then_inc(std_ready, 1)

            def take_q(b, h):
                act.wait_ge(proj_ready, (b * 2 + h) * 3 + 1)
                if known(b, 1):
                    act.wait_ge(score_ready, b * 2 + h - 1)
                for i in range(HEADS3):
                    part = slice(HD * i, HD * i + HD)
                    done = act.activation(qs[h][part, :, i, :], proj[0][part, :].rearrange("p (w q) -> p w q", w=CW),
                                          ACT.Identity, bias=qbias[part, 0:1], scale=HD ** -0.5)
                done.then_inc(q_taken, 1)

            def exponent(b, h):
                act.wait_ge(shifted, b * 2 + h + 1)
                act.activation(prob[h][:, :, :], logit[h][:, :, :], ACT.Exp).then_inc(exp_done, 1)

            def take_mixed(b, h, par):
                act.wait_ge(mixed_ready, b * 2 + h + 1)
                if known(b, 2):
                    act.wait_ge(result_ready, b * 2 - 2)
                at = SHIFT + HALF * h
                done = act.activation(oT[par][:, at:at + HALF], mixed[:, :], ACT.Identity, bias=qbias[:, 2:3])
                if h == 1:
                    done = act.activation(oT[par][:, 0:SHIFT], mixed[:, HALF - SHIFT:], ACT.Identity, bias=qbias[:, 2:3])
                done.then_inc(mixed_taken, 1)

            def step(b, h, par):
                take_q(b, h)
                if h == 1:
                    exponent(b, 0)
                elif known(b, 1):
                    exponent(b - 1, 1)
                if known(b, 1):
                    take_mixed(b - 1, h, 1 - par)
                if h == 0 and not (isinstance(b, int) and b == B - 1):
                    root(b + 1)
                    take_turned(b + 1, 1 - par)

            def start():
                act.wait_ge(table_ready, 1)
                root(0)
                take_turned(0, 0)

            batches(act, step, start)
            exponent(B - 1, 1)
            take_mixed(B - 1, 0, 1)
            take_mixed(B - 1, 1, 1)

        @block.vector
        def _(dve):
            steps = Steps(dve, setup)
            dve.wait_ge(turned, 1)
            dve.tensor_copy(wT[:, :, :].rearrange("p i c -> p (i c)"), turn[0][:, :]).then_inc(weights_ready, 1)
            dve.wait_ge(loaded, 16 * loads)
            steps.did(dve.tensor_scalar(qbias[:, 0:1], qbias[:, 0:1], HD ** -0.5, None, ALU.mult))
            for q in range(WINDOW):
                done = dve.tensor_copy(bias[:, q:q + 1], toeplitz[:, WINDOW - 1 - q:WINDOW - q])
            steps.did(done)
            steps.settle()
            dve.memset(var[:, :], 1.0).then_inc(table_ready, 1)
            dve.wait_ge(table_ready, 1)

            front = Steps(dve, front_steps)
            pre = Steps(dve, pre_steps)
            post = Steps(dve, post_steps)

            def normalise(b):
                front.round(b)
                for j in range(NT):
                    front.did(dve.bn_stats(bn[:, j, :], tokens[:, bass.ds(b * NT + j, 1), :].rearrange("p a c -> p (a c)")))
                if known(b, 1):
                    dve.wait_ge(turn_ready, b)
                front.settle()
                front.did(dve.tensor_copy(rstd[:, 0:1], bn[:, 0, 0:1]))
                for j in range(NT):
                    front.did(dve.bn_aggr(mv[:, j, :], bn[:, j, :]))
                front.settle()
                dve.tensor_scalar(var[:, :], mv[:, :, 1], TOKEN_EPS, None, ALU.add).then_inc(var_ready, 1)
                dve.wait_ge(std_ready, b + 1)
                front.then(dve.reciprocal(rstd[:, :], std[:, :]))
                for j in range(NT):
                    done = dve.tensor_scalar(u[:, j, :], tokens[:, bass.ds(b * NT + j, 1), :].rearrange("p a c -> p (a c)"),
                                             mv[:, j, 0:1], rstd[:, j:j + 1], ALU.subtract, ALU.mult)
                done.then_inc(u_ready, 1)

            def take_kv(b, h, par):
                dve.wait_ge(proj_ready, (b * 2 + h) * 3 + 2)
                if known(b, 1):
                    dve.wait_ge(score_ready, b * 2 + h - 1)
                dve.tensor_scalar(kT[h][:, :], proj[1][:, :], qbias[:, 1:2], None, ALU.add).then_inc(k_taken, 1)
                dve.wait_ge(proj_ready, (b * 2 + h) * 3 + 3)
                if known(b, 2):
                    dve.wait_ge(mixed_ready, b * 2 + h - 3)
                for i in range(HEADS3):
                    part = slice(HD * i, HD * i + HD)
                    done = dve.transpose(vs[2 * par + h][part, :, i, :], proj[2][part, :].rearrange("p (w q) -> p w q", w=CW))
                done.then_inc(v_taken, 1)

            def before_exp(b, h):
                pre.round(b * 2 + h)
                dve.wait_ge(score_ready, b * 2 + h + 1)
                table = last_bias[:, :, :] if h == 1 else bias[:, :].unsqueeze(1).to_broadcast([P, CW, WINDOW])
                dve.tensor_tensor(logit[h][:, :, :], score[:, :].rearrange("p (w q) -> p w q", w=CW), table, ALU.add
                                  ).then_inc(score_taken, 1)
                dve.wait_ge(score_taken, b * 2 + h + 1)
                pre.then(dve.tensor_reduce(top[h][:, :], logit[h][:, :, :], AX.X, ALU.max))
                dve.tensor_tensor(logit[h][:, :, :], logit[h][:, :, :],
                                  top[h][:, :].unsqueeze(2).to_broadcast([P, CW, WINDOW]), ALU.subtract
                                  ).then_inc(shifted, 1)

            def after_exp(b, h):
                post.round(b * 2 + h)
                dve.wait_ge(exp_done, b * 2 + h + 1)
                post.then(dve.tensor_reduce(total[h][:, :], prob[h][:, :, :], AX.X, ALU.add))
                post.then(dve.reciprocal(total[h][:, :], total[h][:, :]))
                post.then(dve.tensor_tensor(prob[h][:, :, :], prob[h][:, :, :],
                                            total[h][:, :].unsqueeze(2).to_broadcast([P, CW, WINDOW]), ALU.mult))
                if known(b, 1):
                    dve.wait_ge(mixed_ready, b * 2 + h - 1)
                dve.transpose(pT[h][:, :], prob[h][:, :, :].rearrange("p w q -> p (w q)")).then_inc(pT_ready, 1)

            def add(b):
                dve.wait_ge(prepared, b + 1)
                for half in range(2):
                    dve.wait_ge(result_ready, b * 2 + half + 1)
                    rows4 = tokens[:, bass.ds(b * NT + 4 * half, 4), :]
                    dve.tensor_tensor(rows4, rows4, result[:, :].rearrange("p (a c) -> p a c", a=4), ALU.add
                                      ).then_inc(result_taken, 1)

            def step(b, h, par):
                if known(b, 1):
                    after_exp(b - 1, h)
                take_kv(b, h, par)
                if h == 0 and known(b, 2):
                    add(b - 2)
                if h == 1:
                    before_exp(b, 0)
                elif known(b, 1):
                    before_exp(b - 1, 1)
                if h == 0 and not (isinstance(b, int) and b == B - 1):
                    normalise(b + 1)

            dve.wait_ge(masks_ready, 1)
            batches(dve, step, lambda: normalise(0))
            add(B - 2)
            after_exp(B - 1, 0)
            before_exp(B - 1, 1)
            after_exp(B - 1, 1)
            add(B - 1)


def experts_silu(nc, ins, ident, tokens, sorted_rows, sorted_results):
    kind = Expert("silu", 341)
    W = kind.width
    chunks = kind.chunks
    with ExitStack() as ctx:
        t = Tools(nc, ctx)
        gates = t.sbuf("s_gates", [P, TT, 2])
        places = t.sbuf("s_places", [P, TT, 2], I32)
        owner = t.sbuf("s_owner", [1, SLOT_TILES], I32)
        w_up = t.sbuf("s_w_up", [P, E, W])
        w_gate = t.sbuf("s_w_gate", [P, E, W])
        w_down = t.sbuf("s_w_down", [P, E, len(chunks), C])
        router = t.sbuf("s_router", [P, E])
        with ExitStack() as setup:
            t = Tools(nc, setup)
            rows_of = E * W
            full = rows_of // P
            rest = rows_of - full * P
            raw = [t.sbuf(f"s_raw{i}", [P, full + 1, C]) for i in range(2)]
            raw_down = t.sbuf("s_raw_down", [P, E, W])
            raw_router = t.sbuf("s_raw_router", [E, C])
            turn = [t.psum(f"s_turn{i}", [P, HALF]) for i in range(2)]
            loaded = t.sem("s_loaded")
            turned = t.sem("s_turned")
            taken = t.sem("s_taken")
            block = setup.enter_context(nc.Block())

            jobs = []
            for m, into in ((0, w_up), (1, w_gate)):
                flat = into[:, :, :].rearrange("p e h -> p (e h)")
                for j in range(0, full, 4):
                    n = min(4, full - j)
                    jobs.append(([raw[m][:, j + i, :] for i in range(n)], P, flat[:, P * j:P * (j + n)]))
                jobs.append(([raw[m][0:rest, full, :]], P, flat[:, P * full:]))
            for e in range(E):
                whole = [c for c in chunks if c[1] == P]
                jobs.append(([raw_down[:, e, at:at + P] for at, _ in whole], P,
                             w_down[:, e, 0:len(whole), :].rearrange("p k c -> p (k c)")))
                at, width = chunks[-1]
                jobs.append(([raw_down[:, e, at:at + width]], width, w_down[0:width, e, len(chunks) - 1, :]))
            jobs.append(([raw_router[:, :]], P, router[:, :]))

            @block.sync
            def _(sp):
                for m, name in enumerate(("L3_ffn_w1", "L3_ffn_w3")):
                    flat = ins[name].rearrange("e h c -> (e h) c")
                    sp.dma_start(raw[m][:, 0:full, :], flat[0:full * P, :].rearrange("(j p) c -> p j c", p=P)
                                 ).then_inc(loaded, 16)
                    sp.dma_start(raw[m][0:rest, full, :], flat[full * P:, :]).then_inc(loaded, 16)
                sp.dma_start(raw_down[:, :, :], ins["L3_ffn_w2"].rearrange("e c h -> c e h")).then_inc(loaded, 16)
                sp.dma_start(raw_router[:, :], ins["L3_ffn_router_w"]).then_inc(loaded, 16)
                sp.wait_ge(loaded, 96)

            @block.tensor
            def _(pe):
                pe.wait_ge(loaded, 96)
                for n, (parts, height, _) in enumerate(jobs):
                    if n >= 2:
                        pe.wait_ge(taken, n - 1)
                    at = 0
                    for part in parts:
                        width = part.shape[0]
                        done = pe.transpose(turn[n % 2][0:height, at:at + width], part, ident[0:width, 0:width])
                        at += width
                    done.then_inc(turned, 1)

            @block.vector
            def _(dve):
                for n, (parts, height, into) in enumerate(jobs):
                    dve.wait_ge(turned, n + 1)
                    dve.tensor_copy(into, turn[n % 2][0:height, 0:sum(part.shape[0] for part in parts)]
                                    ).then_inc(taken, 1)

        normed = Tools(nc, ctx).sbuf("s_normed", [P, TT, C])
        with ExitStack() as routing:
            masks = [Tools(nc, routing).sbuf(f"s_mask{i}", [P, TT, E]) for i in range(2)]
            route(nc, kind, router, None, ident, tokens, normed, masks, gates, places, owner, "sr_")
        run_experts(nc, kind, w_up, w_gate, w_down, None, None, ident, tokens, normed, gates, places,
                    owner, sorted_rows, sorted_results, "sx_")


INPUTS = ['x', 'L0_conv_Wq', 'L0_conv_bq', 'L0_conv_Wk', 'L0_conv_bk', 'L0_conv_Wv', 'L0_conv_bv',
          'L0_conv_gamma', 'L1_conv_weight', 'L1_conv_bias', 'L2_attn_kln_weight', 'L2_attn_kln_bias',
          'L2_attn_vln_weight', 'L2_attn_vln_bias', 'L2_ffn_Wr', 'L2_ffn_br', 'L2_ffn_ln_g', 'L2_ffn_ln_b',
          'L2_ffn_W1', 'L2_ffn_b1', 'L2_ffn_W2', 'L2_ffn_b2', 'L3_attn_w_qkv', 'L3_attn_b_qkv',
          'L3_attn_rel_pos', 'L3_attn_w_out', 'L3_attn_b_out', 'L3_ffn_router_w', 'L3_ffn_w1', 'L3_ffn_w2',
          'L3_ffn_w3']


def build(nc, ins, out, sorted_rows, sorted_results):
    with ExitStack() as ctx:
        t = Tools(nc, ctx)
        ident = t.sbuf("ident", [P, P])
        tokens = t.sbuf("tokens", [P, TT, C])
        made = t.sem("made")
        with nc.Block() as block:
            @block.gpsimd
            def _(pool):
                make_identity(pool, Steps(pool, made), ident[:, :])
        with ExitStack() as early:
            t = Tools(nc, early)
            feats = t.sbuf("feats", [P, B, N])
            stats = t.sbuf("stats", [P, 2 * B, 6])
            conv_attention(nc, ins, ident, feats, stats, sorted_rows)
            whiten(nc, ins, ident, feats, stats, tokens)
        linear_attention(nc, ins, ident, tokens)
        experts_gelu(nc, ins, ident, tokens, sorted_rows, sorted_results)
        window_attention(nc, ins, ident, tokens)
        experts_silu(nc, ins, ident, tokens, sorted_rows, sorted_results)
        store_images(nc, ident, tokens, out)


def kernel(**inputs):
    import numpy as np
    import concourse.bacc as bacc
    from concourse.bass_utils import run_bass_kernel_spmd

    nc = bacc.Bacc("TRN2", target_bir_lowering=False, num_devices=1)
    arrays, ins = {}, {}
    for name in INPUTS:
        a = np.ascontiguousarray(inputs[name])
        arrays[f"in_{name}"] = a
        ins[name] = nc.dram_tensor(f"in_{name}", a.shape, mybir.dt.from_np(a.dtype), kind="ExternalInput").ap()
    out = nc.dram_tensor("out", (B, C, 32, 32), F32, kind="ExternalOutput").ap()
    sorted_rows, sorted_results = ([nc.dram_tensor(f"sorted_{what}{g}", (SLOTS, C), F32, kind="Internal").ap()
                                    for g in range(GROUPS)] for what in ("rows", "results"))
    build(nc, ins, out, sorted_rows, sorted_results)
    r = run_bass_kernel_spmd(nc, [arrays], core_ids=[0])
    return r.results[0]["out"]
```

```python
from contextlib import ExitStack

import concourse.bass as bass
from concourse import mybir

ALU = mybir.AluOpType
ACT = mybir.ActivationFunctionType
AX = mybir.AxisListType
F32 = mybir.dt.float32
F32R = mybir.dt.float32r
BF16 = mybir.dt.bfloat16
I32 = mybir.dt.int32

P = 128
B, C, N = 8, 128, 1024
NT = N // P
TT = B * NT
CQ = C // 2
HALF = 512


class Tools:

    def __init__(self, nc, ctx):
        self.nc, self.ctx = nc, ctx

    def sbuf(self, name, shape, dtype=F32):
        return self.ctx.enter_context(self.nc.sbuf_tensor(name, shape, dtype))

    def psum(self, name, shape, dtype=F32):
        return self.ctx.enter_context(self.nc.psum_tensor(name, shape, dtype))

    def sem(self, name):
        return self.ctx.enter_context(self.nc.semaphore(name))


class ClearedTools(Tools):

    def __init__(self, nc, ctx):
        super().__init__(nc, ctx)
        self.sems = []
        ctx.callback(self.clear)

    def clear(self):
        self.nc.clear_and_free_semaphores(self.sems)
        self.nc.all_engine_barrier()

    def sem(self, name):
        self.sems.append(self.nc.alloc_semaphore(name))
        return self.sems[-1]


class Steps:

    def __init__(self, engine, sem):
        self.engine, self.sem, self.n, self.base, self.per = engine, sem, 0, 0, None

    def round(self, i):
        if self.per is None and self.n:
            self.per = self.n
        if self.per is not None:
            assert self.n == self.per
            self.base = i * self.per
        self.n = 0

    def did(self, instruction):
        instruction.then_inc(self.sem, 1)
        self.n += 1

    def settle(self):
        self.engine.wait_ge(self.sem, self.base + self.n)

    def then(self, instruction):
        self.did(instruction)
        self.settle()


def row_to_all(ap, parts=P):
    return ap.partition_broadcast(parts)


def make_identity(pool, steps, tile):
    steps.then(pool.memset(tile, 0.0))
    steps.then(pool.affine_select(out=tile, in_=tile, compare_op=ALU.not_equal, fill=1.0, base=0,
                                  pattern=[[-1, P]], channel_multiplier=1))



def conv_attention(nc, ins, ident, feats, stats, sorted_rows):
    x = ins["x"].rearrange("b c h w -> b c (h w)")
    with ExitStack() as ctx:
        t = ClearedTools(nc, ctx)
        xin = [t.sbuf(f"xin{i}", [P, N]) for i in range(2)]
        wrow = [t.sbuf(f"wrow{i}", [P, C]) for i in range(3)]
        wT = [t.sbuf(f"wT{i}", [P, P]) for i in range(3)]
        bq = t.sbuf("bq", [P, 1])
        bk = t.sbuf("bk", [P, 1])
        bv = t.sbuf("bv", [P, C])
        gamma = t.sbuf("gamma", [P, 1])
        q = [t.sbuf(f"q{i}", [P, N]) for i in range(2)]
        k = [t.sbuf(f"k{i}", [P, N]) for i in range(2)]
        v = [t.sbuf(f"v{i}", [P, NT, C]) for i in range(2)]
        probs = [t.sbuf(f"probs{i}", [P, N]) for i in range(2)]
        vs = [t.sbuf(f"vs{i}", [P, C]) for i in range(2)]
        nmax = [t.sbuf(f"nmax{i}", [P, 1]) for i in range(2)]
        zsum = [t.sbuf(f"zsum{i}", [P, 1]) for i in range(2)]
        rz = [t.sbuf(f"rz{i}", [P, 1]) for i in range(2)]
        score = [t.psum(f"score{i}", [P, N]) for i in range(2)]
        out = t.psum("attended", [P, N])
        proj = [t.psum(f"proj{i}", [P, HALF]) for i in range(2)]

        weights_loaded = t.sem("weights_loaded")
        x_loaded = [t.sem(f"x_loaded{i}") for i in range(2)]
        weights_turned = t.sem("weights_turned")
        weights_ready = t.sem("weights_ready")
        proj_ready = t.sem("proj_ready")
        qk_taken = t.sem("qk_taken")
        v_taken = t.sem("v_taken")
        score_ready = t.sem("score_ready")
        max_ready = t.sem("max_ready")
        exp_done = t.sem("exp_done")
        vs_ready = t.sem("vs_ready")
        av_done = t.sem("av_done")
        feats_ready = t.sem("feats_ready")
        rz_ready = t.sem("rz_ready")
        stats_ready = t.sem("stats_ready")
        zeros = t.sbuf("zeros", [P, 8 * C])
        zeroed = t.sem("zeroed")
        cleared = t.sem("cleared")
        block = ctx.enter_context(nc.Block())

        @block.sync
        def _(sp):
            for w, name in ((0, "L0_conv_Wq"), (1, "L0_conv_Wk")):
                for r in range(2):
                    sp.dma_start(wrow[w][CQ * r:CQ * r + CQ, :], ins[name]).then_inc(weights_loaded, 16)
            sp.dma_start(wrow[2][:, :], ins["L0_conv_Wv"]).then_inc(weights_loaded, 16)
            for i in range(2):
                sp.dma_start(xin[i][:, :], x[i]).then_inc(x_loaded[i], 16)
            for tile, name in ((bq, "L0_conv_bq"), (bk, "L0_conv_bk")):
                for r in range(2):
                    sp.dma_start(tile[CQ * r:CQ * r + CQ, :],
                                 ins[name].rearrange("(c a) -> c a", a=1)).then_inc(weights_loaded, 16)
            sp.dma_start(bv[:, :], row_to_all(ins["L0_conv_bv"])).then_inc(weights_loaded, 16)
            sp.dma_start(gamma[:, :], row_to_all(ins["L0_conv_gamma"])).then_inc(weights_loaded, 16)
            for b in range(2, B):
                sp.wait_ge(feats_ready, b - 1)
                sp.dma_start(xin[b % 2][:, :], x[b]).then_inc(x_loaded[b % 2], 16)


        @block.gpsimd
        def _(pool):
            pool.memset(zeros[:, :], 0.0).then_inc(zeroed, 1)
            pool.wait_ge(zeroed, 1)
            for rows in sorted_rows:
                for at in range(0, SLOTS, 8 * P):
                    pool.dma_start(rows[at:at + 8 * P, :].rearrange("(p k) c -> p (k c)", p=P),
                                   zeros[:, :]).then_inc(cleared, 16)
            pool.wait_ge(cleared, 16 * len(sorted_rows) * (SLOTS // (8 * P)))

        @block.tensor
        def _(pe):
            pe.wait_ge(weights_loaded, 160 + 16)
            for i in range(3):
                turned = pe.transpose(proj[0][:, P * i:P * i + P], wrow[i][:, :], ident[:, :])
            turned.then_inc(weights_turned, 1)
            pe.wait_ge(weights_ready, 1)

            def project(b, par, item, first):
                if item == 0:
                    pe.wait_ge(x_loaded[par], (b - par) * 8 + 16)
                if item < 2:
                    if not first:
                        pe.wait_ge(v_taken, b * 2 - 1 + item)
                else:
                    pe.wait_ge(qk_taken, b * 4 + item - 1)
                bank = proj[item % 2]
                if item < 4:
                    w = wT[item // 2]
                    pe.matmul(bank[:, :], w[:, :], xin[par][:, HALF * (item % 2):HALF * (item % 2) + HALF],
                              start=True, stop=True).then_inc(proj_ready, 1)
                else:
                    for j in range(4):
                        at = P * (4 * (item - 4) + j)
                        done = pe.matmul(bank[:, P * j:P * j + P], xin[par][:, at:at + P], wT[2][:, :],
                                         start=True, stop=True)
                    done.then_inc(proj_ready, 1)

            def scores(b, par, n):
                if n == 0:
                    pe.wait_ge(qk_taken, b * 4 + 4)
                if not (isinstance(b, int) and b * NT + n < 2):
                    pe.wait_ge(exp_done, b * NT + n - 1)
                rows = slice(CQ * (n % 2), CQ * (n % 2) + CQ)
                for h in range(2):
                    done = pe.matmul(score[n % 2][:, HALF * h:HALF * h + HALF], k[par][rows, P * n:P * n + P],
                                     q[par][rows, HALF * h:HALF * h + HALF], start=True, stop=True)
                done.then_inc(score_ready, 1)

            def attend(b, n):
                pe.wait_ge(vs_ready, b * NT + n + 1)
                if n == 0 and not (isinstance(b, int) and b == 0):
                    pe.wait_ge(feats_ready, b)
                for h in range(2):
                    done = pe.matmul(out[:, HALF * h:HALF * h + HALF], vs[n % 2][:, :],
                                     probs[n % 2][:, HALF * h:HALF * h + HALF],
                                     start=(n == 0), stop=(n == NT - 1))
                done.then_inc(av_done, 1)

            def batch(b, par, first=False, last=False):
                for n in range(NT):
                    scores(b, par, n)
                    if n >= 2:
                        attend(b, n - 2)
                    elif not first:
                        attend(b - 1, NT + n - 2)
                    for item in {2: (0, 1), 3: (2, 3), 4: (4,), 5: (5,)}.get(n, ()) if not last else ():
                        project(b + 1, 1 - par, item, False)

            for item in range(6):
                project(0, 0, item, True)
            batch(0, 0, first=True)
            batch(1, 1)
            with pe.Fori(2, B - 3, 2) as b:
                batch(b, 0)
                batch(b + 1, 1)
            batch(B - 2, 0)
            batch(B - 1, 1, last=True)
            attend(B - 1, NT - 2)
            attend(B - 1, NT - 1)

        @block.vector
        def _(dve):
            dve.wait_ge(weights_turned, 1)
            for i in range(3):
                done = dve.tensor_copy(wT[i][:, :], proj[0][:, P * i:P * i + P])
            done.then_inc(weights_ready, 1)

            def take_values(b, par, h):
                dve.wait_ge(proj_ready, b * 6 + 5 + h)
                dve.tensor_tensor(v[par][:, 4 * h:4 * h + 4, :],
                                  proj[h][:, :].rearrange("p (a c) -> p a c", a=4),
                                  bv[:, :].unsqueeze(1).to_broadcast([P, 4, C]), ALU.add).then_inc(v_taken, 1)

            def row_max(b, n):
                dve.wait_ge(score_ready, b * NT + n + 1)
                dve.tensor_reduce(nmax[n % 2][:, :], score[n % 2][:, :], AX.X, ALU.max,
                                  negate=True).then_inc(max_ready, 1)

            def scale_values(b, par, n):
                dve.wait_ge(exp_done, b * NT + n + 1)
                if n % 4 == 0:
                    dve.wait_ge(v_taken, b * 2 + 1 + n // 4)
                dve.reciprocal(rz[n % 2][:, :], zsum[n % 2][:, :]).then_inc(rz_ready, 1)
                dve.wait_ge(rz_ready, b * NT + n + 1)
                dve.tensor_scalar(vs[n % 2][:, :], v[par][:, n, :], rz[n % 2][:, 0:1], None,
                                  ALU.mult).then_inc(vs_ready, 1)

            def finish(b, par):
                dve.wait_ge(av_done, b * NT + NT)
                dve.scalar_tensor_tensor(out=feats[:, bass.ds(b, 1), :].rearrange("p a n -> p (a n)"),
                                         in0=out[:, :], scalar=gamma[:, 0:1], in1=xin[par][:, :],
                                         op0=ALU.mult, op1=ALU.add).then_inc(feats_ready, 1)
                dve.wait_ge(feats_ready, b + 1)
                for h in range(2):
                    dve.bn_stats(stats[:, bass.ds(b * 2 + h, 1), :].rearrange("p a s -> p (a s)"),
                                 feats[:, bass.ds(b, 1), HALF * h:HALF * h + HALF].rearrange("p a n -> p (a n)"),
                                 ).then_inc(stats_ready, 1)

            def batch(b, par, first=False, last=False):
                for n in range(NT):
                    row_max(b, n)
                    if n >= 1:
                        scale_values(b, par, n - 1)
                    elif not first:
                        scale_values(b - 1, 1 - par, NT - 1)
                    if n == 1 and not first:
                        finish(b - 1, 1 - par)
                    if n in (5, 6) and not last:
                        take_values(b + 1, 1 - par, n - 5)

            take_values(0, 0, 0)
            take_values(0, 0, 1)
            batch(0, 0, first=True)
            batch(1, 1)
            with dve.Fori(2, B - 3, 2) as b:
                batch(b, 0)
                batch(b + 1, 1)
            batch(B - 2, 0)
            batch(B - 1, 1, last=True)
            scale_values(B - 1, 1, NT - 1)
            finish(B - 1, 1)

        @block.scalar
        def _(act):
            act.wait_ge(weights_loaded, 176)

            def take_projection(b, par, item):
                into, bias = ((q, bq), (k, bk))[item // 2]
                at = slice(HALF * (item % 2), HALF * (item % 2) + HALF)
                act.wait_ge(proj_ready, b * 6 + item + 1)
                act.activation(into[par][:, at], proj[item % 2][:, :], ACT.Identity,
                               bias=bias[:, 0:1]).then_inc(qk_taken, 1)

            def exponent(b, n):
                act.wait_ge(max_ready, b * NT + n + 1)
                if not (isinstance(b, int) and b * NT + n < 2):
                    act.wait_ge(av_done, b * NT + n - 1)
                act.activation(probs[n % 2][:, :], score[n % 2][:, :], ACT.Exp, bias=nmax[n % 2][:, 0:1],
                               accum_out=zsum[n % 2][:, 0:1]).then_inc(exp_done, 1)

            def batch(b, par, first=False, last=False):
                for n in range(NT):
                    exponent(b, n)
                    for item in {2: (0, 1), 3: (2, 3)}.get(n, ()) if not last else ():
                        take_projection(b + 1, 1 - par, item)

            for item in range(4):
                take_projection(0, 0, item)
            batch(0, 0, first=True)
            batch(1, 1)
            with act.Fori(2, B - 3, 2) as b:
                batch(b, 0)
                batch(b + 1, 1)
            batch(B - 2, 0)
            batch(B - 1, 1, last=True)



GROUP = 32
WHITEN_STEPS = 5
WHITEN_EPS = 1e-05


def whiten(nc, ins, ident, feats, stats, tokens):
    with ExitStack() as ctx:
        t = ClearedTools(nc, ctx)
        centred = [t.sbuf(f"centred{i}", [P, N]) for i in range(2)]
        turned = [t.sbuf(f"turned{i}", [P, NT, C]) for i in range(2)]
        mean = t.sbuf("mean", [P, 2])
        negmean = t.sbuf("negmean", [P, 1])
        blocks = t.sbuf("blocks", [P, P])
        sigma = t.sbuf("sigma", [P, P])
        scratch = t.sbuf("scratch", [P, P])
        diag = t.sbuf("diag", [P, 1])
        rtrace = t.sbuf("rtrace", [P, 1])
        root = t.sbuf("root", [P, 1])
        power = [t.sbuf(f"power{i}", [P, P]) for i in range(3)]
        weight = t.sbuf("weight", [P, C])
        bias = t.sbuf("bias", [P, C])
        mix = t.sbuf("mix", [P, P])
        turn = [[t.psum(f"turn{i}{h}", [P, HALF]) for h in range(2)] for i in range(2)]
        cov = t.psum("cov", [P, HALF])
        small = t.psum("small", [P, HALF])

        params_loaded = t.sem("params_loaded")
        blocks_ready = t.sem("blocks_ready")
        centred_ready = t.sem("centred_ready")
        turn_ready = t.sem("turn_ready")
        turned_low = t.sem("turned_low")
        turned_high = t.sem("turned_high")
        cov_done = t.sem("cov_done")
        dve_steps = t.sem("dve_steps")
        pool_steps = t.sem("pool_steps")
        operand_ready = t.sem("operand_ready")
        product_ready = t.sem("product_ready")
        root_ready = t.sem("root_ready")
        root_asked = t.sem("root_asked")
        recentred = t.sem("recentred")
        mixed = t.sem("mixed")
        mixed_taken = t.sem("mixed_taken")
        block = ctx.enter_context(nc.Block())
        small_products = 1 + 3 * (WHITEN_STEPS - 1)

        @block.sync
        def _(sp):
            sp.dma_start(weight[:, :], row_to_all(ins["L1_conv_weight"].rearrange("a c h w -> (a c h w)"))
                         ).then_inc(params_loaded, 16)
            sp.dma_start(bias[:, :], row_to_all(ins["L1_conv_bias"].rearrange("a c h w -> (a c h w)"))
                         ).then_inc(params_loaded, 16)

        @block.gpsimd
        def _(pool):
            steps = Steps(pool, pool_steps)
            steps.then(pool.memset(blocks[:, :], 1.0))
            grid = blocks[:, :].rearrange("p (g c) -> p g c", g=P // GROUP)
            steps.then(pool.affine_select(out=grid, in_=grid, compare_op=ALU.is_ge, fill=0.0, base=0,
                                          pattern=[[-GROUP, P // GROUP], [0, GROUP]], channel_multiplier=1))
            pool.affine_select(out=grid, in_=grid, compare_op=ALU.is_ge, fill=0.0, base=GROUP - 1,
                               pattern=[[GROUP, P // GROUP], [0, GROUP]],
                               channel_multiplier=-1).then_inc(blocks_ready, 1)

        @block.tensor
        def _(pe):
            def turn_batch(b, par, first):
                pe.wait_ge(centred_ready, b + 1)
                if not first:
                    pe.wait_ge(turned_low, b - 1)
                    pe.wait_ge(turned_high, b - 1)
                for h in range(2):
                    for j in range(4):
                        at = P * (4 * h + j)
                        done = pe.transpose(turn[par][h][:, P * j:P * j + P], centred[par][:, at:at + P],
                                            ident[:, :])
                    done.then_inc(turn_ready, 1)

            def covariance(b, par, start, stop):
                pe.wait_ge(turned_low, b + 1)
                pe.wait_ge(turned_high, b + 1)
                for j in range(NT):
                    done = pe.matmul(cov[:, 0:P], turned[par][:, j, :], turned[par][:, j, :],
                                     start=(start and j == 0), stop=(stop and j == NT - 1),
                                     skip_group_check=True)
                done.then_inc(cov_done, 1)

            turn_batch(0, 0, True)
            turn_batch(1, 1, True)
            covariance(0, 0, True, False)
            with pe.Fori(1, B - 2, 2) as b:
                turn_batch(b + 1, 0, False)
                covariance(b, 1, False, False)
                turn_batch(b + 2, 1, False)
                covariance(b + 1, 0, False, False)
            covariance(B - 1, 1, False, True)

            for i in range(small_products):
                pe.wait_ge(operand_ready, i + 1)
                if i == 0:
                    pe.matmul(small[:, 0:1], blocks[:, :], diag[:, :], start=True, stop=True
                              ).then_inc(product_ready, 1)
                else:
                    left, right = ((power[0], power[0]), (power[1], power[0]), (power[2], sigma))[(i - 1) % 3]
                    pe.matmul(small[:, 0:P], left[:, :], right[:, :], start=True, stop=True
                              ).then_inc(product_ready, 1)
            pe.wait_ge(operand_ready, small_products + 1)

            def mix_batch(b, par, first):
                pe.wait_ge(recentred, b + 1)
                if not first:
                    pe.wait_ge(mixed_taken, b * 2 - 2)
                for h in range(2):
                    for j in range(4):
                        at = P * (4 * h + j)
                        done = pe.matmul(turn[par][h][:, P * j:P * j + P], centred[par][:, at:at + P],
                                         mix[:, :], start=True, stop=True)
                    done.then_inc(mixed, 1)

            mix_batch(0, 0, True)
            mix_batch(1, 1, True)
            with pe.Fori(2, B - 1, 2) as b:
                mix_batch(b, 0, False)
                mix_batch(b + 1, 1, False)

        @block.scalar
        def _(act):
            def take(b, par):
                act.wait_ge(turn_ready, b * 2 + 2)
                act.activation(turned[par][:, 4:8, :], turn[par][1][:, :].rearrange("p (a c) -> p a c", a=4),
                               ACT.Copy).then_inc(turned_high, 1)

            take(0, 0)
            take(1, 1)
            with act.Fori(2, B - 1, 2) as b:
                for par in range(2):
                    act.wait_ge(cov_done, b + par - 1)
                    take(b + par, par)
            act.wait_ge(root_asked, 1)
            act.activation(root[:, :], rtrace[:, :], ACT.Sqrt).then_inc(root_ready, 1)

        @block.vector
        def _(dve):
            steps = Steps(dve, dve_steps)
            steps.then(dve.bn_aggr(mean[:, :], stats[:, :, :].rearrange("p a s -> p (a s)")))
            steps.then(dve.tensor_scalar(negmean[:, :], mean[:, 0:1], -1.0, None, ALU.mult))

            def centre(b, par, signal):
                dve.tensor_scalar(centred[par][:, :], feats[:, bass.ds(b, 1), :].rearrange("p a n -> p (a n)"),
                                  negmean[:, 0:1], None, ALU.add).then_inc(signal, 1)

            def take(b, par, first):
                dve.wait_ge(turn_ready, b * 2 + 1)
                if not first:
                    dve.wait_ge(cov_done, b - 1)
                dve.tensor_copy(turned[par][:, 0:4, :], turn[par][0][:, :].rearrange("p (a c) -> p a c", a=4)
                                ).then_inc(turned_low, 1)

            centre(0, 0, centred_ready)
            centre(1, 1, centred_ready)
            take(0, 0, True)
            take(1, 1, True)
            with dve.Fori(2, B - 1, 2) as b:
                for par in range(2):
                    dve.wait_ge(turn_ready, (b + par) * 2 - 2)
                    centre(b + par, par, centred_ready)
                for par in range(2):
                    take(b + par, par, False)

            dve.wait_ge(cov_done, B)
            dve.wait_ge(blocks_ready, 1)
            steps.then(dve.scalar_tensor_tensor(out=sigma[:, :], in0=cov[:, 0:P], scalar=1.0 / (B * N),
                                                in1=blocks[:, :], op0=ALU.mult, op1=ALU.mult))
            steps.then(dve.scalar_tensor_tensor(out=sigma[:, :], in0=ident[:, :], scalar=WHITEN_EPS,
                                                in1=sigma[:, :], op0=ALU.mult, op1=ALU.add))
            steps.then(dve.tensor_tensor(scratch[:, :], sigma[:, :], ident[:, :], ALU.mult))
            dve.tensor_reduce(diag[:, :], scratch[:, :], AX.X, ALU.add).then_inc(operand_ready, 1)
            dve.wait_ge(product_ready, 1)
            steps.then(dve.reciprocal(rtrace[:, :], small[:, 0:1]))
            dve.tensor_scalar(sigma[:, :], sigma[:, :], rtrace[:, 0:1], None, ALU.mult).then_inc(root_asked, 1)
            dve.wait_ge(root_asked, 1)
            steps.then(dve.tensor_scalar(scratch[:, :], sigma[:, :], -0.5, None, ALU.mult))
            dve.scalar_tensor_tensor(out=power[0][:, :], in0=ident[:, :], scalar=1.5, in1=scratch[:, :],
                                     op0=ALU.mult, op1=ALU.add).then_inc(operand_ready, 1)
            n = 1
            for _ in range(WHITEN_STEPS - 1):
                for into in (1, 2):
                    n += 1
                    dve.wait_ge(product_ready, n)
                    dve.tensor_copy(power[into][:, :], small[:, 0:P]).then_inc(operand_ready, 1)
                n += 1
                steps.then(dve.tensor_scalar(scratch[:, :], power[0][:, :], 1.5, None, ALU.mult))
                dve.wait_ge(product_ready, n)
                dve.scalar_tensor_tensor(out=power[0][:, :], in0=small[:, 0:P], scalar=-0.5, in1=scratch[:, :],
                                         op0=ALU.mult, op1=ALU.add).then_inc(operand_ready, 1)
            dve.wait_ge(root_ready, 1)
            dve.wait_ge(params_loaded, 32)
            dve.wait_ge(operand_ready, n + 1)
            dve.scalar_tensor_tensor(out=mix[:, :], in0=power[0][:, :], scalar=root[:, 0:1], in1=weight[:, :],
                                     op0=ALU.mult, op1=ALU.mult).then_inc(operand_ready, 1)

            def give_tokens(b, par):
                for h in range(2):
                    dve.wait_ge(mixed, b * 2 + h + 1)
                    dve.tensor_tensor(tokens[:, bass.ds(b * NT + 4 * h, 4), :],
                                      turn[par][h][:, :].rearrange("p (a c) -> p a c", a=4),
                                      bias[:, :].unsqueeze(1).to_broadcast([P, 4, C]), ALU.add
                                      ).then_inc(mixed_taken, 1)

            centre(0, 0, recentred)
            centre(1, 1, recentred)
            with dve.Fori(0, B - 3, 2) as b:
                for par in range(2):
                    give_tokens(b + par, par)
                    centre(b + par + 2, par, recentred)
            give_tokens(B - 2, 0)
            give_tokens(B - 1, 1)



def store_images(nc, ident, tokens, out):
    image = out.rearrange("b c h w -> b c (h w)")
    with ExitStack() as ctx:
        t = Tools(nc, ctx)
        rows = [t.sbuf(f"rows{i}", [P, NT, C]) for i in range(2)]
        plane = [t.sbuf(f"plane{i}", [P, N]) for i in range(2)]
        turn = [t.psum(f"oturn{i}", [P, N]) for i in range(2)]
        rows_ready = t.sem("rows_ready")
        turned = t.sem("oturned")
        plane_ready = t.sem("plane_ready")
        stored = [t.sem(f"stored{i}") for i in range(2)]
        block = ctx.enter_context(nc.Block())

        @block.vector
        def _(dve):
            def stage(b, par):
                dve.tensor_copy(rows[par][:, :, :], tokens[:, bass.ds(b * NT, NT), :]).then_inc(rows_ready, 1)
            stage(0, 0)
            stage(1, 1)
            with dve.Fori(2, B - 1, 2) as b:
                for par in range(2):
                    dve.wait_ge(turned, b + par - 1)
                    stage(b + par, par)

        @block.tensor
        def _(pe):
            def turn_batch(b, par, first):
                pe.wait_ge(rows_ready, b + 1)
                if not first:
                    pe.wait_ge(plane_ready, b - 1)
                for j in range(NT):
                    done = pe.transpose(turn[par][:, P * j:P * j + P], rows[par][:, j, :], ident[:, :])
                done.then_inc(turned, 1)
            turn_batch(0, 0, True)
            turn_batch(1, 1, True)
            with pe.Fori(2, B - 1, 2) as b:
                for par in range(2):
                    turn_batch(b + par, par, False)

        @block.scalar
        def _(act):
            def take(b, par, first):
                act.wait_ge(turned, b + 1)
                if not first:
                    act.wait_ge(stored[par], (b - par) * 8)
                act.activation(plane[par][:, :], turn[par][:, :], ACT.Copy).then_inc(plane_ready, 1)
            take(0, 0, True)
            take(1, 1, True)
            with act.Fori(2, B - 1, 2) as b:
                for par in range(2):
                    take(b + par, par, False)

        @block.sync
        def _(sp):
            for b in range(B):
                sp.wait_ge(plane_ready, b + 1)
                sp.dma_start(image[b], plane[b % 2][:, :]).then_inc(stored[b % 2], 16)
            for par in range(2):
                sp.wait_ge(stored[par], 16 * B // 2)



HEADS2 = 8
HC = C // HEADS2
TOKEN_EPS = 1e-05
HEAD_EPS = 1e-05


def linear_attention(nc, ins, ident, tokens):
    with ExitStack() as ctx:
        t = ClearedTools(nc, ctx)
        names = ["kln_weight", "kln_bias", "vln_weight", "vln_bias"]
        column = t.sbuf("lcolumn", [P, 2])
        rows = t.sbuf("lrows", [P, 2, C])
        blocks = t.sbuf("lblocks", [P, C])
        ones = t.sbuf("lones", [P, P])
        factor = [t.sbuf(f"lfactor{i}", [P, C]) for i in range(4)]
        head_sum = [t.sbuf(f"head_sum{i}", [P, NT * HEADS2]) for i in range(2)]
        offset = [t.sbuf(f"offset{i}", [P, N]) for i in range(2)]
        square = [t.sbuf(f"square{i}", [P, N]) for i in range(2)]
        bn = [t.sbuf(f"lbn{i}", [P, NT, 6]) for i in range(2)]
        mv = [t.sbuf(f"lmv{i}", [P, NT, 2]) for i in range(2)]
        var = [t.sbuf(f"lvar{i}", [P, NT * HEADS2 + NT]) for i in range(2)]
        std = [t.sbuf(f"lstd{i}", [P, NT * HEADS2 + NT]) for i in range(2)]
        rstd = [t.sbuf(f"lrstd{i}", [P, NT]) for i in range(2)]
        scale = [t.sbuf(f"lscale{i}", [P, NT * HEADS2]) for i in range(2)]
        z = [t.sbuf(f"z{i}", [P, NT, C + 1]) for i in range(2)]
        u = [t.sbuf(f"lu{i}", [P, NT, C]) for i in range(2)]
        uT = [t.sbuf(f"luT{i}", [P, N]) for i in range(2)]
        sums = [t.sbuf(f"lsums{i}", [P, 1]) for i in range(2)]
        kv = [t.sbuf(f"kv{i}", [P, C]) for i in range(2)]
        turn = [t.psum(f"lturn{h}", [P, HALF]) for h in range(2)]
        gram = [t.psum(f"gram{i}", [P, HALF]) for i in range(2)]
        result = [t.psum(f"lresult{h}", [P, HALF]) for h in range(2)]
        GS = slice(256, 256 + C)

        params_loaded = t.sem("lparams_loaded")
        blocks_ready = t.sem("lblocks_ready")
        pool_steps = t.sem("lpool_steps")
        setup_steps = t.sem("lsetup_steps")
        front_steps = t.sem("lfront_steps")
        back_steps = t.sem("lback_steps")
        offset_ready = t.sem("offset_ready")
        square_ready = t.sem("square_ready")
        var_ready = t.sem("lvar_ready")
        std_ready = t.sem("lstd_ready")
        z_ready = t.sem("z_ready")
        u_ready = t.sem("lu_ready")
        turn_ready = t.sem("lturn_ready")
        uT_ready = t.sem("luT_ready")
        gram_ready = t.sem("gram_ready")
        kv_ready = t.sem("kv_ready")
        result_ready = t.sem("lresult_ready")
        added = t.sem("ladded")
        block = ctx.enter_context(nc.Block())

        @block.sync
        def _(sp):
            for i in range(2):
                sp.dma_start(column[:, i:i + 1], ins["L2_attn_" + names[i]].rearrange("h a d -> (h d) a")
                             ).then_inc(params_loaded, 16)
                sp.dma_start(rows[:, i, :], row_to_all(ins["L2_attn_" + names[2 + i]].rearrange("h a d -> (h a d)"))
                             ).then_inc(params_loaded, 16)

        @block.gpsimd
        def _(pool):
            steps = Steps(pool, pool_steps)
            steps.did(pool.memset(ones[:, :], 1.0))
            for i in range(2):
                steps.did(pool.memset(z[i][:, :, C:C + 1], 1.0))
            steps.then(pool.memset(blocks[:, :], 1.0))
            grid = blocks[:, :].rearrange("p (g c) -> p g c", g=HEADS2)
            steps.then(pool.affine_select(out=grid, in_=grid, compare_op=ALU.is_ge, fill=0.0, base=0,
                                          pattern=[[-HC, HEADS2], [0, HC]], channel_multiplier=1))
            pool.affine_select(out=grid, in_=grid, compare_op=ALU.is_ge, fill=0.0, base=HC - 1,
                               pattern=[[HC, HEADS2], [0, HC]], channel_multiplier=-1).then_inc(blocks_ready, 1)

        @block.vector
        def _(dve):
            steps = Steps(dve, setup_steps)
            dve.wait_ge(params_loaded, 64)
            dve.wait_ge(blocks_ready, 1)
            for i, (col, row, over) in enumerate(((0, 0, 1.0 / N), (0, 1, 1.0 / N), (1, 0, 1.0 / N), (1, 1, 1.0))):
                steps.then(dve.tensor_scalar(factor[i][:, :], rows[:, row, :], column[:, col:col + 1], over,
                                             ALU.mult, ALU.mult))
                steps.then(dve.tensor_tensor(factor[i][:, :], factor[i][:, :], blocks[:, :], ALU.mult))
            steps.then(dve.tensor_tensor(factor[3][:, :], factor[3][:, :], ident[:, :], ALU.add))

            front = Steps(dve, front_steps)
            back = Steps(dve, back_steps)

            def front_half(b, par):
                front.round(b)
                batch = tokens[:, bass.ds(b * NT, NT), :].rearrange("p j (h d) -> p (j h) d", h=HEADS2)
                front.did(dve.tensor_reduce(head_sum[par][:, :], batch, AX.X, ALU.add))
                for j in range(NT):
                    front.did(dve.bn_stats(bn[par][:, j, :], tokens[:, bass.ds(b * NT + j, 1), :]
                                           .rearrange("p a c -> p (a c)")))
                front.settle()
                front.did(dve.tensor_scalar(head_sum[par][:, :], head_sum[par][:, :], 1.0 / HC, None, ALU.mult))
                for j in range(NT):
                    front.did(dve.bn_aggr(mv[par][:, j, :], bn[par][:, j, :]))
                front.settle()
                dve.tensor_tensor(offset[par][:, :].rearrange("p (g d) -> p g d", d=HC), batch,
                                  head_sum[par][:, :].unsqueeze(2).to_broadcast([P, NT * HEADS2, HC]),
                                  ALU.subtract).then_inc(offset_ready, 1)
                front.did(dve.tensor_scalar(var[par][:, NT * HEADS2:], mv[par][:, :, 1], TOKEN_EPS, None, ALU.add))
                dve.wait_ge(square_ready, b + 1)
                front.then(dve.tensor_reduce(head_sum[par][:, :], square[par][:, :].rearrange("p (g d) -> p g d", d=HC),
                                             AX.X, ALU.add))
                dve.tensor_scalar(var[par][:, 0:NT * HEADS2], head_sum[par][:, :], 1.0 / (HC - 1), None,
                                  ALU.mult).then_inc(var_ready, 1)

            def front_rest(b, par):
                dve.wait_ge(std_ready, b + 1)
                front.then(dve.reciprocal(rstd[par][:, :], std[par][:, NT * HEADS2:]))
                for j in range(NT):
                    done = dve.tensor_scalar(u[par][:, j, :], tokens[:, bass.ds(b * NT + j, 1), :]
                                             .rearrange("p a c -> p (a c)"), mv[par][:, j, 0:1],
                                             rstd[par][:, j:j + 1], ALU.subtract, ALU.mult)
                done.then_inc(u_ready, 1)
                scales = scale[par][:, :].rearrange("p (j h) -> p j h", h=HEADS2)
                spread = rstd[par][:, :].unsqueeze(2).to_broadcast([P, NT, HEADS2])
                front.then(dve.tensor_tensor(scales, std[par][:, 0:NT * HEADS2].rearrange("p (j h) -> p j h", h=HEADS2),
                                             spread, ALU.mult))
                front.then(dve.tensor_scalar(scale[par][:, :], scale[par][:, :], HEAD_EPS, None, ALU.add))
                front.then(dve.reciprocal(scale[par][:, :], scale[par][:, :]))
                front.then(dve.tensor_tensor(scales, scales, spread, ALU.mult))
                dve.tensor_tensor(z[par][:, :, 0:C].rearrange("p j (h d) -> p j h d", h=HEADS2),
                                  offset[par][:, :].rearrange("p (j h d) -> p j h d", j=NT, h=HEADS2),
                                  scales.unsqueeze(3).to_broadcast([P, NT, HEADS2, HC]), ALU.mult
                                  ).then_inc(z_ready, 1)

            def combine(b, par):
                back.round(b)
                dve.wait_ge(gram_ready, b + 1)
                back.did(dve.tensor_copy(sums[par][:, :], gram[par][:, C:C + 1]))
                back.then(dve.tensor_tensor(kv[par][:, :], gram[par][:, 0:C], factor[0][:, :], ALU.mult))
                back.then(dve.scalar_tensor_tensor(out=kv[par][:, :], in0=factor[1][:, :], scalar=sums[par][:, 0:1],
                                                   in1=kv[par][:, :], op0=ALU.mult, op1=ALU.add))
                back.then(dve.tensor_tensor(u[par][:, 0, :], gram[par][:, GS], factor[2][:, :], ALU.mult))
                back.then(dve.tensor_tensor(kv[par][:, :], kv[par][:, :], u[par][:, 0, :], ALU.add))
                dve.tensor_tensor(kv[par][:, :], kv[par][:, :], factor[3][:, :], ALU.add).then_inc(kv_ready, 1)

            def add(b, par):
                dve.wait_ge(result_ready, b + 1)
                for h in range(2):
                    rows4 = tokens[:, bass.ds(b * NT + 4 * h, 4), :]
                    done = dve.tensor_tensor(rows4, rows4, result[h][:, :].rearrange("p (a c) -> p a c", a=4), ALU.add)
                done.then_inc(added, 1)

            def batch(b, par, first=False):
                front_half(b, par)
                if not first:
                    combine(b - 1, 1 - par)
                front_rest(b, par)
                if not first:
                    add(b - 1, 1 - par)

            batch(0, 0, first=True)
            batch(1, 1)
            with dve.Fori(2, B - 1, 2) as b:
                batch(b, 0)
                batch(b + 1, 1)
            combine(B - 1, 1)
            add(B - 1, 1)

        @block.scalar
        def _(act):
            def batch(b, par):
                act.wait_ge(offset_ready, b + 1)
                act.activation(square[par][:, :], offset[par][:, :], ACT.Square).then_inc(square_ready, 1)
                act.wait_ge(var_ready, b + 1)
                act.activation(std[par][:, :], var[par][:, :], ACT.Sqrt).then_inc(std_ready, 1)
                act.wait_ge(turn_ready, b + 1)
                for h in range(2):
                    done = act.activation(uT[par][:, HALF * h:HALF * h + HALF], turn[h][:, :], ACT.Copy)
                done.then_inc(uT_ready, 1)

            batch(0, 0)
            batch(1, 1)
            with act.Fori(2, B - 1, 2) as b:
                batch(b, 0)
                batch(b + 1, 1)

        @block.tensor
        def _(pe):
            pe.wait_ge(pool_steps, 4)

            def batch(b, par, first=False):
                pe.wait_ge(u_ready, b + 1)
                if not first:
                    pe.wait_ge(uT_ready, b)
                for j in range(NT):
                    done = pe.transpose(turn[j // 4][:, P * (j % 4):P * (j % 4) + P], u[par][:, j, :], ident[:, :])
                done.then_inc(turn_ready, 1)
                pe.wait_ge(z_ready, b + 1)
                for j in range(NT):
                    pe.matmul(gram[par][:, 0:C + 1], z[par][:, j, 0:C], z[par][:, j, :],
                              start=(j == 0), stop=(j == NT - 1))
                for j in range(NT):
                    done = pe.matmul(gram[par][:, GS], ones[:, :], z[par][:, j, 0:C],
                                     start=(j == 0), stop=(j == NT - 1))
                done.then_inc(gram_ready, 1)

            def give(b, par, first=False):
                pe.wait_ge(kv_ready, b + 1)
                pe.wait_ge(uT_ready, b + 1)
                if not first:
                    pe.wait_ge(added, b)
                for j in range(NT):
                    done = pe.matmul(result[j // 4][:, P * (j % 4):P * (j % 4) + P], uT[par][:, P * j:P * j + P],
                                     kv[par][:, :], start=True, stop=True)
                done.then_inc(result_ready, 1)

            batch(0, 0, first=True)
            give(0, 0, first=True)
            batch(1, 1)
            with pe.Fori(1, B - 2, 2) as b:
                give(b, 1)
                batch(b + 1, 0)
                give(b + 1, 0)
                batch(b + 2, 1)
            give(B - 1, 1)



E = 8
GROUPS = 4
GT = TT // GROUPS
QUADS = -(-(2 * GT + E - 1) // 4)
GS_TILES = 4 * QUADS
SLOT_TILES = GROUPS * GS_TILES
SLOTS = GS_TILES * P
UNIT = 4
UNITS = GT // UNIT
BIG = 3.0e38
ROUND = 1.5 * 2.0 ** 23


class Expert:

    def __init__(self, kind, width):
        self.gelu = kind == "gelu"
        self.width = width
        self.even = width + width % 2
        self.chunks = [(k, min(P, width - k)) for k in range(0, width, P)]


def route(nc, kind, router, rbias, ident, tokens, normed, masks, gates, places, owner, tag):
    with ExitStack() as ctx:
        t = Tools(nc, ctx)
        bn = [t.sbuf(f"{tag}bn{i}", [P, NT, 6]) for i in range(2)]
        mv = [t.sbuf(f"{tag}mv{i}", [P, NT, 2]) for i in range(2)]
        var = [t.sbuf(f"{tag}var{i}", [P, NT]) for i in range(2)]
        std = [t.sbuf(f"{tag}std{i}", [P, NT]) for i in range(2)]
        rstd = [t.sbuf(f"{tag}rstd{i}", [P, NT]) for i in range(2)]
        std2 = [t.sbuf(f"{tag}std2{i}", [P, NT]) for i in range(2)]
        u = [t.sbuf(f"{tag}u{i}", [P, NT, C]) for i in range(2)]
        uT = [t.sbuf(f"{tag}uT{i}", [P, N]) for i in range(2)]
        logits = t.sbuf(f"{tag}logits", [P, TT, E])
        work = t.sbuf(f"{tag}work", [P, TT, E])
        best = [t.sbuf(f"{tag}best{i}", [P, TT]) for i in range(2)]
        first = t.sbuf(f"{tag}first", [P, TT])
        rank = t.sbuf(f"{tag}rank", [P, E])
        rank_i = t.sbuf(f"{tag}rank_i", [P, E], I32)
        chosen = t.sbuf(f"{tag}chosen", [P, GROUPS, E, GT], BF16)
        upper = t.sbuf(f"{tag}upper", [P, P], BF16)
        ones = t.sbuf(f"{tag}ones", [P, P], BF16)
        ones_row = t.sbuf(f"{tag}ones_row", [P, GROUPS * E * GT])
        count = t.sbuf(f"{tag}count", [P, GROUPS * E, GT])
        before = t.sbuf(f"{tag}before", [P, GROUPS * E, GT])
        total = t.sbuf(f"{tag}total", [P, GROUPS, E])
        running = t.sbuf(f"{tag}running", [P, GROUPS, E])
        padded = t.sbuf(f"{tag}padded", [P, GROUPS, E])
        ends = t.sbuf(f"{tag}ends", [P, GROUPS, E])
        shift = t.sbuf(f"{tag}shift", [P, GROUPS, E])
        slot_i = t.sbuf(f"{tag}slot_i", [1, GS_TILES], I32)
        slot_f = t.sbuf(f"{tag}slot_f", [1, GS_TILES])
        passed = t.sbuf(f"{tag}passed", [1, GS_TILES, E])
        owner_f = t.sbuf(f"{tag}owner_f", [1, SLOT_TILES])
        slot_no = t.sbuf(f"{tag}slot_no", [P, TT, 2])
        part_i = [t.sbuf(f"{tag}part{i}", [P, TT, 2], I32) for i in range(2)]
        turn = [[t.psum(f"{tag}turn{i}{h}", [P, HALF]) for h in range(2)] for i in range(2)]
        score = [t.psum(f"{tag}score{i}", [P, HALF]) for i in range(2)]
        ahead = t.psum(f"{tag}ahead", [P, HALF])
        totals = t.psum(f"{tag}totals", [P, HALF])

        constants = t.sem(f"{tag}constants")
        pool_steps = t.sem(f"{tag}pool_steps")
        front_steps = t.sem(f"{tag}front_steps")
        steps_sem = t.sem(f"{tag}steps")
        var_ready = t.sem(f"{tag}var_ready")
        std_ready = t.sem(f"{tag}std_ready")
        u_ready = t.sem(f"{tag}u_ready")
        copied = t.sem(f"{tag}copied")
        turn_ready = t.sem(f"{tag}turn_ready")
        uT_ready = t.sem(f"{tag}uT_ready")
        score_ready = t.sem(f"{tag}score_ready")
        score_taken = t.sem(f"{tag}score_taken")
        exp_asked = t.sem(f"{tag}exp_asked")
        exp_done = t.sem(f"{tag}exp_done")
        chosen_ready = t.sem(f"{tag}chosen_ready")
        counted = t.sem(f"{tag}counted")
        norms = 2 if kind.gelu else 1
        block = ctx.enter_context(nc.Block())

        @block.gpsimd
        def _(pool):
            steps = Steps(pool, pool_steps)
            steps.did(pool.iota(rank_i[:, :], [[-1, E]], base=E, channel_multiplier=0))
            steps.did(pool.iota(slot_i[:, :], [[P, GS_TILES]], base=0, channel_multiplier=0))
            steps.did(pool.memset(ones[:, :], 1.0))
            steps.did(pool.memset(ones_row[:, :], 1.0))
            steps.then(pool.memset(upper[:, :], 1.0))
            steps.did(pool.tensor_copy(rank[:, :], rank_i[:, :]))
            steps.did(pool.tensor_copy(slot_f[:, :], slot_i[:, :]))
            steps.then(pool.affine_select(out=upper[:, :], in_=upper[:, :], compare_op=ALU.is_gt, fill=0.0, base=0,
                                          pattern=[[1, P]], channel_multiplier=-1))
            pool.memset(owner_f[:, :], 0.0).then_inc(constants, 1)

            def keep(b, par):
                pool.wait_ge(u_ready, b + 1)
                pool.tensor_copy(normed[:, bass.ds(b * NT, NT), :], u[par][:, :, :]).then_inc(copied, 1)
            keep(0, 0)
            keep(1, 1)
            with pool.Fori(2, B - 1, 2) as b:
                keep(b, 0)
                keep(b + 1, 1)

        @block.tensor
        def _(pe):
            def turn_batch(b, par, first=False):
                pe.wait_ge(u_ready, b + 1)
                if not first:
                    pe.wait_ge(uT_ready, b - 1)
                for j in range(NT):
                    done = pe.transpose(turn[par][j // 4][:, P * (j % 4):P * (j % 4) + P], u[par][:, j, :], ident[:, :])
                done.then_inc(turn_ready, 1)

            def score_batch(b, par, first=False):
                pe.wait_ge(uT_ready, b + 1)
                if not first:
                    pe.wait_ge(score_taken, b - 1)
                for j in range(NT):
                    done = pe.matmul(score[par][:, E * j:E * j + E], uT[par][:, P * j:P * j + P], router[:, :],
                                     start=True, stop=True)
                done.then_inc(score_ready, 1)

            turn_batch(0, 0, first=True)
            turn_batch(1, 1, first=True)
            score_batch(0, 0, first=True)
            turn_batch(2, 0)
            score_batch(1, 1, first=True)
            with pe.Fori(2, B - 3, 2) as b:
                for par in range(2):
                    turn_batch(b + par + 1, 1 - par)
                    score_batch(b + par, par)
            turn_batch(B - 1, 1)
            score_batch(B - 2, 0)
            score_batch(B - 1, 1)
            pe.wait_ge(constants, 1)
            pe.wait_ge(chosen_ready, 1)
            flat = chosen[:, :, :, :].rearrange("p g e t -> p (g e t)")
            pe.matmul(ahead[:, :], upper[:, :], flat, start=True, stop=True).then_inc(counted, 1)
            pe.matmul(totals[:, :], ones[:, :], flat, start=True, stop=True).then_inc(counted, 1)

        @block.scalar
        def _(act):
            def batch(b, par, first=False):
                act.wait_ge(var_ready, b * norms + 1)
                act.activation(std[par][:, :], var[par][:, :], ACT.Sqrt).then_inc(std_ready, 1)
                if kind.gelu:
                    act.wait_ge(var_ready, b * norms + 2)
                    act.activation(std2[par][:, :], var[par][:, :], ACT.Sqrt).then_inc(std_ready, 1)
                act.wait_ge(turn_ready, b + 1)
                for h in range(2):
                    done = act.activation(uT[par][:, HALF * h:HALF * h + HALF], turn[par][h][:, :], ACT.Copy)
                done.then_inc(uT_ready, 1)
            batch(0, 0, True)
            batch(1, 1, True)
            with act.Fori(2, B - 1, 2) as b:
                for par in range(2):
                    act.wait_ge(score_ready, b + par - 1)
                    batch(b + par, par)
            act.wait_ge(exp_asked, 1)
            act.activation(work[:, :, :], work[:, :, :], ACT.Exp).then_inc(exp_done, 1)
            act.activation(best[1][:, :], best[1][:, :], ACT.Exp).then_inc(exp_done, 1)

        @block.vector
        def _(dve):
            front = Steps(dve, front_steps)

            def normalise(b, par, first=False):
                front.round(b)
                for j in range(NT):
                    front.did(dve.bn_stats(bn[par][:, j, :], tokens[:, bass.ds(b * NT + j, 1), :]
                                           .rearrange("p a c -> p (a c)")))
                if not first:
                    dve.wait_ge(copied, b - 1)
                    dve.wait_ge(turn_ready, b - 1)
                front.settle()
                front.did(dve.tensor_copy(rstd[par][:, 0:1], bn[par][:, 0, 0:1]))
                for j in range(NT):
                    front.did(dve.bn_aggr(mv[par][:, j, :], bn[par][:, j, :]))
                front.settle()
                dve.tensor_scalar(var[par][:, :], mv[par][:, :, 1], TOKEN_EPS, None, ALU.add).then_inc(var_ready, 1)
                dve.wait_ge(std_ready, b * norms + 1)
                front.then(dve.reciprocal(rstd[par][:, :], std[par][:, :]))
                if kind.gelu:
                    front.then(dve.tensor_tensor(var[par][:, :], rstd[par][:, :], rstd[par][:, :], ALU.mult))
                    front.then(dve.tensor_tensor(var[par][:, :], var[par][:, :], mv[par][:, :, 1], ALU.mult))
                    dve.tensor_scalar(var[par][:, :], var[par][:, :], TOKEN_EPS, None, ALU.add).then_inc(var_ready, 1)
                    dve.wait_ge(std_ready, b * norms + 2)
                    front.then(dve.reciprocal(var[par][:, :], std2[par][:, :]))
                    front.then(dve.tensor_tensor(rstd[par][:, :], rstd[par][:, :], var[par][:, :], ALU.mult))
                for j in range(NT):
                    done = dve.tensor_scalar(u[par][:, j, :], tokens[:, bass.ds(b * NT + j, 1), :]
                                             .rearrange("p a c -> p (a c)"), mv[par][:, j, 0:1],
                                             rstd[par][:, j:j + 1], ALU.subtract, ALU.mult)
                done.then_inc(u_ready, 1)

            def take_scores(b, par):
                dve.wait_ge(score_ready, b + 1)
                rows = logits[:, bass.ds(b * NT, NT), :]
                given = score[par][:, 0:NT * E].rearrange("p (j e) -> p j e", e=E)
                if kind.gelu:
                    dve.tensor_tensor(rows, given, std2[par][:, :].unsqueeze(2).to_broadcast([P, NT, E]),
                                      ALU.mult).then_inc(score_taken, 1)
                else:
                    dve.tensor_copy(rows, given).then_inc(score_taken, 1)

            normalise(0, 0, first=True)
            normalise(1, 1, first=True)
            with dve.Fori(2, B - 1, 2) as b:
                for par in range(2):
                    take_scores(b + par - 2, par)
                    normalise(b + par, par)
            take_scores(B - 2, 0)
            take_scores(B - 1, 1)

            steps = Steps(dve, steps_sem)
            dve.wait_ge(score_taken, B)
            dve.wait_ge(constants, 1)
            over_e = [P, TT, E]
            if kind.gelu:
                steps.then(dve.tensor_tensor(logits[:, :, :], logits[:, :, :],
                                             rbias[:, :].unsqueeze(1).to_broadcast(over_e), ALU.add))
            ranks = rank[:, :].unsqueeze(1).to_broadcast(over_e)
            for r in range(2):
                steps.then(dve.tensor_reduce(best[r][:, :], logits[:, :, :] if r == 0 else work[:, :, :],
                                             AX.X, ALU.max))
                steps.then(dve.tensor_tensor(masks[r][:, :, :], logits[:, :, :] if r == 0 else work[:, :, :],
                                             best[r][:, :].unsqueeze(2).to_broadcast(over_e), ALU.is_ge))
                steps.then(dve.tensor_tensor(masks[r][:, :, :], masks[r][:, :, :], ranks, ALU.mult))
                steps.then(dve.tensor_reduce(first[:, :], masks[r][:, :, :], AX.X, ALU.max))
                steps.then(dve.tensor_tensor(masks[r][:, :, :], masks[r][:, :, :],
                                             first[:, :].unsqueeze(2).to_broadcast(over_e), ALU.is_equal))
                if r == 0:
                    steps.then(dve.scalar_tensor_tensor(out=work[:, :, :], in0=masks[0][:, :, :], scalar=-BIG,
                                                        in1=logits[:, :, :], op0=ALU.mult, op1=ALU.add))
            dve.tensor_tensor(chosen[:, :, :, :].rearrange("p g e t -> p g t e"),
                              masks[0][:, :, :].rearrange("p (g t) e -> p g t e", g=GROUPS),
                              masks[1][:, :, :].rearrange("p (g t) e -> p g t e", g=GROUPS),
                              ALU.add).then_inc(chosen_ready, 1)

            steps.did(dve.tensor_tensor(work[:, :, :], logits[:, :, :],
                                        best[0][:, :].unsqueeze(2).to_broadcast(over_e), ALU.subtract))
            dve.tensor_tensor(best[1][:, :], best[1][:, :], best[0][:, :], ALU.subtract).then_inc(exp_asked, 1)
            dve.wait_ge(exp_done, 2)
            if kind.gelu:
                steps.then(dve.tensor_scalar(best[0][:, :], best[1][:, :], 1.0, None, ALU.add))
            else:
                steps.then(dve.tensor_reduce(first[:, :], work[:, :, :], AX.X, ALU.add))
                steps.then(dve.scalar_tensor_tensor(out=best[0][:, :], in0=first[:, :], scalar=1e-09,
                                                    in1=best[1][:, :], op0=ALU.mult, op1=ALU.add))
                steps.then(dve.tensor_scalar(best[0][:, :], best[0][:, :], 1.0, None, ALU.add))
            steps.then(dve.reciprocal(best[0][:, :], best[0][:, :]))
            steps.did(dve.tensor_copy(gates[:, :, 0], best[0][:, :]))
            steps.did(dve.tensor_tensor(gates[:, :, 1], best[1][:, :], best[0][:, :], ALU.mult))

            dve.wait_ge(counted, 2)
            flat = lambda x: x[:, :, :].rearrange("p a b -> p (a b)")
            steps.then(dve.tensor_copy(flat(count), totals[:, :]))
            steps.did(dve.tensor_tensor_scan(flat(before), ones_row[:, :], flat(count), 0.0, ALU.mult, ALU.add))
            steps.then(dve.tensor_reduce(flat(total), count[:, :, :], AX.X, ALU.add))
            steps.did(dve.tensor_tensor_scan(flat(running), ones_row[:, 0:GROUPS * E], flat(total), 0.0,
                                             ALU.mult, ALU.add))
            steps.then(dve.tensor_scalar(flat(padded), flat(total), (P - 1) / 2.0, 1.0 / P, ALU.add, ALU.mult))
            steps.then(dve.tensor_scalar(flat(padded), flat(padded), ROUND, None, ALU.add))
            steps.then(dve.tensor_scalar(flat(padded), flat(padded), -ROUND, float(P), ALU.add, ALU.mult))
            for g in range(GROUPS):
                steps.did(dve.tensor_tensor_scan(ends[:, g, :], ones_row[:, 0:E], padded[:, g, :], 0.0,
                                                 ALU.mult, ALU.add))
            steps.settle()
            steps.did(dve.tensor_tensor(flat(shift), flat(ends), flat(padded), ALU.subtract))
            steps.did(dve.tensor_tensor(flat(total), flat(running), flat(total), ALU.subtract))
            steps.then(dve.tensor_tensor(flat(before), flat(before), flat(count), ALU.subtract))
            steps.did(dve.tensor_tensor(flat(shift), flat(shift), flat(total), ALU.subtract))
            steps.then(dve.tensor_tensor(flat(before), flat(before), ahead[:, :], ALU.add))
            steps.then(dve.tensor_tensor(before[:, :, :], before[:, :, :],
                                         flat(shift).unsqueeze(2).to_broadcast([P, GROUPS * E, GT]), ALU.add))
            for r in range(2):
                steps.then(dve.tensor_tensor(work[:, :, :].rearrange("p (g t) e -> p g t e", g=GROUPS),
                                             masks[r][:, :, :].rearrange("p (g t) e -> p g t e", g=GROUPS),
                                             before[:, :, :].rearrange("p (g e) t -> p g t e", g=GROUPS), ALU.mult))
                steps.then(dve.tensor_reduce(slot_no[:, :, r], work[:, :, :], AX.X, ALU.add))
            steps.then(dve.tensor_copy(flat(part_i[0]), flat(slot_no)))
            steps.did(dve.tensor_scalar(flat(places), flat(part_i[0]), -4 * P, None, ALU.bitwise_and))
            steps.did(dve.tensor_scalar(flat(part_i[1]), flat(part_i[0]), P - 1, 2, ALU.bitwise_and,
                                        ALU.logical_shift_left))
            steps.settle()
            steps.then(dve.tensor_scalar(flat(part_i[0]), flat(part_i[0]), 7, 3, ALU.logical_shift_right,
                                         ALU.bitwise_and))
            steps.then(dve.tensor_tensor(flat(places), flat(places), flat(part_i[1]), ALU.bitwise_or))
            steps.then(dve.tensor_tensor(flat(places), flat(places), flat(part_i[0]), ALU.bitwise_or))
            for g in range(GROUPS):
                steps.then(dve.tensor_tensor(passed[:, :, :], ends[0:1, g, :].unsqueeze(1).to_broadcast([1, GS_TILES, E]),
                                             slot_f[:, :].unsqueeze(2).to_broadcast([1, GS_TILES, E]), ALU.is_le))
                steps.then(dve.tensor_reduce(owner_f[:, GS_TILES * g:GS_TILES * g + GS_TILES], passed[:, :, :],
                                             AX.X, ALU.add))
            steps.then(dve.tensor_scalar(owner_f[:, :], owner_f[:, :], float(E - 1), None, ALU.min))
            eights = owner_f[:, :].rearrange("a (q k) -> a q k", k=8)
            for k in range(6, -1, -1):
                steps.then(dve.scalar_tensor_tensor(out=eights[:, :, k], in0=eights[:, :, k + 1], scalar=float(E),
                                                    in1=eights[:, :, k], op0=ALU.mult, op1=ALU.add))
            steps.then(dve.tensor_copy(owner[:, :], eights[:, :, 0]))


def run_experts(nc, kind, w_up, w_gate, w_down, up_bias, down_bias, ident, tokens, normed, gates, places,
                owner, sorted_rows, sorted_results, tag):
    row_quads = [x.rearrange("(q p k) c -> q p (k c)", p=P, k=4) for x in sorted_rows]
    result_quads = [x.rearrange("(q p k) c -> q p (k c)", p=P, k=4) for x in sorted_results]
    W, WE = kind.width, kind.even
    chunks = kind.chunks
    whole = sum(width == P for _, width in chunks)
    with ExitStack() as ctx:
        t = Tools(nc, ctx)
        send = [t.sbuf(f"{tag}send{i}", [P, UNIT, C]) for i in range(2)]
        send_at = [t.sbuf(f"{tag}send_at{i}", [P, UNIT, 2], I32) for i in range(2)]
        fetch = [t.sbuf(f"{tag}fetch{i}", [P, UNIT, 2, C]) for i in range(2)]
        fetch_at = [t.sbuf(f"{tag}fetch_at{i}", [P, UNIT, 2], I32) for i in range(2)]
        xq = [t.sbuf(f"{tag}xq{i}", [P, 4, C]) for i in range(2)]
        yq = [t.sbuf(f"{tag}yq{i}", [P, 4, C]) for i in range(2)]
        xT = [t.sbuf(f"{tag}xT_{part}", [P, 4, P], F32R) for part in ("high", "low")]
        silu = None if kind.gelu else [t.sbuf(f"{tag}silu{i}", [P, W]) for i in range(2)]
        hidden = [t.sbuf(f"{tag}hidden{i}", [P, W]) for i in range(2)]
        hT = [t.sbuf(f"{tag}hT{i}", [P, len(chunks), P]) for i in range(2)]
        ones = t.sbuf(f"{tag}ones", [3, P], BF16)
        up = [t.psum(f"{tag}up{i}", [P, HALF]) for i in range(2)]
        gate = None if kind.gelu else [t.psum(f"{tag}gate{i}", [P, HALF]) for i in range(2)]
        hturn = [t.psum(f"{tag}hturn{i}", [P, HALF]) for i in range(2)]
        xturn = t.psum(f"{tag}xturn", [P, P])
        down = t.psum(f"{tag}down", [P, C])

        staged = t.sem(f"{tag}staged")
        indexed = t.sem(f"{tag}indexed")
        sent = [t.sem(f"{tag}sent{i}") for i in range(2)]
        fetched = [t.sem(f"{tag}fetched{i}") for i in range(2)]
        fetch_used = t.sem(f"{tag}fetch_used")
        x_loaded = [t.sem(f"{tag}x_loaded{i}") for i in range(2)]
        y_stored = [t.sem(f"{tag}y_stored{i}") for i in range(2)]
        ones_ready = t.sem(f"{tag}ones_ready")
        x_turned = t.sem(f"{tag}x_turned")
        x_high = t.sem(f"{tag}x_high")
        xT_ready = t.sem(f"{tag}xT_ready")
        up_done = t.sem(f"{tag}up_done")
        silu_ready = None if kind.gelu else t.sem(f"{tag}silu_ready")
        hidden_ready = t.sem(f"{tag}hidden_ready")
        h_turned = t.sem(f"{tag}h_turned")
        hT_ready = t.sem(f"{tag}hT_ready")
        down_done = t.sem(f"{tag}down_done")
        y_ready = t.sem(f"{tag}y_ready")
        added = t.sem(f"{tag}added")
        block = ctx.enter_context(nc.Block())
        last = SLOT_TILES - 1

        def known(s, least):
            return not isinstance(s, int) or s >= least

        @block.gpsimd
        def _(pool):
            pool.memset(ones[:, :], 1.0).then_inc(ones_ready, 1)
            sent_goal = [pool.alloc_register(f"{tag}sent_goal{i}") for i in range(2)]
            used_goal = [pool.alloc_register(f"{tag}used_goal{i}") for i in range(2)]
            staged_goal = pool.alloc_register(f"{tag}staged_goal")
            indexed_goal = pool.alloc_register(f"{tag}indexed_goal")
            for i in range(2):
                pool.reg_mov(sent_goal[i], 2 * UNIT * 16)
                pool.reg_mov(used_goal[i], 1 + i)
            pool.reg_mov(staged_goal, 2)
            pool.reg_mov(indexed_goal, 1)

            def send_unit(g, n, par):
                if known(n, 2):
                    pool.wait_ge(sent[par], sent_goal[par])
                    pool.reg_add(sent_goal[par], sent_goal[par], 2 * UNIT * 16)
                pool.tensor_copy(send[par][:, :, :], normed[:, bass.ds(n * UNIT, UNIT), :]).then_inc(staged, 1)
                pool.tensor_copy(send_at[par][:, :, :], places[:, bass.ds(n * UNIT, UNIT), :]).then_inc(staged, 1)
                pool.wait_ge(staged, staged_goal)
                pool.reg_add(staged_goal, staged_goal, 2)
                for i in range(UNIT):
                    for r in range(2):
                        pool.indirect_dma_start(
                            out=sorted_rows[g], out_offset=bass.IndirectOffsetOnAxis(ap=send_at[par][:, i, r:r + 1], axis=0),
                            in_=send[par][:, i, :], in_offset=None).then_inc(sent[par], 16)

            def fetch_unit(g, n, par):
                if known(n, 2):
                    pool.wait_ge(fetch_used, used_goal[par])
                    pool.reg_add(used_goal[par], used_goal[par], 2)
                pool.tensor_copy(fetch_at[par][:, :, :], places[:, bass.ds(n * UNIT, UNIT), :]).then_inc(indexed, 1)
                pool.wait_ge(indexed, indexed_goal)
                pool.reg_add(indexed_goal, indexed_goal, 1)
                for i in range(UNIT):
                    for r in range(2):
                        pool.indirect_dma_start(
                            out=fetch[par][:, i, r, :], out_offset=None, in_=sorted_results[g],
                            in_offset=bass.IndirectOffsetOnAxis(ap=fetch_at[par][:, i, r:r + 1], axis=0)
                            ).then_inc(fetched[par], 16)

            def over_units(g, unit):
                start = g * UNITS
                if g == 0:
                    unit(g, 0, 0)
                    unit(g, 1, 1)
                    start = 2
                if start < (g + 1) * UNITS:
                    with pool.Fori(start, (g + 1) * UNITS - 1, 2) as n:
                        unit(g, n, 0)
                        unit(g, n + 1, 1)

            def fetch_group(g):
                for par in range(2):
                    pool.wait_ge(y_stored[par], 16 * (g + 1) * QUADS // 2)
                over_units(g, fetch_unit)

            over_units(0, send_unit)
            for g in range(1, GROUPS):
                over_units(g, send_unit)
                fetch_group(g - 1)
            fetch_group(GROUPS - 1)

        @block.sync
        def _(sp):
            def load(g, q, par):
                if known(q, 2) or g > 0:
                    sp.wait_ge(x_turned, q * 4 + (g * GS_TILES - 4))
                sp.dma_start(xq[par][:, :, :], row_quads[g][bass.ds(q, 1), :, :].rearrange("a p (k c) -> p (a k) c", k=4)
                             ).then_inc(x_loaded[par], 16)

            def store(g, q, par):
                sp.wait_ge(y_ready, q * 4 + (g * GS_TILES + 4))
                sp.dma_start(result_quads[g][bass.ds(q, 1), :, :].rearrange("a p (k c) -> p (a k) c", k=4),
                             yq[par][:, :, :]).then_inc(y_stored[par], 16)

            for g in range(GROUPS):
                for par in range(2):
                    sp.wait_ge(sent[par], (g + 1) * (UNITS // 2) * 2 * UNIT * 16)
                for par in range(2):
                    load(g, par, par)
                    if g > 0:
                        store(g - 1, QUADS - 2 + par, par)
                with sp.Fori(2, QUADS - 1, 2) as q:
                    for par in range(2):
                        load(g, q + par, par)
                        store(g, q + par - 2, par)
            store(GROUPS - 1, QUADS - 2, 0)
            store(GROUPS - 1, QUADS - 1, 1)
            for par in range(2):
                sp.wait_ge(y_stored[par], 16 * GROUPS * QUADS // 2)

        @block.tensor
        def _(pe):
            def owners(q):
                word = pe.value_load(owner[0:1, bass.ds(q, 1)], min_val=0, max_val=E ** 8 - 1)
                return [(word >> 3 * k) & E - 1 for k in range(8)]

            def product(out, left, right, final=True):
                for i, (l, r) in enumerate(((0, 0), (0, 1), (1, 0))):
                    done = pe.matmul(out, left[l], right[r], start=(i == 0), stop=(final and i == 2))
                return done

            def turn_x(s, k, qpar):
                if k == 0:
                    pe.wait_ge(x_loaded[qpar], (s - 4 * qpar) * 2 + 16)
                if known(s, 1):
                    pe.wait_ge(xT_ready, s)
                pe.transpose(xturn[:, :], xq[qpar][:, k, :], ident[:, :]).then_inc(x_turned, 1)

            def go_up(s, k, e):
                par = k % 2
                pe.wait_ge(xT_ready, s + 1)
                if known(s, 2):
                    pe.wait_ge(hidden_ready, s - 1)
                left = [part[:, k, :] for part in xT]
                rows = lambda w: [part[:, bass.ds(e, 1), 0:WE].rearrange("p a h -> p (a h)") for part in w]
                done = product(up[par][:, 0:WE], left, rows(w_up), final=not kind.gelu)
                if kind.gelu:
                    done = pe.matmul(up[par][:, 0:W], ones[:, :],
                                     up_bias[:, bass.ds(e, 1), :].rearrange("p a h -> p (a h)"), start=False, stop=True)
                else:
                    done = product(gate[par][:, 0:WE], left, rows(w_gate))
                done.then_inc(up_done, 1)

            def turn_hidden(s, par):
                pe.wait_ge(hidden_ready, s + 1)
                if known(s, 2):
                    pe.wait_ge(hT_ready, s - 1)
                for i, (at, width) in enumerate(chunks):
                    done = pe.transpose(hturn[par][0:width, P * i:P * i + P], hidden[par][:, at:at + width], ident[:, :])
                done.then_inc(h_turned, 1)

            def go_down(s, par, e):
                pe.wait_ge(hT_ready, s + 1)
                if known(s, 1):
                    pe.wait_ge(y_ready, s)
                for i, (at, width) in enumerate(chunks):
                    done = pe.matmul(down[:, :], hT[par][0:width, i, :],
                                     w_down[0:width, bass.ds(e, 1), i, :].rearrange("p a c -> p (a c)"),
                                     start=(i == 0), stop=(i == len(chunks) - 1 and not kind.gelu))
                if kind.gelu:
                    done = pe.matmul(down[:, :], ones[:, :],
                                     down_bias[:, bass.ds(e, 1), :].rearrange("p a c -> p (a c)"), start=False, stop=True)
                done.then_inc(down_done, 1)

            def step(s, k, qpar, e, e_down, ending=False):
                if not (ending and k == 3):
                    turn_x(s + 1, (k + 1) % 4, qpar if k < 3 else 1 - qpar)
                go_up(s, k, e)
                if known(s, 1):
                    turn_hidden(s - 1, 1 - k % 2)
                if known(s, 2):
                    go_down(s - 2, k % 2, e_down)

            if kind.gelu:
                pe.wait_ge(ones_ready, 1)
            turn_x(0, 0, 0)
            e = owners(0)
            for k in range(8):
                step(k, k % 4, k // 4, e[k], e[k - 2])
            with pe.Fori(1, SLOT_TILES // 8 - 1, 1) as q:
                e = owners(q - 1)[6:] + owners(q)
                for k in range(8):
                    step(q * 8 + k, k % 4, k // 4, e[2 + k], e[k])
            e = owners(SLOT_TILES // 8 - 2)[6:] + owners(SLOT_TILES // 8 - 1)
            for k in range(8):
                step(SLOT_TILES - 8 + k, k % 4, k // 4, e[2 + k], e[k], ending=(k // 4 == 1))
            turn_hidden(last, 1)
            go_down(last - 1, 0, e[8])
            go_down(last, 1, e[9])

        @block.scalar
        def _(act):
            def act_hidden(s, par):
                act.wait_ge(up_done, s + 1)
                if kind.gelu:
                    if known(s, 2):
                        act.wait_ge(h_turned, s - 1)
                    act.activation(hidden[par][:, :], up[par][:, 0:W], ACT.Gelu).then_inc(hidden_ready, 1)
                else:
                    if known(s, 2):
                        act.wait_ge(hidden_ready, s - 1)
                    act.activation(silu[par][:, :], up[par][:, 0:W], ACT.Silu).then_inc(silu_ready, 1)

            def take_hidden(s, par):
                act.wait_ge(h_turned, s + 1)
                if known(s, 2):
                    act.wait_ge(down_done, s - 1)
                done = act.activation(hT[par][:, 0:whole, :],
                                      hturn[par][:, 0:P * whole].rearrange("p (k m) -> p k m", m=P), ACT.Copy)
                if whole < len(chunks):
                    width = chunks[whole][1]
                    done = act.activation(hT[par][0:width, whole, :], hturn[par][0:width, P * whole:P * whole + P],
                                          ACT.Copy)
                done.then_inc(hT_ready, 1)

            def step(s, k):
                act_hidden(s, k % 2)
                if known(s, 1):
                    take_hidden(s - 1, 1 - k % 2)

            for k in range(4):
                step(k, k)
            with act.Fori(4, SLOT_TILES - 3, 4) as s:
                for k in range(4):
                    step(s + k, k)
            take_hidden(last, 1)

        @block.vector
        def _(dve):
            def take_x_high(s, k):
                dve.wait_ge(x_turned, s + 1)
                if known(s, 4):
                    dve.wait_ge(up_done, s - 3)
                dve.tensor_copy(xT[0][:, k, :], xturn[:, :]).then_inc(x_high, 1)

            def take_x_low(s, k):
                dve.wait_ge(x_high, s + 1)
                dve.tensor_tensor(xT[1][:, k, :], xturn[:, :], xT[0][:, k, :].bitcast(F32), ALU.subtract
                                  ).then_inc(xT_ready, 1)

            def gate_hidden(s, par):
                dve.wait_ge(silu_ready, s + 1)
                if known(s, 2):
                    dve.wait_ge(h_turned, s - 1)
                dve.tensor_tensor(hidden[par][:, :], silu[par][:, :], gate[par][:, 0:W], ALU.mult
                                  ).then_inc(hidden_ready, 1)

            def take_down(s, k, qpar):
                if k == 0 and known(s, 8):
                    dve.wait_ge(y_stored[qpar], (s - 4 * qpar) * 2)
                dve.wait_ge(down_done, s + 1)
                dve.tensor_copy(yq[qpar][:, k, :], down[:, :]).then_inc(y_ready, 1)

            def add_result(n, i, par, r):
                if i == 0 and r == 0:
                    dve.wait_ge(fetched[par], (n - par) * (UNIT * 16) + 2 * UNIT * 16)
                if r == 1:
                    dve.wait_ge(added, n * UNIT + (i + 1))
                row = tokens[:, bass.ds(n * UNIT + i, 1), :].rearrange("p a c -> p (a c)")
                done = dve.scalar_tensor_tensor(
                    out=row, in0=fetch[par][:, i, r, :],
                    scalar=gates[:, bass.ds(n * UNIT + i, 1), r:r + 1].rearrange("p a b -> p (a b)"),
                    in1=row, op0=ALU.mult, op1=ALU.add)
                if r == 0:
                    done.then_inc(added, 1)
                elif i == UNIT - 1:
                    done.then_inc(fetch_used, 1)

            def step(s, k, qpar, ending=False, unit=None):
                more = not (ending and k == 3)
                if more:
                    take_x_high(s + 1, (k + 1) % 4)
                if unit:
                    add_result(unit[0], k, unit[1], 0)
                if known(s, 3):
                    take_down(s - 3, (k + 1) % 4, qpar if k == 3 else 1 - qpar)
                if more:
                    take_x_low(s + 1, (k + 1) % 4)
                if not kind.gelu:
                    gate_hidden(s, k % 2)
                if unit:
                    add_result(unit[0], k, unit[1], 1)

            take_x_high(0, 0)
            take_x_low(0, 0)
            for k in range(4):
                step(k, k, 0)
            for k in range(4):
                step(4 + k, k, 1)
            with dve.Fori(8, GS_TILES - 7, 8) as s:
                for k in range(8):
                    step(s + k, k % 4, 0 if k < 4 else 1)
            for g in range(1, GROUPS):
                start = g * GS_TILES
                for k in range(8):
                    step(start + k, k % 4, k // 4)
                with dve.Fori(0, UNITS - 1, 2) as n:
                    for k in range(8):
                        step(n * 4 + (start + 8 + k), k % 4, k // 4, unit=(n + ((g - 1) * UNITS + k // 4), k // 4))
                end = (g + 1) * GS_TILES
                final = end - 8 if g == GROUPS - 1 else end
                with dve.Fori(start + 8 + 4 * UNITS, final - 7, 8) as s:
                    for k in range(8):
                        step(s + k, k % 4, k // 4)
            for k in range(8):
                step(SLOT_TILES - 8 + k, k % 4, k // 4, ending=(k // 4 == 1))
            take_down(last - 2, 1, 1)
            take_down(last - 1, 2, 1)
            take_down(last, 3, 1)
            with dve.Fori((GROUPS - 1) * UNITS, GROUPS * UNITS - 1, 2) as n:
                for par in range(2):
                    for r in range(2):
                        for i in range(UNIT):
                            add_result(n + par, i, par, r)


def experts_gelu(nc, ins, ident, tokens, sorted_rows, sorted_results):
    kind = Expert("gelu", 512)
    W = kind.width
    HC = W // P
    with ExitStack() as ctx:
        t = Tools(nc, ctx)
        gates = t.sbuf("g_gates", [P, TT, 2])
        places = t.sbuf("g_places", [P, TT, 2], I32)
        owner = t.sbuf("g_owner", [1, SLOT_TILES // 8], I32)
        w_up = [t.sbuf(f"g_w_up_{part}", [P, E, W], F32R) for part in ("high", "low")]
        w_down = t.sbuf("g_w_down", [P, E, HC, C])
        up_bias = t.sbuf("g_up_bias", [3, E, W], BF16)
        down_bias = t.sbuf("g_down_bias", [3, E, C], BF16)
        router = t.sbuf("g_router", [P, E])
        rbias = t.sbuf("g_rbias", [P, E])
        with ExitStack() as setup:
            t = Tools(nc, setup)
            raw_up = t.sbuf("g_raw_up", [P, E, W])
            scale = t.sbuf("g_scale", [P, E])
            shift = t.sbuf("g_shift", [P, E])
            bias = [t.sbuf("g_bias_up", [E * HC, P]), t.sbuf("g_bias_down", [E, C])]
            parts = [[t.sbuf(f"g_part{i}{m}", [rows, P], BF16) for i in range(3)] for m, rows in enumerate((E * HC, E))]
            extra_sb = t.sbuf("g_extra_sb", [P, E * HC])
            extra = t.psum("g_extra", [P, E * HC])
            extraT = t.psum("g_extraT", [E * HC, P])
            loaded = [t.sem(f"g_loaded{i}") for i in range(3)]
            extra_ready = t.sem("g_extra_ready")
            extra_taken = t.sem("g_extra_taken")
            extra_turned = t.sem("g_extra_turned")
            scaled = t.sem("g_scaled")
            splits = t.sem("g_splits")
            parts_ready = t.sem("g_parts_ready")
            highs = t.sem("g_highs")
            placed = t.sem("g_placed")
            block = setup.enter_context(nc.Block())

            @block.sync
            def _(sp):
                sp.dma_start(raw_up[:, :, :], ins["L2_ffn_W1"].rearrange("e c h -> c e h")).then_inc(loaded[0], 16)
                sp.dma_start(shift[:, :], ins["L2_ffn_ln_b"].rearrange("e c -> c e"), allow_slow_non_contiguous=True
                             ).then_inc(loaded[0], 16)
                sp.dma_start(scale[:, :], ins["L2_ffn_ln_g"].rearrange("e c -> c e"), allow_slow_non_contiguous=True
                             ).then_inc(loaded[0], 16)
                sp.dma_start(bias[0][:, :], ins["L2_ffn_b1"].rearrange("e (k p) -> (e k) p", p=P)).then_inc(loaded[1], 16)
                sp.dma_start(bias[1][:, :], ins["L2_ffn_b2"]).then_inc(loaded[1], 16)
                sp.dma_start(router[:, :], ins["L2_ffn_Wr"]).then_inc(loaded[1], 16)
                sp.dma_start(rbias[:, :], row_to_all(ins["L2_ffn_br"])).then_inc(loaded[1], 16)
                sp.dma_start(w_down[:, :, :, :].rearrange("p e k c -> p (e k) c"),
                             ins["L2_ffn_W2"].rearrange("e (k p) c -> p (e k) c", p=P)).then_inc(loaded[2], 16)
                sp.wait_ge(parts_ready, 2)
                for i in range(3):
                    sp.dma_start(up_bias[i:i + 1, :, :].rearrange("a e h -> a (e h)"), parts[0][i][:, :]
                                 ).then_inc(placed, 16)
                    sp.dma_start(down_bias[i:i + 1, :, :].rearrange("a e c -> a (e c)"), parts[1][i][:, :]
                                 ).then_inc(placed, 16)
                sp.wait_ge(placed, 6 * 16)
                sp.wait_ge(loaded[1], 64)
                sp.wait_ge(loaded[2], 16)

            @block.tensor
            def _(pe):
                pe.wait_ge(loaded[0], 48)
                for e in range(E):
                    for k in range(HC):
                        j = e * HC + k
                        done = pe.matmul(extra[:, j:j + 1], raw_up[:, e, P * k:P * k + P], shift[:, e:e + 1],
                                         start=True, stop=True)
                done.then_inc(extra_ready, 1)
                pe.wait_ge(extra_taken, 1)
                pe.transpose(extraT[:, :], extra_sb[:, :], ident[:, :]).then_inc(extra_turned, 1)

            @block.scalar
            def _(act):
                for e in range(E):
                    act.wait_ge(scaled, e + 1)
                    act.activation(w_up[0][:, e, :], raw_up[:, e, :], ACT.Copy).then_inc(highs, 1)

            @block.vector
            def _(dve):
                steps = Steps(dve, splits)
                dve.wait_ge(extra_ready, 1)
                dve.tensor_copy(extra_sb[:, :], extra[:, :]).then_inc(extra_taken, 1)
                for e in range(E):
                    dve.tensor_scalar(raw_up[:, e, :], raw_up[:, e, :], scale[:, e:e + 1], None, ALU.mult
                                      ).then_inc(scaled, 1)
                dve.wait_ge(loaded[1], 64)
                dve.wait_ge(extra_turned, 1)
                steps.then(dve.tensor_tensor(bias[0][:, :], bias[0][:, :], extraT[:, :], ALU.add))
                for i in range(3):
                    for m in range(2):
                        done = dve.tensor_copy(parts[m][i][:, :], bias[m][:, :])
                        if i < 2:
                            steps.did(done)
                        else:
                            done.then_inc(parts_ready, 1)
                    if i < 2:
                        steps.settle()
                        for m in range(2):
                            steps.did(dve.tensor_tensor(bias[m][:, :], bias[m][:, :], parts[m][i][:, :], ALU.subtract))
                        steps.settle()
                for e in range(E):
                    dve.wait_ge(highs, e + 1)
                    dve.tensor_tensor(w_up[1][:, e, :], raw_up[:, e, :], w_up[0][:, e, :].bitcast(F32), ALU.subtract)

        normed = Tools(nc, ctx).sbuf("g_normed", [P, TT, C])
        with ExitStack() as routing:
            masks = [Tools(nc, routing).sbuf(f"g_mask{i}", [P, TT, E]) for i in range(2)]
            route(nc, kind, router, rbias, ident, tokens, normed, masks, gates, places, owner, "gr_")
        run_experts(nc, kind, w_up, None, w_down, up_bias, down_bias, ident, tokens, normed, gates, places,
                    owner, sorted_rows, sorted_results, "gx_")



WINDOW = 32
SHIFT = WINDOW // 2
HEADS3 = 4
HD = C // HEADS3
CW = HALF // WINDOW
MASKED = -1.0e30


def window_attention(nc, ins, ident, tokens):
    with ExitStack() as ctx:
        t = Tools(nc, ctx)
        rows = t.sbuf("w_rows", [P, 4, C])
        wT = t.sbuf("w_wT", [P, 4, C])
        qbias = t.sbuf("w_qbias", [P, 3])
        obias = t.sbuf("w_obias", [P, C])
        toeplitz = t.sbuf("w_toeplitz", [P, WINDOW])
        bias = t.sbuf("w_bias", [P, WINDOW])
        last_bias = t.sbuf("w_last_bias", [P, CW, WINDOW])
        bn = t.sbuf("w_bn", [P, NT, 6])
        mv = t.sbuf("w_mv", [P, NT, 2])
        var = t.sbuf("w_var", [P, NT])
        std = t.sbuf("w_std", [P, NT])
        rstd = t.sbuf("w_rstd", [P, NT])
        u = t.sbuf("w_u", [P, NT, C])
        uT = [t.sbuf(f"w_uT{i}", [P, N + SHIFT]) for i in range(2)]
        qs = [t.sbuf(f"w_qs{i}", [P, CW, HEADS3, WINDOW]) for i in range(2)]
        kT = [t.sbuf(f"w_kT{i}", [P, HALF]) for i in range(2)]
        vs = [t.sbuf(f"w_vs{i}", [P, CW, HEADS3, HD]) for i in range(4)]
        logit = [t.sbuf(f"w_logit{i}", [P, CW, WINDOW]) for i in range(2)]
        top = [t.sbuf(f"w_top{i}", [P, CW]) for i in range(2)]
        prob = [t.sbuf(f"w_prob{i}", [P, CW, WINDOW]) for i in range(2)]
        total = [t.sbuf(f"w_total{i}", [P, CW]) for i in range(2)]
        pT = [t.sbuf(f"w_pT{i}", [P, HALF]) for i in range(2)]
        oT = [t.sbuf(f"w_oT{i}", [P, SHIFT + N]) for i in range(2)]
        turn = [t.psum(f"w_turn{i}", [P, HALF]) for i in range(2)]
        proj = [t.psum(f"w_proj{i}", [P, HALF]) for i in range(3)]
        score = t.psum("w_score", [P, HALF])
        mixed = t.psum("w_mixed", [P, HALF])
        result = t.psum("w_result", [P, HALF])

        loaded = t.sem("w_loaded")
        turned = t.sem("w_turned")
        weights_ready = t.sem("w_weights_ready")
        pool_steps = t.sem("w_pool_steps")
        masks_ready = t.sem("w_masks_ready")
        setup = t.sem("w_setup")
        table_ready = t.sem("w_table_ready")
        front_steps = t.sem("w_front_steps")
        var_ready = t.sem("w_var_ready")
        std_ready = t.sem("w_std_ready")
        u_ready = t.sem("w_u_ready")
        turn_ready = t.sem("w_turn_ready")
        uT_ready = t.sem("w_uT_ready")
        prepared = t.sem("w_prepared")
        result_ready = t.sem("w_result_ready")
        result_taken = t.sem("w_result_taken")
        proj_ready = t.sem("w_proj_ready")
        q_taken = t.sem("w_q_taken")
        k_taken = t.sem("w_k_taken")
        v_taken = t.sem("w_v_taken")
        score_ready = t.sem("w_score_ready")
        score_taken = t.sem("w_score_taken")
        pre_steps = t.sem("w_pre_steps")
        shifted = t.sem("w_shifted")
        exp_done = t.sem("w_exp_done")
        post_steps = t.sem("w_post_steps")
        pT_ready = t.sem("w_pT_ready")
        mixed_ready = t.sem("w_mixed_ready")
        mixed_taken = t.sem("w_mixed_taken")
        block = ctx.enter_context(nc.Block())
        loads = 8 + HEADS3

        def batches(engine, step, turn_first):
            turn_first()
            for b in range(2):
                for h in range(2):
                    step(b, h, b)
            with engine.Fori(2, B - 3, 2) as b:
                for par in range(2):
                    for h in range(2):
                        step(b + par, h, par)
            for b in (B - 2, B - 1):
                for h in range(2):
                    step(b, h, b % 2)

        def known(x, least):
            return not isinstance(x, int) or x >= least

        @block.sync
        def _(sp):
            for i in range(3):
                sp.dma_start(rows[:, i, :], ins["L3_attn_w_qkv"][P * i:P * i + P, :]).then_inc(loaded, 16)
                sp.dma_start(qbias[:, i:i + 1], ins["L3_attn_b_qkv"][P * i:P * i + P].rearrange("(c a) -> c a", a=1)
                             ).then_inc(loaded, 16)
            sp.dma_start(rows[:, 3, :], ins["L3_attn_w_out"]).then_inc(loaded, 16)
            sp.dma_start(obias[:, :], row_to_all(ins["L3_attn_b_out"])).then_inc(loaded, 16)
            rel = ins["L3_attn_rel_pos"]
            for h in range(HEADS3):
                windows = bass.AP(tensor=rel.tensor, offset=h * (2 * WINDOW - 1), ap=[[1, WINDOW], [1, WINDOW]])
                sp.dma_start(toeplitz[WINDOW * h:WINDOW * h + WINDOW, :], windows).then_inc(loaded, 16)

        @block.gpsimd
        def _(pool):
            steps = Steps(pool, pool_steps)
            for x in (*qs, *vs):
                steps.did(pool.memset(x[:, :, :, :], 0.0))
            pool.wait_ge(table_ready, 1)
            steps.then(pool.tensor_copy(last_bias[:, :, :], bias[:, :].unsqueeze(1).to_broadcast([P, CW, WINDOW])))
            for h in range(HEADS3):
                part = slice(WINDOW * h, WINDOW * h + WINDOW)
                steps.did(pool.affine_select(out=last_bias[part, CW - 1, SHIFT:], in_=last_bias[part, CW - 1, SHIFT:],
                                             compare_op=ALU.is_ge, fill=MASKED, base=-SHIFT,
                                             pattern=[[0, WINDOW - SHIFT]], channel_multiplier=1))
                steps.did(pool.affine_select(out=last_bias[part, CW - 1, 0:SHIFT], in_=last_bias[part, CW - 1, 0:SHIFT],
                                             compare_op=ALU.is_ge, fill=MASKED, base=SHIFT - 1,
                                             pattern=[[0, SHIFT]], channel_multiplier=-1))
            steps.settle()
            pool.memset(std[:, :], 1.0).then_inc(masks_ready, 1)

            def prepare(b):
                pool.wait_ge(u_ready, b + 1)
                batch = tokens[:, bass.ds(b * NT, NT), :]
                pool.tensor_tensor(batch, batch, obias[:, :].unsqueeze(1).to_broadcast([P, NT, C]), ALU.add
                                   ).then_inc(prepared, 1)
            pool.wait_ge(loaded, 16 * loads)
            with pool.Fori(0, B) as b:
                prepare(b)

        @block.tensor
        def _(pe):
            pe.wait_ge(loaded, 16 * loads)
            for i in range(4):
                done = pe.transpose(turn[0][:, P * i:P * i + P], rows[:, i, :], ident[:, :])
            done.then_inc(turned, 1)
            pe.wait_ge(weights_ready, 1)
            pe.wait_ge(pool_steps, 6)

            def turn_batch(b):
                pe.wait_ge(u_ready, b + 1)
                if known(b, 1):
                    pe.wait_ge(uT_ready, b)
                for j in range(NT):
                    done = pe.transpose(turn[j // 4][:, P * (j % 4):P * (j % 4) + P], u[:, j, :], ident[:, :])
                done.then_inc(turn_ready, 1)

            def project(b, h, par):
                pe.wait_ge(uT_ready, b + 1)
                for i, taken in enumerate((q_taken, k_taken, v_taken)):
                    if known(b, 1) or h == 1:
                        pe.wait_ge(taken, b * 2 + h)
                    at = SHIFT + HALF * h
                    pe.matmul(proj[i][:, :], wT[:, i, :], uT[par][:, at:at + HALF], start=True, stop=True
                              ).then_inc(proj_ready, 1)

            def scores(b, h):
                pe.wait_ge(q_taken, b * 2 + h + 1)
                pe.wait_ge(k_taken, b * 2 + h + 1)
                if known(b, 1) or h == 1:
                    pe.wait_ge(score_taken, b * 2 + h)
                for w in range(CW):
                    done = pe.matmul(score[:, WINDOW * w:WINDOW * w + WINDOW],
                                     qs[h][:, w, :, :].rearrange("p h q -> p (h q)"),
                                     kT[h][:, WINDOW * w:WINDOW * w + WINDOW], start=True, stop=True)
                done.then_inc(score_ready, 1)

            def mix(b, h, par):
                pe.wait_ge(v_taken, b * 2 + h + 1)
                pe.wait_ge(pT_ready, b * 2 + h + 1)
                if known(b, 1) or h == 1:
                    pe.wait_ge(mixed_taken, b * 2 + h)
                for w in range(CW):
                    done = pe.matmul(mixed[:, WINDOW * w:WINDOW * w + WINDOW],
                                     vs[2 * par + h][:, w, :, :].rearrange("p h d -> p (h d)"),
                                     pT[h][:, WINDOW * w:WINDOW * w + WINDOW], start=True, stop=True)
                done.then_inc(mixed_ready, 1)

            def give(b, par):
                pe.wait_ge(mixed_taken, b * 2 + 2)
                for half in range(2):
                    if known(b, 1) or half == 1:
                        pe.wait_ge(result_taken, b * 2 + half)
                    for j in range(4):
                        at = P * (4 * half + j)
                        done = pe.matmul(result[:, P * j:P * j + P], oT[par][:, at:at + P], wT[:, 3, :],
                                         start=True, stop=True)
                    done.then_inc(result_ready, 1)

            def step(b, h, par):
                project(b, h, par)
                if h == 0 and known(b, 2):
                    give(b - 2, par)
                if h == 1:
                    scores(b, 0)
                elif known(b, 1):
                    scores(b - 1, 1)
                if known(b, 1):
                    mix(b - 1, h, 1 - par)
                if h == 0 and not (isinstance(b, int) and b == B - 1):
                    turn_batch(b + 1)

            batches(pe, step, lambda: turn_batch(0))
            give(B - 2, 0)
            scores(B - 1, 1)
            mix(B - 1, 0, 1)
            mix(B - 1, 1, 1)
            give(B - 1, 1)

        @block.scalar
        def _(act):
            act.wait_ge(masks_ready, 1)

            def take_turned(b, par):
                act.wait_ge(turn_ready, b + 1)
                for h in range(2):
                    act.activation(uT[par][:, HALF * h:HALF * h + HALF], turn[h][:, :], ACT.Copy)
                act.activation(uT[par][:, N:N + SHIFT], turn[0][:, 0:SHIFT], ACT.Copy).then_inc(uT_ready, 1)

            def root(b):
                act.wait_ge(var_ready, b + 1)
                act.activation(std[:, :], var[:, :], ACT.Sqrt).then_inc(std_ready, 1)

            def take_q(b, h):
                act.wait_ge(proj_ready, (b * 2 + h) * 3 + 1)
                if known(b, 1):
                    act.wait_ge(score_ready, b * 2 + h - 1)
                for i in range(HEADS3):
                    part = slice(HD * i, HD * i + HD)
                    done = act.activation(qs[h][part, :, i, :], proj[0][part, :].rearrange("p (w q) -> p w q", w=CW),
                                          ACT.Identity, bias=qbias[part, 0:1], scale=HD ** -0.5)
                done.then_inc(q_taken, 1)

            def exponent(b, h):
                act.wait_ge(shifted, b * 2 + h + 1)
                act.activation(prob[h][:, :, :], logit[h][:, :, :], ACT.Exp).then_inc(exp_done, 1)

            def take_mixed(b, h, par):
                act.wait_ge(mixed_ready, b * 2 + h + 1)
                if known(b, 2):
                    act.wait_ge(result_ready, b * 2 - 2)
                at = SHIFT + HALF * h
                done = act.activation(oT[par][:, at:at + HALF], mixed[:, :], ACT.Identity, bias=qbias[:, 2:3])
                if h == 1:
                    done = act.activation(oT[par][:, 0:SHIFT], mixed[:, HALF - SHIFT:], ACT.Identity, bias=qbias[:, 2:3])
                done.then_inc(mixed_taken, 1)

            def step(b, h, par):
                take_q(b, h)
                if h == 1:
                    exponent(b, 0)
                elif known(b, 1):
                    exponent(b - 1, 1)
                if known(b, 1):
                    take_mixed(b - 1, h, 1 - par)
                if h == 0 and not (isinstance(b, int) and b == B - 1):
                    root(b + 1)
                    take_turned(b + 1, 1 - par)

            def start():
                act.wait_ge(table_ready, 1)
                root(0)
                take_turned(0, 0)

            batches(act, step, start)
            exponent(B - 1, 1)
            take_mixed(B - 1, 0, 1)
            take_mixed(B - 1, 1, 1)

        @block.vector
        def _(dve):
            steps = Steps(dve, setup)
            dve.wait_ge(turned, 1)
            dve.tensor_copy(wT[:, :, :].rearrange("p i c -> p (i c)"), turn[0][:, :]).then_inc(weights_ready, 1)
            dve.wait_ge(loaded, 16 * loads)
            steps.did(dve.tensor_scalar(qbias[:, 0:1], qbias[:, 0:1], HD ** -0.5, None, ALU.mult))
            for q in range(WINDOW):
                done = dve.tensor_copy(bias[:, q:q + 1], toeplitz[:, WINDOW - 1 - q:WINDOW - q])
            steps.did(done)
            steps.settle()
            dve.memset(var[:, :], 1.0).then_inc(table_ready, 1)
            dve.wait_ge(table_ready, 1)

            front = Steps(dve, front_steps)
            pre = Steps(dve, pre_steps)
            post = Steps(dve, post_steps)

            def normalise(b):
                front.round(b)
                for j in range(NT):
                    front.did(dve.bn_stats(bn[:, j, :], tokens[:, bass.ds(b * NT + j, 1), :].rearrange("p a c -> p (a c)")))
                if known(b, 1):
                    dve.wait_ge(turn_ready, b)
                front.settle()
                front.did(dve.tensor_copy(rstd[:, 0:1], bn[:, 0, 0:1]))
                for j in range(NT):
                    front.did(dve.bn_aggr(mv[:, j, :], bn[:, j, :]))
                front.settle()
                dve.tensor_scalar(var[:, :], mv[:, :, 1], TOKEN_EPS, None, ALU.add).then_inc(var_ready, 1)
                dve.wait_ge(std_ready, b + 1)
                front.then(dve.reciprocal(rstd[:, :], std[:, :]))
                for j in range(NT):
                    done = dve.tensor_scalar(u[:, j, :], tokens[:, bass.ds(b * NT + j, 1), :].rearrange("p a c -> p (a c)"),
                                             mv[:, j, 0:1], rstd[:, j:j + 1], ALU.subtract, ALU.mult)
                done.then_inc(u_ready, 1)

            def take_kv(b, h, par):
                dve.wait_ge(proj_ready, (b * 2 + h) * 3 + 2)
                if known(b, 1):
                    dve.wait_ge(score_ready, b * 2 + h - 1)
                dve.tensor_scalar(kT[h][:, :], proj[1][:, :], qbias[:, 1:2], None, ALU.add).then_inc(k_taken, 1)
                dve.wait_ge(proj_ready, (b * 2 + h) * 3 + 3)
                if known(b, 2):
                    dve.wait_ge(mixed_ready, b * 2 + h - 3)
                for i in range(HEADS3):
                    part = slice(HD * i, HD * i + HD)
                    done = dve.transpose(vs[2 * par + h][part, :, i, :], proj[2][part, :].rearrange("p (w q) -> p w q", w=CW))
                done.then_inc(v_taken, 1)

            def before_exp(b, h):
                pre.round(b * 2 + h)
                dve.wait_ge(score_ready, b * 2 + h + 1)
                table = last_bias[:, :, :] if h == 1 else bias[:, :].unsqueeze(1).to_broadcast([P, CW, WINDOW])
                dve.tensor_tensor(logit[h][:, :, :], score[:, :].rearrange("p (w q) -> p w q", w=CW), table, ALU.add
                                  ).then_inc(score_taken, 1)
                dve.wait_ge(score_taken, b * 2 + h + 1)
                pre.then(dve.tensor_reduce(top[h][:, :], logit[h][:, :, :], AX.X, ALU.max))
                dve.tensor_tensor(logit[h][:, :, :], logit[h][:, :, :],
                                  top[h][:, :].unsqueeze(2).to_broadcast([P, CW, WINDOW]), ALU.subtract
                                  ).then_inc(shifted, 1)

            def after_exp(b, h):
                post.round(b * 2 + h)
                dve.wait_ge(exp_done, b * 2 + h + 1)
                post.then(dve.tensor_reduce(total[h][:, :], prob[h][:, :, :], AX.X, ALU.add))
                post.then(dve.reciprocal(total[h][:, :], total[h][:, :]))
                post.then(dve.tensor_tensor(prob[h][:, :, :], prob[h][:, :, :],
                                            total[h][:, :].unsqueeze(2).to_broadcast([P, CW, WINDOW]), ALU.mult))
                if known(b, 1):
                    dve.wait_ge(mixed_ready, b * 2 + h - 1)
                dve.transpose(pT[h][:, :], prob[h][:, :, :].rearrange("p w q -> p (w q)")).then_inc(pT_ready, 1)

            def add(b):
                dve.wait_ge(prepared, b + 1)
                for half in range(2):
                    dve.wait_ge(result_ready, b * 2 + half + 1)
                    rows4 = tokens[:, bass.ds(b * NT + 4 * half, 4), :]
                    dve.tensor_tensor(rows4, rows4, result[:, :].rearrange("p (a c) -> p a c", a=4), ALU.add
                                      ).then_inc(result_taken, 1)

            def step(b, h, par):
                if known(b, 1):
                    after_exp(b - 1, h)
                take_kv(b, h, par)
                if h == 0 and known(b, 2):
                    add(b - 2)
                if h == 1:
                    before_exp(b, 0)
                elif known(b, 1):
                    before_exp(b - 1, 1)
                if h == 0 and not (isinstance(b, int) and b == B - 1):
                    normalise(b + 1)

            dve.wait_ge(masks_ready, 1)
            batches(dve, step, lambda: normalise(0))
            add(B - 2)
            after_exp(B - 1, 0)
            before_exp(B - 1, 1)
            after_exp(B - 1, 1)
            add(B - 1)


def experts_silu(nc, ins, ident, tokens, sorted_rows, sorted_results):
    kind = Expert("silu", 341)
    W = kind.width
    chunks = kind.chunks
    with ExitStack() as ctx:
        t = Tools(nc, ctx)
        gates = t.sbuf("s_gates", [P, TT, 2])
        places = t.sbuf("s_places", [P, TT, 2], I32)
        owner = t.sbuf("s_owner", [1, SLOT_TILES // 8], I32)
        w_up, w_gate = ([t.sbuf(f"s_w_{name}_{part}", [P, E, kind.even], F32R) for part in ("high", "low")]
                        for name in ("up", "gate"))
        w_down = t.sbuf("s_w_down", [P, E, len(chunks), C])
        router = t.sbuf("s_router", [P, E])
        with ExitStack() as setup:
            t = Tools(nc, setup)
            at_last, rest = chunks[-1]
            K = len(chunks) - 1
            raw = [t.sbuf(f"s_raw{i}", [P, E, K + 1, C]) for i in range(2)]
            raw_down = t.sbuf("s_raw_down", [P, E, W])
            raw_router = t.sbuf("s_raw_router", [E, C])
            turn = [t.psum(f"s_turn{i}", [P, HALF]) for i in range(4)]
            loaded = [t.sem(f"s_loaded{i}") for i in range(3)]
            cleared = t.sem("s_cleared")
            turned = t.sem("s_turned")
            highs = t.sem("s_highs")
            taken = t.sem("s_taken")
            block = setup.enter_context(nc.Block())
            jobs = [(m, e) for m in range(3) for e in range(E)]

            @block.gpsimd
            def _(pool):
                for m in range(2):
                    pool.memset(raw[m][rest // 32 * 32:rest // 32 * 32 + 32, :, K, :], 0.0).then_inc(cleared, 1)

            @block.sync
            def _(sp):
                sp.wait_ge(cleared, 2)
                for m, name in enumerate(("L3_ffn_w1", "L3_ffn_w3")):
                    sp.dma_start(raw[m][0:rest, :, K, :], ins[name][:, at_last:, :].rearrange("e p c -> p e c")
                                 ).then_inc(loaded[m], 16)
                    for k in range(K):
                        sp.dma_start(raw[m][:, :, k, :], ins[name][:, P * k:P * k + P, :].rearrange("e p c -> p e c")
                                     ).then_inc(loaded[m], 16)
                sp.dma_start(raw_down[:, :, :], ins["L3_ffn_w2"].rearrange("e c h -> c e h")).then_inc(loaded[2], 16)
                sp.dma_start(raw_router[:, :], ins["L3_ffn_router_w"]).then_inc(loaded[2], 16)
                sp.wait_ge(loaded[2], 32)

            @block.tensor
            def _(pe):
                for n, (m, e) in enumerate(jobs):
                    if e == 0:
                        pe.wait_ge(loaded[m], 32 if m == 2 else 16 * (K + 1))
                    if n >= 4:
                        pe.wait_ge(*((taken, n - 3) if jobs[n - 4][0] < 2 else (highs, n - 3)))
                    bank = turn[n % 4]
                    for k in range(K):
                        part = raw_down[:, e, P * k:P * k + P] if m == 2 else raw[m][:, e, k, :]
                        pe.transpose(bank[:, P * k:P * k + P], part, ident[:, :])
                    if m == 2:
                        done = pe.transpose(bank[0:rest, P * K:P * K + P], raw_down[:, e, at_last:], ident[:, :])
                    else:
                        width = kind.even - at_last
                        done = pe.transpose(bank[:, at_last:kind.even], raw[m][0:width, e, K, :],
                                            ident[0:width, 0:width])
                    done.then_inc(turned, 1)
                pe.wait_ge(highs, len(jobs) - 3)
                pe.transpose(turn[len(jobs) % 4][:, 0:E], raw_router[:, :], ident[0:E, 0:E]).then_inc(turned, 1)

            def pieces(n, m, e):
                bank = turn[n % 4]
                if m < 2:
                    return [(bank[:, 0:kind.even], [part[:, e, :] for part in (w_up, w_gate)[m]])]
                return [(bank[:, 0:P * K].rearrange("p (k c) -> p k c", c=C), [w_down[:, e, 0:K, :]]),
                        (bank[0:rest, P * K:P * K + P], [w_down[0:rest, e, K, :]])]

            @block.scalar
            def _(act):
                for n, (m, e) in enumerate(jobs):
                    act.wait_ge(turned, n + 1)
                    for given, into in pieces(n, m, e):
                        done = act.activation(into[0], given, ACT.Copy)
                    done.then_inc(highs, 1)

            @block.vector
            def _(dve):
                for n, (m, e) in enumerate(jobs):
                    if m < 2:
                        dve.wait_ge(highs, n + 1)
                        for given, (high, low) in pieces(n, m, e):
                            dve.tensor_tensor(low, given, high.bitcast(F32), ALU.subtract).then_inc(taken, 1)
                dve.wait_ge(turned, len(jobs) + 1)
                dve.tensor_copy(router[:, :], turn[len(jobs) % 4][:, 0:E])

        normed = Tools(nc, ctx).sbuf("s_normed", [P, TT, C])
        with ExitStack() as routing:
            masks = [Tools(nc, routing).sbuf(f"s_mask{i}", [P, TT, E]) for i in range(2)]
            route(nc, kind, router, None, ident, tokens, normed, masks, gates, places, owner, "sr_")
        run_experts(nc, kind, w_up, w_gate, w_down, None, None, ident, tokens, normed, gates, places,
                    owner, sorted_rows, sorted_results, "sx_")


INPUTS = ['x', 'L0_conv_Wq', 'L0_conv_bq', 'L0_conv_Wk', 'L0_conv_bk', 'L0_conv_Wv', 'L0_conv_bv',
          'L0_conv_gamma', 'L1_conv_weight', 'L1_conv_bias', 'L2_attn_kln_weight', 'L2_attn_kln_bias',
          'L2_attn_vln_weight', 'L2_attn_vln_bias', 'L2_ffn_Wr', 'L2_ffn_br', 'L2_ffn_ln_g', 'L2_ffn_ln_b',
          'L2_ffn_W1', 'L2_ffn_b1', 'L2_ffn_W2', 'L2_ffn_b2', 'L3_attn_w_qkv', 'L3_attn_b_qkv',
          'L3_attn_rel_pos', 'L3_attn_w_out', 'L3_attn_b_out', 'L3_ffn_router_w', 'L3_ffn_w1', 'L3_ffn_w2',
          'L3_ffn_w3']


def build(nc, ins, out, sorted_rows, sorted_results):
    with ExitStack() as ctx:
        t = Tools(nc, ctx)
        ident = t.sbuf("ident", [P, P])
        tokens = t.sbuf("tokens", [P, TT, C])
        made = t.sem("made")
        with nc.Block() as block:
            @block.gpsimd
            def _(pool):
                make_identity(pool, Steps(pool, made), ident[:, :])
        with ExitStack() as early:
            t = Tools(nc, early)
            feats = t.sbuf("feats", [P, B, N])
            stats = t.sbuf("stats", [P, 2 * B, 6])
            conv_attention(nc, ins, ident, feats, stats, sorted_rows)
            whiten(nc, ins, ident, feats, stats, tokens)
        linear_attention(nc, ins, ident, tokens)
        experts_gelu(nc, ins, ident, tokens, sorted_rows, sorted_results)
        window_attention(nc, ins, ident, tokens)
        experts_silu(nc, ins, ident, tokens, sorted_rows, sorted_results)
        store_images(nc, ident, tokens, out)


def kernel(**inputs):
    import numpy as np
    import concourse.bacc as bacc
    from concourse.bass_utils import run_bass_kernel_spmd

    nc = bacc.Bacc("TRN2", target_bir_lowering=False, num_devices=1)
    arrays, ins = {}, {}
    for name in INPUTS:
        a = np.ascontiguousarray(inputs[name])
        arrays[f"in_{name}"] = a
        ins[name] = nc.dram_tensor(f"in_{name}", a.shape, mybir.dt.from_np(a.dtype), kind="ExternalInput").ap()
    out = nc.dram_tensor("out", (B, C, 32, 32), F32, kind="ExternalOutput").ap()
    sorted_rows, sorted_results = ([nc.dram_tensor(f"sorted_{what}{g}", (SLOTS, C), F32, kind="Internal").ap()
                                    for g in range(GROUPS)] for what in ("rows", "results"))
    build(nc, ins, out, sorted_rows, sorted_results)
    r = run_bass_kernel_spmd(nc, [arrays], core_ids=[0])
    return r.results[0]["out"]
```

```python
from contextlib import ExitStack

import concourse.bass as bass
from concourse import mybir

ALU = mybir.AluOpType
ACT = mybir.ActivationFunctionType
AX = mybir.AxisListType
F32 = mybir.dt.float32
F32R = mybir.dt.float32r
BF16 = mybir.dt.bfloat16
I32 = mybir.dt.int32

P = 128
B, C, N = 8, 128, 1024
NT = N // P
TT = B * NT
LAG = 4
CQ = C // 2
HALF = 512


class Tools:

    def __init__(self, nc, ctx):
        self.nc, self.ctx = nc, ctx

    def sbuf(self, name, shape, dtype=F32):
        return self.ctx.enter_context(self.nc.sbuf_tensor(name, shape, dtype))

    def psum(self, name, shape, dtype=F32):
        return self.ctx.enter_context(self.nc.psum_tensor(name, shape, dtype))

    def sem(self, name):
        return self.ctx.enter_context(self.nc.semaphore(name))


class ClearedTools(Tools):

    def __init__(self, nc, ctx):
        super().__init__(nc, ctx)
        self.sems = []
        ctx.callback(self.clear)

    def clear(self):
        self.nc.clear_and_free_semaphores(self.sems)
        self.nc.all_engine_barrier()

    def sem(self, name):
        self.sems.append(self.nc.alloc_semaphore(name))
        return self.sems[-1]


class Steps:

    def __init__(self, engine, sem):
        self.engine, self.sem, self.n, self.base, self.per = engine, sem, 0, 0, None

    def round(self, i):
        if self.per is None and self.n:
            self.per = self.n
        if self.per is not None:
            assert self.n == self.per
            self.base = i * self.per
        self.n = 0

    def did(self, instruction):
        instruction.then_inc(self.sem, 1)
        self.n += 1

    def settle(self):
        self.engine.wait_ge(self.sem, self.base + self.n)

    def then(self, instruction):
        self.did(instruction)
        self.settle()


def row_to_all(ap, parts=P):
    return ap.partition_broadcast(parts)


def make_identity(pool, steps, tile):
    steps.then(pool.memset(tile, 0.0))
    steps.then(pool.affine_select(out=tile, in_=tile, compare_op=ALU.not_equal, fill=1.0, base=0,
                                  pattern=[[-1, P]], channel_multiplier=1))



def conv_attention(nc, ins, ident, feats, stats, sorted_rows):
    x = ins["x"].rearrange("b c h w -> b c (h w)")
    with ExitStack() as ctx:
        t = ClearedTools(nc, ctx)
        xin = [t.sbuf(f"xin{i}", [P, N]) for i in range(2)]
        wrow = [t.sbuf(f"wrow{i}", [P, C]) for i in range(3)]
        wT = [t.sbuf(f"wT{i}", [P, P]) for i in range(3)]
        bq = t.sbuf("bq", [P, 1])
        bk = t.sbuf("bk", [P, 1])
        bv = t.sbuf("bv", [P, C])
        gamma = t.sbuf("gamma", [P, 1])
        q_high = [t.sbuf(f"q_high{i}", [P, N], F32R) for i in range(2)]
        q_low = [t.sbuf(f"q_low{i}", [P, N], F32R) for i in range(2)]
        k = [t.sbuf(f"k{i}", [P, N], F32R) for i in range(2)]
        v = [t.sbuf(f"v{i}", [P, NT, C]) for i in range(2)]
        probs = [t.sbuf(f"probs{i}", [P, N]) for i in range(4)]
        probs_high = [t.sbuf(f"probs_high{i}", [P, N], F32R) for i in range(4)]
        probs_low = [t.sbuf(f"probs_low{i}", [P, N], F32R) for i in range(4)]
        vs_high = [t.sbuf(f"vs_high{i}", [P, C], F32R) for i in range(4)]
        vs_low = [t.sbuf(f"vs_low{i}", [P, C], F32R) for i in range(4)]
        nmax = [t.sbuf(f"nmax{i}", [P, 1]) for i in range(4)]
        zsum = [t.sbuf(f"zsum{i}", [P, 1]) for i in range(4)]
        rz = [t.sbuf(f"rz{i}", [P, 1]) for i in range(4)]
        score = [t.psum(f"score{i}", [P, N]) for i in range(2)]
        out = t.psum("attended", [P, N])
        proj = [t.psum(f"proj{i}", [P, HALF]) for i in range(2)]

        weights_loaded = t.sem("weights_loaded")
        x_loaded = [t.sem(f"x_loaded{i}") for i in range(2)]
        weights_turned = t.sem("weights_turned")
        weights_ready = t.sem("weights_ready")
        proj_ready = t.sem("proj_ready")
        qk_high = t.sem("qk_high")
        qk_ready = t.sem("qk_ready")
        v_taken = t.sem("v_taken")
        score_ready = t.sem("score_ready")
        max_ready = t.sem("max_ready")
        exp_done = t.sem("exp_done")
        high_ready = t.sem("probs_high_ready")
        low_ready = t.sem("probs_low_ready")
        vs_high_ready = t.sem("vs_high_ready")
        vs_ready = t.sem("vs_ready")
        av_done = t.sem("av_done")
        feats_loaded = t.sem("feats_loaded")
        feats_ready = t.sem("feats_ready")
        rz_ready = t.sem("rz_ready")
        stats_ready = t.sem("stats_ready")
        zeros = t.sbuf("zeros", [P, 8 * C])
        zeroed = t.sem("zeroed")
        cleared = t.sem("cleared")
        block = ctx.enter_context(nc.Block())

        @block.sync
        def _(sp):
            for w, name in ((0, "L0_conv_Wq"), (1, "L0_conv_Wk")):
                for r in range(2):
                    sp.dma_start(wrow[w][CQ * r:CQ * r + CQ, :], ins[name]).then_inc(weights_loaded, 16)
            sp.dma_start(wrow[2][:, :], ins["L0_conv_Wv"]).then_inc(weights_loaded, 16)
            for tile, name in ((bq, "L0_conv_bq"), (bk, "L0_conv_bk")):
                for r in range(2):
                    sp.dma_start(tile[CQ * r:CQ * r + CQ, :],
                                 ins[name].rearrange("(c a) -> c a", a=1)).then_inc(weights_loaded, 16)
            sp.dma_start(bv[:, :], row_to_all(ins["L0_conv_bv"])).then_inc(weights_loaded, 16)
            sp.dma_start(gamma[:, :], row_to_all(ins["L0_conv_gamma"])).then_inc(weights_loaded, 16)
            for i in range(2):
                sp.dma_start(xin[i][:, :], x[i]).then_inc(x_loaded[i], 16)
            sp.dma_start(feats[:, :, :], x.rearrange("b c n -> c b n")).then_inc(feats_loaded, 16)
            for b in range(2, B):
                sp.wait_ge(proj_ready, 6 * (b - 1))
                sp.dma_start(xin[b % 2][:, :], x[b]).then_inc(x_loaded[b % 2], 16)

        @block.gpsimd
        def _(pool):
            pool.memset(zeros[:, :], 0.0).then_inc(zeroed, 1)
            pool.wait_ge(zeroed, 1)
            for rows in sorted_rows:
                for at in range(0, rows.shape[0], 8 * P):
                    pool.dma_start(rows[at:at + 8 * P, :].rearrange("(p k) c -> p (k c)", p=P),
                                   zeros[:, :]).then_inc(cleared, 16)
            with pool.Fori(0, B * NT - 3, 4) as tile:
                for i in range(4):
                    pool.wait_ge(high_ready, tile + (i + 1))
                    pool.tensor_tensor(probs_low[i][:, :], probs[i][:, :], probs_high[i][:, :].bitcast(F32), ALU.subtract
                                       ).then_inc(low_ready, 1)
            pool.wait_ge(cleared, 16 * SLOT_TILES // 8)

        @block.tensor
        def _(pe):
            pe.wait_ge(weights_loaded, 160 + 16)
            for i in range(3):
                turned = pe.transpose(proj[0][:, P * i:P * i + P], wrow[i][:, :], ident[:, :])
            turned.then_inc(weights_turned, 1)
            pe.wait_ge(weights_ready, 1)

            def project(b, par, item, first):
                if item == 0:
                    pe.wait_ge(x_loaded[par], (b - par) * 8 + 16)
                if item < 2:
                    if not first:
                        pe.wait_ge(v_taken, b * 2 - 1 + item)
                else:
                    pe.wait_ge(qk_ready, b * 4 + item - 1)
                bank = proj[item % 2]
                if item < 4:
                    w = wT[item // 2]
                    pe.matmul(bank[:, :], w[:, :], xin[par][:, HALF * (item % 2):HALF * (item % 2) + HALF],
                              start=True, stop=True).then_inc(proj_ready, 1)
                else:
                    for j in range(4):
                        at = P * (4 * (item - 4) + j)
                        done = pe.matmul(bank[:, P * j:P * j + P], xin[par][:, at:at + P], wT[2][:, :],
                                         start=True, stop=True)
                    done.then_inc(proj_ready, 1)

            def scores(b, par, n):
                if n == 0:
                    pe.wait_ge(qk_ready, b * 4 + 4)
                if not (isinstance(b, int) and b * NT + n < 2):
                    pe.wait_ge(exp_done, b * NT + n - 1)
                for h in range(2):
                    for part in (q_low, q_high):
                        done = pe.matmul(score[n % 2][:, HALF * h:HALF * h + HALF], k[par][:, P * n:P * n + P],
                                         part[par][:, HALF * h:HALF * h + HALF],
                                         start=(part is q_low), stop=(part is q_high))
                done.then_inc(score_ready, 1)

            def attend(b, n):
                pe.wait_ge(vs_ready, b * NT + n + 1)
                pe.wait_ge(low_ready, b * NT + n + 1)
                if n == 0 and not (isinstance(b, int) and b == 0):
                    pe.wait_ge(feats_ready, b)
                for i, (left, right) in enumerate(((vs_high, probs_high), (vs_low, probs_high), (vs_high, probs_low))):
                    for h in range(2):
                        done = pe.matmul(out[:, HALF * h:HALF * h + HALF], left[n % 4][:, :],
                                         right[n % 4][:, HALF * h:HALF * h + HALF],
                                         start=(n == 0 and i == 0), stop=(n == NT - 1 and i == 2))
                done.then_inc(av_done, 1)

            def batch(b, par, first=False, last=False):
                for n in range(NT):
                    scores(b, par, n)
                    if n >= LAG:
                        attend(b, n - LAG)
                    elif not first:
                        attend(b - 1, NT + n - LAG)
                    if n >= 2 and not last:
                        project(b + 1, 1 - par, n - 2, False)

            for item in range(6):
                project(0, 0, item, True)
            batch(0, 0, first=True)
            batch(1, 1)
            with pe.Fori(2, B - 3, 2) as b:
                batch(b, 0)
                batch(b + 1, 1)
            batch(B - 2, 0)
            batch(B - 1, 1, last=True)
            for n in range(NT - LAG, NT):
                attend(B - 1, n)

        @block.vector
        def _(dve):
            dve.wait_ge(weights_turned, 1)
            for i in range(3):
                done = dve.tensor_copy(wT[i][:, :], proj[0][:, P * i:P * i + P])
            done.then_inc(weights_ready, 1)

            def take_values(b, par, h):
                dve.wait_ge(proj_ready, b * 6 + 5 + h)
                dve.tensor_tensor(v[par][:, 4 * h:4 * h + 4, :],
                                  proj[h][:, :].rearrange("p (a c) -> p a c", a=4),
                                  bv[:, :].unsqueeze(1).to_broadcast([P, 4, C]), ALU.add).then_inc(v_taken, 1)

            def take_low(b, par, item):
                dve.wait_ge(qk_high, b * 4 + item + 1)
                at = slice(HALF * (item % 2), HALF * (item % 2) + HALF)
                if item < 2:
                    high, low, rows, bias = q_high, q_low, slice(0, P), bq
                else:
                    high, low, rows, bias = k, k, slice(CQ, P), bk
                dve.scalar_tensor_tensor(out=low[par][rows, at], in0=proj[item % 2][rows, :], scalar=bias[rows, 0:1],
                                         in1=high[par][rows, at].bitcast(F32), op0=ALU.add, op1=ALU.subtract
                                         ).then_inc(qk_ready, 1)

            def row_max(b, n):
                dve.wait_ge(score_ready, b * NT + n + 1)
                dve.tensor_reduce(nmax[n % 4][:, :], score[n % 2][:, :], AX.X, ALU.max,
                                  negate=True).then_inc(max_ready, 1)

            def scale_values(b, par, n):
                dve.wait_ge(exp_done, b * NT + n + 1)
                if n % 4 == 0:
                    dve.wait_ge(v_taken, b * 2 + 1 + n // 4)
                if not (isinstance(b, int) and b * NT + n < 4):
                    dve.wait_ge(av_done, b * NT + n - 3)
                dve.reciprocal(rz[n % 4][:, :], zsum[n % 4][:, :]).then_inc(rz_ready, 1)
                dve.wait_ge(rz_ready, b * NT + n + 1)
                dve.tensor_scalar(vs_high[n % 4][:, :], v[par][:, n, :], rz[n % 4][:, 0:1], None,
                                  ALU.mult).then_inc(vs_high_ready, 1)
                dve.wait_ge(vs_high_ready, b * NT + n + 1)
                dve.scalar_tensor_tensor(out=vs_low[n % 4][:, :], in0=v[par][:, n, :], scalar=rz[n % 4][:, 0:1],
                                         in1=vs_high[n % 4][:, :].bitcast(F32), op0=ALU.mult, op1=ALU.subtract
                                         ).then_inc(vs_ready, 1)

            def finish(b, par):
                dve.wait_ge(av_done, b * NT + NT)
                if isinstance(b, int) and b == 0:
                    dve.wait_ge(feats_loaded, 16)
                batch_feats = feats[:, bass.ds(b, 1), :].rearrange("p a n -> p (a n)")
                dve.scalar_tensor_tensor(out=batch_feats, in0=out[:, :], scalar=gamma[:, 0:1], in1=batch_feats,
                                         op0=ALU.mult, op1=ALU.add).then_inc(feats_ready, 1)
                dve.wait_ge(feats_ready, b + 1)
                for h in range(2):
                    dve.bn_stats(stats[:, bass.ds(b * 2 + h, 1), :].rearrange("p a s -> p (a s)"),
                                 feats[:, bass.ds(b, 1), HALF * h:HALF * h + HALF].rearrange("p a n -> p (a n)"),
                                 ).then_inc(stats_ready, 1)

            def batch(b, par, first=False, last=False):
                for n in range(NT):
                    row_max(b, n)
                    if n >= 1:
                        scale_values(b, par, n - 1)
                    elif not first:
                        scale_values(b - 1, 1 - par, NT - 1)
                    if n == LAG - 1 and not first:
                        finish(b - 1, 1 - par)
                    if n == 0 and not first:
                        take_values(b, par, 1)
                    if 3 <= n <= 6 and not last:
                        take_low(b + 1, 1 - par, n - 3)
                    if n == 7 and not last:
                        take_values(b + 1, 1 - par, 0)

            for item in range(4):
                take_low(0, 0, item)
            take_values(0, 0, 0)
            take_values(0, 0, 1)
            batch(0, 0, first=True)
            batch(1, 1)
            with dve.Fori(2, B - 3, 2) as b:
                batch(b, 0)
                batch(b + 1, 1)
            batch(B - 2, 0)
            batch(B - 1, 1, last=True)
            scale_values(B - 1, 1, NT - 1)
            finish(B - 1, 1)

        @block.scalar
        def _(act):
            act.wait_ge(weights_loaded, 176)

            def take_projection(b, par, item):
                into, bias = ((q_high, bq), (k, bk))[item // 2]
                at = slice(HALF * (item % 2), HALF * (item % 2) + HALF)
                act.wait_ge(proj_ready, b * 6 + item + 1)
                act.activation(into[par][:, at], proj[item % 2][:, :], ACT.Identity,
                               bias=bias[:, 0:1]).then_inc(qk_high, 1)

            def exponent(b, n):
                act.wait_ge(max_ready, b * NT + n + 1)
                if not (isinstance(b, int) and b * NT + n < 4):
                    act.wait_ge(av_done, b * NT + n - 3)
                act.activation(probs[n % 4][:, :], score[n % 2][:, :], ACT.Exp, bias=nmax[n % 4][:, 0:1],
                               accum_out=zsum[n % 4][:, 0:1]).then_inc(exp_done, 1)
                act.wait_ge(exp_done, b * NT + n + 1)
                act.activation(probs_high[n % 4][:, :], probs[n % 4][:, :], ACT.Copy).then_inc(high_ready, 1)

            def batch(b, par, first=False, last=False):
                for n in range(NT):
                    exponent(b, n)
                    if 2 <= n <= 5 and not last:
                        take_projection(b + 1, 1 - par, n - 2)

            for item in range(4):
                take_projection(0, 0, item)
            batch(0, 0, first=True)
            batch(1, 1)
            with act.Fori(2, B - 3, 2) as b:
                batch(b, 0)
                batch(b + 1, 1)
            batch(B - 2, 0)
            batch(B - 1, 1, last=True)



GROUP = 32
WHITEN_STEPS = 5
WHITEN_EPS = 1e-05


def whiten(nc, ins, ident, feats, stats, tokens):
    with ExitStack() as ctx:
        t = ClearedTools(nc, ctx)
        centred = [t.sbuf(f"centred{i}", [P, N]) for i in range(2)]
        turned = [t.sbuf(f"turned{i}", [P, NT, C]) for i in range(2)]
        mean = t.sbuf("mean", [P, 2])
        negmean = t.sbuf("negmean", [P, 1])
        blocks = t.sbuf("blocks", [P, P])
        sigma = t.sbuf("sigma", [P, P])
        scratch = t.sbuf("scratch", [P, P])
        diag = t.sbuf("diag", [P, 1])
        rtrace = t.sbuf("rtrace", [P, 1])
        root = t.sbuf("root", [P, 1])
        power = [t.sbuf(f"power{i}", [P, P]) for i in range(3)]
        weight = t.sbuf("weight", [P, C])
        bias = t.sbuf("bias", [P, C])
        mix = t.sbuf("mix", [P, P])
        turn = [[t.psum(f"turn{i}{h}", [P, HALF]) for h in range(2)] for i in range(2)]
        cov = t.psum("cov", [P, HALF])
        small = t.psum("small", [P, HALF])

        params_loaded = t.sem("params_loaded")
        blocks_ready = t.sem("blocks_ready")
        centred_ready = t.sem("centred_ready")
        turn_ready = t.sem("turn_ready")
        turned_low = t.sem("turned_low")
        turned_high = t.sem("turned_high")
        cov_done = t.sem("cov_done")
        dve_steps = t.sem("dve_steps")
        pool_steps = t.sem("pool_steps")
        operand_ready = t.sem("operand_ready")
        product_ready = t.sem("product_ready")
        root_ready = t.sem("root_ready")
        root_asked = t.sem("root_asked")
        recentred = t.sem("recentred")
        mixed = t.sem("mixed")
        mixed_taken = t.sem("mixed_taken")
        block = ctx.enter_context(nc.Block())
        small_products = 1 + 3 * (WHITEN_STEPS - 1)

        @block.sync
        def _(sp):
            sp.dma_start(weight[:, :], row_to_all(ins["L1_conv_weight"].rearrange("a c h w -> (a c h w)"))
                         ).then_inc(params_loaded, 16)
            sp.dma_start(bias[:, :], row_to_all(ins["L1_conv_bias"].rearrange("a c h w -> (a c h w)"))
                         ).then_inc(params_loaded, 16)

        @block.gpsimd
        def _(pool):
            steps = Steps(pool, pool_steps)
            steps.then(pool.memset(blocks[:, :], 1.0))
            grid = blocks[:, :].rearrange("p (g c) -> p g c", g=P // GROUP)
            steps.then(pool.affine_select(out=grid, in_=grid, compare_op=ALU.is_ge, fill=0.0, base=0,
                                          pattern=[[-GROUP, P // GROUP], [0, GROUP]], channel_multiplier=1))
            pool.affine_select(out=grid, in_=grid, compare_op=ALU.is_ge, fill=0.0, base=GROUP - 1,
                               pattern=[[GROUP, P // GROUP], [0, GROUP]],
                               channel_multiplier=-1).then_inc(blocks_ready, 1)

        @block.tensor
        def _(pe):
            def turn_batch(b, par, first):
                pe.wait_ge(centred_ready, b + 1)
                if not first:
                    pe.wait_ge(turned_low, b - 1)
                    pe.wait_ge(turned_high, b - 1)
                for h in range(2):
                    for j in range(4):
                        at = P * (4 * h + j)
                        done = pe.transpose(turn[par][h][:, P * j:P * j + P], centred[par][:, at:at + P],
                                            ident[:, :])
                    done.then_inc(turn_ready, 1)

            def covariance(b, par, start, stop):
                pe.wait_ge(turned_low, b + 1)
                pe.wait_ge(turned_high, b + 1)
                for j in range(NT):
                    done = pe.matmul(cov[:, 0:P], turned[par][:, j, :], turned[par][:, j, :],
                                     start=(start and j == 0), stop=(stop and j == NT - 1),
                                     skip_group_check=True)
                done.then_inc(cov_done, 1)

            turn_batch(0, 0, True)
            turn_batch(1, 1, True)
            covariance(0, 0, True, False)
            with pe.Fori(1, B - 2, 2) as b:
                turn_batch(b + 1, 0, False)
                covariance(b, 1, False, False)
                turn_batch(b + 2, 1, False)
                covariance(b + 1, 0, False, False)
            covariance(B - 1, 1, False, True)

            for i in range(small_products):
                pe.wait_ge(operand_ready, i + 1)
                if i == 0:
                    pe.matmul(small[:, 0:1], blocks[:, :], diag[:, :], start=True, stop=True
                              ).then_inc(product_ready, 1)
                else:
                    left, right = ((power[0], power[0]), (power[1], power[0]), (power[2], sigma))[(i - 1) % 3]
                    pe.matmul(small[:, 0:P], left[:, :], right[:, :], start=True, stop=True
                              ).then_inc(product_ready, 1)
            pe.wait_ge(operand_ready, small_products + 1)

            def mix_batch(b, par, first):
                pe.wait_ge(recentred, b + 1)
                if not first:
                    pe.wait_ge(mixed_taken, b * 2 - 2)
                for h in range(2):
                    for j in range(4):
                        at = P * (4 * h + j)
                        done = pe.matmul(turn[par][h][:, P * j:P * j + P], centred[par][:, at:at + P],
                                         mix[:, :], start=True, stop=True)
                    done.then_inc(mixed, 1)

            mix_batch(0, 0, True)
            mix_batch(1, 1, True)
            with pe.Fori(2, B - 1, 2) as b:
                mix_batch(b, 0, False)
                mix_batch(b + 1, 1, False)

        @block.scalar
        def _(act):
            def take(b, par):
                act.wait_ge(turn_ready, b * 2 + 2)
                act.activation(turned[par][:, 4:8, :], turn[par][1][:, :].rearrange("p (a c) -> p a c", a=4),
                               ACT.Copy).then_inc(turned_high, 1)

            take(0, 0)
            take(1, 1)
            with act.Fori(2, B - 1, 2) as b:
                for par in range(2):
                    act.wait_ge(cov_done, b + par - 1)
                    take(b + par, par)
            act.wait_ge(root_asked, 1)
            act.activation(root[:, :], rtrace[:, :], ACT.Sqrt).then_inc(root_ready, 1)

        @block.vector
        def _(dve):
            steps = Steps(dve, dve_steps)
            steps.then(dve.bn_aggr(mean[:, :], stats[:, :, :].rearrange("p a s -> p (a s)")))
            steps.then(dve.tensor_scalar(negmean[:, :], mean[:, 0:1], -1.0, None, ALU.mult))

            def centre(b, par, signal):
                dve.tensor_scalar(centred[par][:, :], feats[:, bass.ds(b, 1), :].rearrange("p a n -> p (a n)"),
                                  negmean[:, 0:1], None, ALU.add).then_inc(signal, 1)

            def take(b, par, first):
                dve.wait_ge(turn_ready, b * 2 + 1)
                if not first:
                    dve.wait_ge(cov_done, b - 1)
                dve.tensor_copy(turned[par][:, 0:4, :], turn[par][0][:, :].rearrange("p (a c) -> p a c", a=4)
                                ).then_inc(turned_low, 1)

            centre(0, 0, centred_ready)
            centre(1, 1, centred_ready)
            take(0, 0, True)
            take(1, 1, True)
            with dve.Fori(2, B - 1, 2) as b:
                for par in range(2):
                    dve.wait_ge(turn_ready, (b + par) * 2 - 2)
                    centre(b + par, par, centred_ready)
                for par in range(2):
                    take(b + par, par, False)

            dve.wait_ge(cov_done, B)
            dve.wait_ge(blocks_ready, 1)
            steps.then(dve.scalar_tensor_tensor(out=sigma[:, :], in0=cov[:, 0:P], scalar=1.0 / (B * N),
                                                in1=blocks[:, :], op0=ALU.mult, op1=ALU.mult))
            steps.then(dve.scalar_tensor_tensor(out=sigma[:, :], in0=ident[:, :], scalar=WHITEN_EPS,
                                                in1=sigma[:, :], op0=ALU.mult, op1=ALU.add))
            steps.then(dve.tensor_tensor(scratch[:, :], sigma[:, :], ident[:, :], ALU.mult))
            dve.tensor_reduce(diag[:, :], scratch[:, :], AX.X, ALU.add).then_inc(operand_ready, 1)
            dve.wait_ge(product_ready, 1)
            steps.then(dve.reciprocal(rtrace[:, :], small[:, 0:1]))
            dve.tensor_scalar(sigma[:, :], sigma[:, :], rtrace[:, 0:1], None, ALU.mult).then_inc(root_asked, 1)
            dve.wait_ge(root_asked, 1)
            steps.then(dve.tensor_scalar(scratch[:, :], sigma[:, :], -0.5, None, ALU.mult))
            dve.scalar_tensor_tensor(out=power[0][:, :], in0=ident[:, :], scalar=1.5, in1=scratch[:, :],
                                     op0=ALU.mult, op1=ALU.add).then_inc(operand_ready, 1)
            n = 1
            for _ in range(WHITEN_STEPS - 1):
                for into in (1, 2):
                    n += 1
                    dve.wait_ge(product_ready, n)
                    dve.tensor_copy(power[into][:, :], small[:, 0:P]).then_inc(operand_ready, 1)
                n += 1
                steps.then(dve.tensor_scalar(scratch[:, :], power[0][:, :], 1.5, None, ALU.mult))
                dve.wait_ge(product_ready, n)
                dve.scalar_tensor_tensor(out=power[0][:, :], in0=small[:, 0:P], scalar=-0.5, in1=scratch[:, :],
                                         op0=ALU.mult, op1=ALU.add).then_inc(operand_ready, 1)
            dve.wait_ge(root_ready, 1)
            dve.wait_ge(params_loaded, 32)
            dve.wait_ge(operand_ready, n + 1)
            dve.scalar_tensor_tensor(out=mix[:, :], in0=power[0][:, :], scalar=root[:, 0:1], in1=weight[:, :],
                                     op0=ALU.mult, op1=ALU.mult).then_inc(operand_ready, 1)

            def give_tokens(b, par):
                for h in range(2):
                    dve.wait_ge(mixed, b * 2 + h + 1)
                    dve.tensor_tensor(tokens[:, bass.ds(b * NT + 4 * h, 4), :],
                                      turn[par][h][:, :].rearrange("p (a c) -> p a c", a=4),
                                      bias[:, :].unsqueeze(1).to_broadcast([P, 4, C]), ALU.add
                                      ).then_inc(mixed_taken, 1)

            centre(0, 0, recentred)
            centre(1, 1, recentred)
            with dve.Fori(0, B - 3, 2) as b:
                for par in range(2):
                    give_tokens(b + par, par)
                    centre(b + par + 2, par, recentred)
            give_tokens(B - 2, 0)
            give_tokens(B - 1, 1)



def store_images(nc, ident, tokens, out):
    image = out.rearrange("b c h w -> b c (h w)")
    with ExitStack() as ctx:
        t = Tools(nc, ctx)
        rows = [t.sbuf(f"rows{i}", [P, NT, C]) for i in range(2)]
        plane = [t.sbuf(f"plane{i}", [P, N]) for i in range(2)]
        turn = [t.psum(f"oturn{i}", [P, N]) for i in range(2)]
        rows_ready = t.sem("rows_ready")
        turned = t.sem("oturned")
        plane_ready = t.sem("plane_ready")
        stored = [t.sem(f"stored{i}") for i in range(2)]
        block = ctx.enter_context(nc.Block())

        @block.vector
        def _(dve):
            def stage(b, par):
                dve.tensor_copy(rows[par][:, :, :], tokens[:, bass.ds(b * NT, NT), :]).then_inc(rows_ready, 1)
            stage(0, 0)
            stage(1, 1)
            with dve.Fori(2, B - 1, 2) as b:
                for par in range(2):
                    dve.wait_ge(turned, b + par - 1)
                    stage(b + par, par)

        @block.tensor
        def _(pe):
            def turn_batch(b, par, first):
                pe.wait_ge(rows_ready, b + 1)
                if not first:
                    pe.wait_ge(plane_ready, b - 1)
                for j in range(NT):
                    done = pe.transpose(turn[par][:, P * j:P * j + P], rows[par][:, j, :], ident[:, :])
                done.then_inc(turned, 1)
            turn_batch(0, 0, True)
            turn_batch(1, 1, True)
            with pe.Fori(2, B - 1, 2) as b:
                for par in range(2):
                    turn_batch(b + par, par, False)

        @block.scalar
        def _(act):
            def take(b, par, first):
                act.wait_ge(turned, b + 1)
                if not first:
                    act.wait_ge(stored[par], (b - par) * 8)
                act.activation(plane[par][:, :], turn[par][:, :], ACT.Copy).then_inc(plane_ready, 1)
            take(0, 0, True)
            take(1, 1, True)
            with act.Fori(2, B - 1, 2) as b:
                for par in range(2):
                    take(b + par, par, False)

        @block.sync
        def _(sp):
            for b in range(B):
                sp.wait_ge(plane_ready, b + 1)
                sp.dma_start(image[b], plane[b % 2][:, :]).then_inc(stored[b % 2], 16)
            for par in range(2):
                sp.wait_ge(stored[par], 16 * B // 2)



HEADS2 = 8
HC = C // HEADS2
TOKEN_EPS = 1e-05
HEAD_EPS = 1e-05

class TokenNorm:

    def __init__(self, t, tag, twice=False):
        self.bn = t.sbuf(f"{tag}norm_bn", [P, TT, 6])
        self.mean = t.sbuf(f"{tag}norm_mean", [P, TT])
        self.half = t.sbuf(f"{tag}norm_half", [P, TT])
        self.var = t.sbuf(f"{tag}norm_var", [P, TT])
        self.eps_var = t.sbuf(f"{tag}norm_eps_var", [P, TT])
        self.root = [t.sbuf(f"{tag}norm_root{i}", [P, TT]) for i in range(1 + twice)]
        self.rstd = t.sbuf(f"{tag}norm_rstd", [P, TT])
        self.stats_sem = t.sem(f"{tag}norm_stats")
        self.steps_sem = t.sem(f"{tag}norm_steps")
        self.asked = t.sem(f"{tag}norm_asked")
        self.rooted = t.sem(f"{tag}norm_rooted")
        self.asked_n = self.rooted_n = 0
        self.steps = None

    def root_of(self, act, start=0, end=B):
        at = slice(start * NT, end * NT)
        for root in self.root:
            self.rooted_n += 1
            act.wait_ge(self.asked, self.rooted_n)
            act.activation(root[:, at], self.eps_var[:, at], ACT.Sqrt).then_inc(self.rooted, 1)

    def run(self, dve, tokens, start=0, end=B):
        def stats(b):
            for j in range(2 * NT):
                dve.bn_stats(self.bn[:, bass.ds(b * NT + j, 1), :].rearrange("p a c -> p (a c)"),
                             tokens[:, bass.ds(b * NT + j, 1), :].rearrange("p a c -> p (a c)")
                             ).then_inc(self.stats_sem, 1)
        if end - start == 2:
            stats(start)
        else:
            with dve.Fori(start, end - 1, 2) as b:
                stats(b)
        dve.wait_ge(self.stats_sem, end * NT)
        if self.steps is None:
            self.steps = Steps(dve, self.steps_sem)
        steps = self.steps
        at = slice(start * NT, end * NT)
        even, odd = (self.bn[:, at, 3 * i:3 * i + 3] for i in range(2))
        mean, half, var, eps_var, rstd = (x[:, at] for x in (self.mean, self.half, self.var, self.eps_var, self.rstd))
        steps.did(dve.tensor_tensor(half, even[:, :, 1], odd[:, :, 1], ALU.subtract))
        steps.did(dve.tensor_tensor(mean, even[:, :, 1], odd[:, :, 1], ALU.add))
        steps.did(dve.tensor_tensor(var, even[:, :, 2], odd[:, :, 2], ALU.add))
        steps.settle()
        steps.did(dve.tensor_tensor(half, half, half, ALU.mult))
        steps.did(dve.tensor_scalar(mean, mean, 0.5, None, ALU.mult))
        steps.did(dve.tensor_scalar(var, var, 1.0 / C, None, ALU.mult))
        steps.settle()
        steps.then(dve.scalar_tensor_tensor(out=var, in0=half, scalar=0.25, in1=var, op0=ALU.mult, op1=ALU.add))
        self.asked_n += 1
        dve.tensor_scalar(eps_var, var, TOKEN_EPS, None, ALU.add).then_inc(self.asked, 1)
        dve.wait_ge(self.rooted, self.asked_n)
        steps.then(dve.reciprocal(rstd, self.root[0][:, at]))
        if len(self.root) == 2:
            steps.then(dve.tensor_tensor(half, rstd, rstd, ALU.mult))
            steps.then(dve.tensor_tensor(half, half, var, ALU.mult))
            self.asked_n += 1
            dve.tensor_scalar(eps_var, half, TOKEN_EPS, None, ALU.add).then_inc(self.asked, 1)
            dve.wait_ge(self.rooted, self.asked_n)
            steps.then(dve.reciprocal(half, self.root[1][:, at]))
            steps.then(dve.tensor_tensor(rstd, rstd, half, ALU.mult))

    def apply(self, dve, tokens, b, u):
        for j in range(NT):
            at = bass.ds(b * NT + j, 1)
            done = dve.tensor_scalar(u[:, j, :], tokens[:, at, :].rearrange("p a c -> p (a c)"), self.mean[:, at],
                                     self.rstd[:, at], ALU.subtract, ALU.mult)
        return done


def linear_attention(nc, ins, ident, tokens):
    with ExitStack() as ctx:
        t = ClearedTools(nc, ctx)
        names = ["kln_weight", "kln_bias", "vln_weight", "vln_bias"]
        column = t.sbuf("lcolumn", [P, 2])
        rows = t.sbuf("lrows", [P, 2, C])
        blocks = t.sbuf("lblocks", [P, C])
        ones = t.sbuf("lones", [P, P])
        factor = [t.sbuf(f"lfactor{i}", [P, C]) for i in range(4)]
        head_sum = [t.sbuf(f"head_sum{i}", [P, NT * HEADS2]) for i in range(2)]
        offset = [t.sbuf(f"offset{i}", [P, N]) for i in range(2)]
        square = [t.sbuf(f"square{i}", [P, N]) for i in range(2)]
        norm = TokenNorm(t, "l")
        var = [t.sbuf(f"lvar{i}", [P, NT * HEADS2]) for i in range(2)]
        std = [t.sbuf(f"lstd{i}", [P, NT * HEADS2]) for i in range(2)]
        scale = [t.sbuf(f"lscale{i}", [P, NT * HEADS2]) for i in range(2)]
        term = t.sbuf("lterm", [P, C])
        z = [t.sbuf(f"z{i}", [P, NT, C + 1]) for i in range(2)]
        u = [t.sbuf(f"lu{i}", [P, NT, C]) for i in range(2)]
        uT = [t.sbuf(f"luT{i}", [P, N]) for i in range(2)]
        sums = [t.sbuf(f"lsums{i}", [P, 1]) for i in range(2)]
        kv = [t.sbuf(f"kv{i}", [P, C]) for i in range(2)]
        turn = [t.psum(f"lturn{h}", [P, HALF]) for h in range(2)]
        gram = [t.psum(f"gram{i}", [P, HALF]) for i in range(2)]
        result = [t.psum(f"lresult{h}", [P, HALF]) for h in range(2)]
        GS = slice(256, 256 + C)

        params_loaded = t.sem("lparams_loaded")
        blocks_ready = t.sem("lblocks_ready")
        pool_steps = t.sem("lpool_steps")
        setup_steps = t.sem("lsetup_steps")
        centre_steps = t.sem("lcentre_steps")
        squares_summed = t.sem("lsquares_summed")
        front_steps = t.sem("lfront_steps")
        back_steps = t.sem("lback_steps")
        offset_ready = t.sem("offset_ready")
        square_ready = t.sem("square_ready")
        var_ready = t.sem("lvar_ready")
        std_ready = t.sem("lstd_ready")
        z_ready = t.sem("z_ready")
        norm_ready = t.sem("lnorm_ready")
        centred = t.sem("lcentred")
        u_ready = t.sem("lu_ready")
        turn_ready = t.sem("lturn_ready")
        uT_ready = t.sem("luT_ready")
        gram_ready = t.sem("gram_ready")
        kv_ready = t.sem("kv_ready")
        result_ready = t.sem("lresult_ready")
        added = t.sem("ladded")
        block = ctx.enter_context(nc.Block())

        @block.sync
        def _(sp):
            for i in range(2):
                sp.dma_start(column[:, i:i + 1], ins["L2_attn_" + names[i]].rearrange("h a d -> (h d) a")
                             ).then_inc(params_loaded, 16)
                sp.dma_start(rows[:, i, :], row_to_all(ins["L2_attn_" + names[2 + i]].rearrange("h a d -> (h a d)"))
                             ).then_inc(params_loaded, 16)

        @block.gpsimd
        def _(pool):
            steps = Steps(pool, pool_steps)
            steps.did(pool.memset(ones[:, :], 1.0))
            for i in range(2):
                steps.did(pool.memset(z[i][:, :, C:C + 1], 1.0))
            steps.then(pool.memset(blocks[:, :], 1.0))
            grid = blocks[:, :].rearrange("p (g c) -> p g c", g=HEADS2)
            steps.then(pool.affine_select(out=grid, in_=grid, compare_op=ALU.is_ge, fill=0.0, base=0,
                                          pattern=[[-HC, HEADS2], [0, HC]], channel_multiplier=1))
            pool.affine_select(out=grid, in_=grid, compare_op=ALU.is_ge, fill=0.0, base=HC - 1,
                               pattern=[[HC, HEADS2], [0, HC]], channel_multiplier=-1).then_inc(blocks_ready, 1)

            def normalise(b, par, first=False):
                if not first:
                    pool.wait_ge(turn_ready, b - 1)
                at = bass.ds(b * NT, NT)
                over = lambda x: x[:, at].unsqueeze(2).to_broadcast([P, NT, C])
                pool.tensor_tensor(u[par][:, :, :], tokens[:, at, :], over(norm.mean), ALU.subtract).then_inc(centred, 1)
                pool.wait_ge(centred, b + 1)
                pool.tensor_tensor(u[par][:, :, :], u[par][:, :, :], over(norm.rstd), ALU.mult).then_inc(u_ready, 1)

            pool.wait_ge(norm_ready, 1)
            normalise(0, 0, first=True)
            normalise(1, 1, first=True)
            with pool.Fori(2, B - 1, 2) as b:
                normalise(b, 0)
                normalise(b + 1, 1)

        @block.vector
        def _(dve):
            norm.run(dve, tokens)
            dve.tensor_copy(term[:, 0:1], norm.rstd[:, 0:1]).then_inc(norm_ready, 1)
            dve.wait_ge(norm_ready, 1)

            steps = Steps(dve, setup_steps)
            dve.wait_ge(params_loaded, 64)
            dve.wait_ge(blocks_ready, 1)
            for i, (col, row, over) in enumerate(((0, 0, 1.0 / N), (0, 1, 1.0 / N), (1, 0, 1.0 / N), (1, 1, 1.0))):
                steps.then(dve.tensor_scalar(factor[i][:, :], rows[:, row, :], column[:, col:col + 1], over,
                                             ALU.mult, ALU.mult))
                steps.then(dve.tensor_tensor(factor[i][:, :], factor[i][:, :], blocks[:, :], ALU.mult))
            steps.then(dve.tensor_tensor(factor[3][:, :], factor[3][:, :], ident[:, :], ALU.add))

            centre = Steps(dve, centre_steps)
            front = Steps(dve, front_steps)
            back = Steps(dve, back_steps)

            def centre_heads(b, par):
                centre.round(b)
                batch = tokens[:, bass.ds(b * NT, NT), :].rearrange("p j (h d) -> p (j h) d", h=HEADS2)
                centre.then(dve.tensor_reduce(head_sum[par][:, :], batch, AX.X, ALU.add))
                centre.then(dve.tensor_scalar(head_sum[par][:, :], head_sum[par][:, :], 1.0 / HC, None, ALU.mult))
                dve.tensor_tensor(offset[par][:, :].rearrange("p (g d) -> p g d", d=HC), batch,
                                  head_sum[par][:, :].unsqueeze(2).to_broadcast([P, NT * HEADS2, HC]),
                                  ALU.subtract).then_inc(offset_ready, 1)

            def variance(b, par):
                dve.wait_ge(square_ready, b + 1)
                dve.tensor_reduce(head_sum[par][:, :], square[par][:, :].rearrange("p (g d) -> p g d", d=HC),
                                  AX.X, ALU.add).then_inc(squares_summed, 1)
                dve.wait_ge(squares_summed, b + 1)
                dve.tensor_scalar(var[par][:, :], head_sum[par][:, :], 1.0 / (HC - 1), None,
                                  ALU.mult).then_inc(var_ready, 1)

            def keys(b, par):
                front.round(b)
                dve.wait_ge(std_ready, b + 1)
                scales = scale[par][:, :].rearrange("p (j h) -> p j h", h=HEADS2)
                spread = norm.rstd[:, bass.ds(b * NT, NT)].unsqueeze(2).to_broadcast([P, NT, HEADS2])
                front.then(dve.tensor_tensor(scales, std[par][:, :].rearrange("p (j h) -> p j h", h=HEADS2),
                                             spread, ALU.mult))
                front.then(dve.tensor_scalar(scale[par][:, :], scale[par][:, :], HEAD_EPS, None, ALU.add))
                front.then(dve.reciprocal(scale[par][:, :], scale[par][:, :]))
                front.then(dve.tensor_tensor(scales, scales, spread, ALU.mult))
                dve.tensor_tensor(z[par][:, :, 0:C].rearrange("p j (h d) -> p j h d", h=HEADS2),
                                  offset[par][:, :].rearrange("p (j h d) -> p j h d", j=NT, h=HEADS2),
                                  scales.unsqueeze(3).to_broadcast([P, NT, HEADS2, HC]), ALU.mult
                                  ).then_inc(z_ready, 1)

            def combine(b, par):
                back.round(b)
                dve.wait_ge(gram_ready, b + 1)
                back.did(dve.tensor_copy(sums[par][:, :], gram[par][:, C:C + 1]))
                back.then(dve.tensor_tensor(kv[par][:, :], gram[par][:, 0:C], factor[0][:, :], ALU.mult))
                back.then(dve.scalar_tensor_tensor(out=kv[par][:, :], in0=factor[1][:, :], scalar=sums[par][:, 0:1],
                                                   in1=kv[par][:, :], op0=ALU.mult, op1=ALU.add))
                back.then(dve.tensor_tensor(term[:, :], gram[par][:, GS], factor[2][:, :], ALU.mult))
                back.then(dve.tensor_tensor(kv[par][:, :], kv[par][:, :], term[:, :], ALU.add))
                dve.tensor_tensor(kv[par][:, :], kv[par][:, :], factor[3][:, :], ALU.add).then_inc(kv_ready, 1)

            def add(b, par):
                dve.wait_ge(result_ready, b + 1)
                for h in range(2):
                    rows4 = tokens[:, bass.ds(b * NT + 4 * h, 4), :]
                    done = dve.tensor_tensor(rows4, rows4, result[h][:, :].rearrange("p (a c) -> p a c", a=4), ALU.add)
                done.then_inc(added, 1)

            def step(b, par, after=True, sums=True, sum2=True):
                if after:
                    centre_heads(b + 1, 1 - par)
                keys(b, par)
                if after:
                    variance(b + 1, 1 - par)
                if sum2:
                    add(b - 2, par)
                if sums:
                    combine(b - 1, 1 - par)

            centre_heads(0, 0)
            variance(0, 0)
            step(0, 0, sums=False, sum2=False)
            step(1, 1, sum2=False)
            with dve.Fori(2, B - 3, 2) as b:
                step(b, 0)
                step(b + 1, 1)
            step(B - 2, 0)
            step(B - 1, 1, after=False)
            combine(B - 1, 1)
            add(B - 2, 0)
            add(B - 1, 1)

        @block.scalar
        def _(act):
            def square_of(b, par):
                act.wait_ge(offset_ready, b + 1)
                act.activation(square[par][:, :], offset[par][:, :], ACT.Square).then_inc(square_ready, 1)
                act.wait_ge(var_ready, b + 1)
                act.activation(std[par][:, :], var[par][:, :], ACT.Sqrt).then_inc(std_ready, 1)

            def batch(b, par, after=True):
                if after:
                    square_of(b + 1, 1 - par)
                act.wait_ge(turn_ready, b + 1)
                for h in range(2):
                    done = act.activation(uT[par][:, HALF * h:HALF * h + HALF], turn[h][:, :], ACT.Copy)
                done.then_inc(uT_ready, 1)

            norm.root_of(act)
            square_of(0, 0)
            batch(0, 0)
            batch(1, 1)
            with act.Fori(2, B - 3, 2) as b:
                batch(b, 0)
                batch(b + 1, 1)
            batch(B - 2, 0)
            batch(B - 1, 1, after=False)

        @block.tensor
        def _(pe):
            pe.wait_ge(pool_steps, 4)

            def batch(b, par, first=False):
                pe.wait_ge(u_ready, b + 1)
                if not first:
                    pe.wait_ge(uT_ready, b)
                for j in range(NT):
                    done = pe.transpose(turn[j // 4][:, P * (j % 4):P * (j % 4) + P], u[par][:, j, :], ident[:, :])
                done.then_inc(turn_ready, 1)
                pe.wait_ge(z_ready, b + 1)
                for j in range(NT):
                    pe.matmul(gram[par][:, 0:C + 1], z[par][:, j, 0:C], z[par][:, j, :],
                              start=(j == 0), stop=(j == NT - 1))
                for j in range(NT):
                    done = pe.matmul(gram[par][:, GS], ones[:, :], z[par][:, j, 0:C],
                                     start=(j == 0), stop=(j == NT - 1))
                done.then_inc(gram_ready, 1)

            def give(b, par, first=False):
                pe.wait_ge(kv_ready, b + 1)
                pe.wait_ge(uT_ready, b + 1)
                if not first:
                    pe.wait_ge(added, b)
                for j in range(NT):
                    done = pe.matmul(result[j // 4][:, P * (j % 4):P * (j % 4) + P], uT[par][:, P * j:P * j + P],
                                     kv[par][:, :], start=True, stop=True)
                done.then_inc(result_ready, 1)

            batch(0, 0, first=True)
            batch(1, 1)
            give(0, 0, first=True)
            with pe.Fori(2, B - 1, 2) as b:
                batch(b, 0)
                give(b - 1, 1)
                batch(b + 1, 1)
                give(b, 0)
            give(B - 1, 1)



E = 8
UNIT = 4

GROUP_TILES = [8, 24, 24, 8]
GROUPS = len(GROUP_TILES)
GROUP_SLOT_TILES = [-(-(2 * n + E - 1) // 8) * 8 for n in GROUP_TILES]
UNITS = [n // UNIT for n in GROUP_TILES]
QUADS = [n // 4 for n in GROUP_SLOT_TILES]
FIRST_TILE, FIRST_SLOT, FIRST_UNIT = ([sum(n[:g]) for g in range(GROUPS + 1)]
                                      for n in (GROUP_TILES, GROUP_SLOT_TILES, UNITS))
SLOT_TILES = FIRST_SLOT[-1]
assert sum(GROUP_TILES) == TT and all(n % 2 == 0 for n in UNITS)
BIG = 3.0e38
ROUND = 1.5 * 2.0 ** 23


class Expert:

    def __init__(self, kind, width):
        self.gelu = kind == "gelu"
        self.width = width
        self.even = width + width % 2
        self.chunks = [(k, min(P, width - k)) for k in range(0, width, P)]


def route(nc, kind, router, rbias, ident, tokens, normed, masks, gates, places, owner, tag,
          setup):
    with ExitStack() as ctx:
        t = Tools(nc, ctx)
        norm = TokenNorm(t, tag, twice=kind.gelu)
        u = [t.sbuf(f"{tag}u{i}", [P, NT, C]) for i in range(2)]
        uT = [t.sbuf(f"{tag}uT{i}", [P, N]) for i in range(2)]
        logits = t.sbuf(f"{tag}logits", [P, TT, E])
        work = t.sbuf(f"{tag}work", [P, TT, E])
        best = [t.sbuf(f"{tag}best{i}", [P, TT]) for i in range(2)]
        first = t.sbuf(f"{tag}first", [P, TT])
        rank = t.sbuf(f"{tag}rank", [P, E])
        rank_i = t.sbuf(f"{tag}rank_i", [P, E], I32)
        chosen = t.sbuf(f"{tag}chosen", [P, E * TT], BF16)
        upper = t.sbuf(f"{tag}upper", [P, P], BF16)
        ones = t.sbuf(f"{tag}ones", [P, P], BF16)
        ones_row = t.sbuf(f"{tag}ones_row", [P, E * TT])
        count = t.sbuf(f"{tag}count", [P, E * TT])
        before = t.sbuf(f"{tag}before", [P, E * TT])
        total = t.sbuf(f"{tag}total", [P, GROUPS, E])
        running = t.sbuf(f"{tag}running", [P, GROUPS, E])
        padded = t.sbuf(f"{tag}padded", [P, GROUPS, E])
        ends = t.sbuf(f"{tag}ends", [P, GROUPS, E])
        shift = t.sbuf(f"{tag}shift", [P, GROUPS, E])
        slot_i = t.sbuf(f"{tag}slot_i", [1, max(GROUP_SLOT_TILES)], I32)
        slot_f = t.sbuf(f"{tag}slot_f", [1, max(GROUP_SLOT_TILES)])
        passed = t.sbuf(f"{tag}passed", [1, SLOT_TILES, E])
        owner_f = t.sbuf(f"{tag}owner_f", [1, SLOT_TILES])
        slot_no = t.sbuf(f"{tag}slot_no", [P, TT, 2])
        part_i = [t.sbuf(f"{tag}part{i}", [P, TT, 2], I32) for i in range(2)]
        turn = [[t.psum(f"{tag}turn{i}{h}", [P, HALF]) for h in range(2)] for i in range(2)]
        score = [t.psum(f"{tag}score{i}", [P, HALF]) for i in range(2)]
        ahead = t.psum(f"{tag}ahead", [P, HALF])
        totals = t.psum(f"{tag}totals", [P, HALF])

        constants = t.sem(f"{tag}constants")
        pool_steps = t.sem(f"{tag}pool_steps")
        steps_sem = t.sem(f"{tag}steps")
        u_ready = t.sem(f"{tag}u_ready")
        copied = t.sem(f"{tag}copied")
        turn_ready = t.sem(f"{tag}turn_ready")
        uT_ready = t.sem(f"{tag}uT_ready")
        score_ready = t.sem(f"{tag}score_ready")
        score_taken = t.sem(f"{tag}score_taken")
        exp_asked = t.sem(f"{tag}exp_asked")
        exp_done = t.sem(f"{tag}exp_done")
        chosen_ready = t.sem(f"{tag}chosen_ready")
        counted = t.sem(f"{tag}counted")
        block = ctx.enter_context(nc.Block())

        @block.sync
        def _(sp):
            setup.sync(sp)

        @block.gpsimd
        def _(pool):
            steps = Steps(pool, pool_steps)
            steps.did(pool.iota(rank_i[:, :], [[-1, E]], base=E, channel_multiplier=0))
            steps.did(pool.iota(slot_i[:, :], [[P, max(GROUP_SLOT_TILES)]], base=0, channel_multiplier=0))
            steps.did(pool.memset(ones[:, :], 1.0))
            steps.did(pool.memset(ones_row[:, :], 1.0))
            steps.then(pool.memset(upper[:, :], 1.0))
            steps.did(pool.tensor_copy(rank[:, :], rank_i[:, :]))
            steps.did(pool.tensor_copy(slot_f[:, :], slot_i[:, :]))
            steps.then(pool.affine_select(out=upper[:, :], in_=upper[:, :], compare_op=ALU.is_gt, fill=0.0, base=0,
                                          pattern=[[1, P]], channel_multiplier=-1))
            pool.memset(owner_f[:, :], 0.0).then_inc(constants, 1)
            setup.gpsimd(pool)

            def keep(b, par):
                pool.wait_ge(u_ready, b + 1)
                pool.tensor_copy(normed[:, bass.ds(b * NT, NT), :], u[par][:, :, :]).then_inc(copied, 1)
            keep(0, 0)
            keep(1, 1)
            with pool.Fori(2, B - 1, 2) as b:
                keep(b, 0)
                keep(b + 1, 1)

        @block.tensor
        def _(pe):
            def turn_batch(b, par, first=False):
                pe.wait_ge(u_ready, b + 1)
                if not first:
                    pe.wait_ge(uT_ready, b - 1)
                for j in range(NT):
                    done = pe.transpose(turn[par][j // 4][:, P * (j % 4):P * (j % 4) + P], u[par][:, j, :], ident[:, :])
                done.then_inc(turn_ready, 1)

            def score_batch(b, par, first=False):
                pe.wait_ge(uT_ready, b + 1)
                if not first:
                    pe.wait_ge(score_taken, b - 1)
                for j in range(NT):
                    done = pe.matmul(score[par][:, E * j:E * j + E], uT[par][:, P * j:P * j + P], router[:, :],
                                     start=True, stop=True)
                done.then_inc(score_ready, 1)

            setup.tensor(pe, totals, ahead)
            turn_batch(0, 0, first=True)
            turn_batch(1, 1, first=True)
            score_batch(0, 0, first=True)
            turn_batch(2, 0)
            score_batch(1, 1, first=True)
            with pe.Fori(2, B - 3, 2) as b:
                for par in range(2):
                    turn_batch(b + par + 1, 1 - par)
                    score_batch(b + par, par)
            turn_batch(B - 1, 1)
            score_batch(B - 2, 0)
            score_batch(B - 1, 1)
            pe.wait_ge(constants, 1)
            pe.wait_ge(chosen_ready, GROUPS)
            pe.matmul(ahead[:, :], upper[:, :], chosen[:, :], start=True, stop=True).then_inc(counted, 1)
            pe.matmul(totals[:, :], ones[:, :], chosen[:, :], start=True, stop=True).then_inc(counted, 1)

        @block.scalar
        def _(act):
            def batch(b, par):
                act.wait_ge(turn_ready, b + 1)
                for h in range(2):
                    done = act.activation(uT[par][:, HALF * h:HALF * h + HALF], turn[par][h][:, :], ACT.Copy)
                done.then_inc(uT_ready, 1)
            norm.root_of(act, 0, 2)
            setup.scalar(act, totals, ahead)
            norm.root_of(act, 2, B)
            batch(0, 0)
            batch(1, 1)
            with act.Fori(2, B - 1, 2) as b:
                for par in range(2):
                    act.wait_ge(score_ready, b + par - 1)
                    batch(b + par, par)
            act.wait_ge(exp_asked, 1)
            act.activation(work[:, :, :], work[:, :, :], ACT.Exp).then_inc(exp_done, 1)
            act.activation(best[1][:, :], best[1][:, :], ACT.Exp).then_inc(exp_done, 1)

        @block.vector
        def _(dve):
            def normalise(b, par, first=False):
                if not first:
                    dve.wait_ge(copied, b - 1)
                    dve.wait_ge(turn_ready, b - 1)
                norm.apply(dve, tokens, b, u[par]).then_inc(u_ready, 1)

            def take_scores(b, par):
                dve.wait_ge(score_ready, b + 1)
                dve.tensor_copy(logits[:, bass.ds(b * NT, NT), :],
                                score[par][:, 0:NT * E].rearrange("p (j e) -> p j e", e=E)).then_inc(score_taken, 1)

            norm.run(dve, tokens, 0, 2)
            normalise(0, 0, first=True)
            normalise(1, 1, first=True)
            norm.run(dve, tokens, 2, B)
            with dve.Fori(2, B - 1, 2) as b:
                for par in range(2):
                    normalise(b + par, par)
                    take_scores(b + par - 2, par)
            take_scores(B - 2, 0)
            take_scores(B - 1, 1)

            steps = Steps(dve, steps_sem)
            dve.wait_ge(score_taken, B)
            dve.wait_ge(constants, 1)
            if kind.gelu:
                dve.wait_ge(setup.loaded[1], 64)
            over_e = [P, TT, E]
            if kind.gelu:
                steps.then(dve.tensor_tensor(logits[:, :, :], logits[:, :, :],
                                             norm.root[1][:, :].unsqueeze(2).to_broadcast(over_e), ALU.mult))
                steps.then(dve.tensor_tensor(logits[:, :, :], logits[:, :, :],
                                             rbias[:, :].unsqueeze(1).to_broadcast(over_e), ALU.add))
            ranks = rank[:, :].unsqueeze(1).to_broadcast(over_e)
            for r in range(2):
                steps.then(dve.tensor_reduce(best[r][:, :], logits[:, :, :] if r == 0 else work[:, :, :],
                                             AX.X, ALU.max))
                steps.then(dve.tensor_tensor(masks[r][:, :, :], logits[:, :, :] if r == 0 else work[:, :, :],
                                             best[r][:, :].unsqueeze(2).to_broadcast(over_e), ALU.is_ge))
                steps.then(dve.tensor_tensor(masks[r][:, :, :], masks[r][:, :, :], ranks, ALU.mult))
                steps.then(dve.tensor_reduce(first[:, :], masks[r][:, :, :], AX.X, ALU.max))
                steps.then(dve.tensor_tensor(masks[r][:, :, :], masks[r][:, :, :],
                                             first[:, :].unsqueeze(2).to_broadcast(over_e), ALU.is_equal))
                if r == 0:
                    steps.then(dve.scalar_tensor_tensor(out=work[:, :, :], in0=masks[0][:, :, :], scalar=-BIG,
                                                        in1=logits[:, :, :], op0=ALU.mult, op1=ALU.add))
            def of_group(x, g):
                return x[:, E * FIRST_TILE[g]:E * FIRST_TILE[g + 1]].rearrange("p (e t) -> p t e", e=E)

            tiles_of = [slice(FIRST_TILE[g], FIRST_TILE[g + 1]) for g in range(GROUPS)]
            for g, tiles in enumerate(tiles_of):
                dve.tensor_tensor(of_group(chosen, g), masks[0][:, tiles, :], masks[1][:, tiles, :], ALU.add
                                  ).then_inc(chosen_ready, 1)

            steps.did(dve.tensor_tensor(work[:, :, :], logits[:, :, :],
                                        best[0][:, :].unsqueeze(2).to_broadcast(over_e), ALU.subtract))
            dve.tensor_tensor(best[1][:, :], best[1][:, :], best[0][:, :], ALU.subtract).then_inc(exp_asked, 1)
            dve.wait_ge(exp_done, 2)
            if kind.gelu:
                steps.then(dve.tensor_scalar(best[0][:, :], best[1][:, :], 1.0, None, ALU.add))
            else:
                steps.then(dve.tensor_reduce(first[:, :], work[:, :, :], AX.X, ALU.add))
                steps.then(dve.scalar_tensor_tensor(out=best[0][:, :], in0=first[:, :], scalar=1e-09,
                                                    in1=best[1][:, :], op0=ALU.mult, op1=ALU.add))
                steps.then(dve.tensor_scalar(best[0][:, :], best[0][:, :], 1.0, None, ALU.add))
            steps.then(dve.reciprocal(best[0][:, :], best[0][:, :]))
            steps.did(dve.tensor_copy(gates[:, :, 0], best[0][:, :]))
            steps.did(dve.tensor_tensor(gates[:, :, 1], best[1][:, :], best[0][:, :], ALU.mult))

            dve.wait_ge(counted, 2)
            flat = lambda x: x[:, :, :].rearrange("p a b -> p (a b)")
            steps.then(dve.tensor_copy(count[:, :], totals[:, :]))
            steps.did(dve.tensor_tensor_scan(before[:, :], ones_row[:, :], count[:, :], 0.0, ALU.mult, ALU.add))
            for g in range(GROUPS):
                steps.did(dve.tensor_reduce(total[:, g, :], of_group(count, g).rearrange("p t e -> p e t"), AX.X,
                                            ALU.add))
            steps.settle()
            steps.did(dve.tensor_tensor_scan(flat(running), ones_row[:, 0:GROUPS * E], flat(total), 0.0,
                                             ALU.mult, ALU.add))
            steps.then(dve.tensor_scalar(flat(padded), flat(total), (P - 1) / 2.0, 1.0 / P, ALU.add, ALU.mult))
            steps.then(dve.tensor_scalar(flat(padded), flat(padded), ROUND, None, ALU.add))
            steps.then(dve.tensor_scalar(flat(padded), flat(padded), -ROUND, float(P), ALU.add, ALU.mult))
            for g in range(GROUPS):
                steps.did(dve.tensor_tensor_scan(ends[:, g, :], ones_row[:, 0:E], padded[:, g, :], 0.0,
                                                 ALU.mult, ALU.add))
            steps.settle()
            steps.did(dve.tensor_tensor(flat(shift), flat(ends), flat(padded), ALU.subtract))
            steps.did(dve.tensor_tensor(flat(total), flat(running), flat(total), ALU.subtract))
            steps.then(dve.tensor_tensor(before[:, :], before[:, :], count[:, :], ALU.subtract))
            steps.did(dve.tensor_tensor(flat(shift), flat(shift), flat(total), ALU.subtract))
            steps.then(dve.tensor_tensor(before[:, :], before[:, :], ahead[:, :], ALU.add))
            for g, n in enumerate(GROUP_TILES):
                steps.did(dve.tensor_tensor(of_group(before, g), of_group(before, g),
                                            shift[:, g, :].unsqueeze(1).to_broadcast([P, n, E]), ALU.add))
            steps.settle()
            for r in range(2):
                for g, tiles in enumerate(tiles_of):
                    steps.did(dve.tensor_tensor(work[:, tiles, :], masks[r][:, tiles, :], of_group(before, g), ALU.mult))
                steps.settle()
                steps.then(dve.tensor_reduce(slot_no[:, :, r], work[:, :, :], AX.X, ALU.add))
            steps.then(dve.tensor_copy(flat(part_i[0]), flat(slot_no)))
            steps.did(dve.tensor_scalar(flat(places), flat(part_i[0]), -4 * P, None, ALU.bitwise_and))
            steps.did(dve.tensor_scalar(flat(part_i[1]), flat(part_i[0]), P - 1, 2, ALU.bitwise_and,
                                        ALU.logical_shift_left))
            steps.settle()
            steps.then(dve.tensor_scalar(flat(part_i[0]), flat(part_i[0]), 7, 3, ALU.logical_shift_right,
                                         ALU.bitwise_and))
            steps.then(dve.tensor_tensor(flat(places), flat(places), flat(part_i[1]), ALU.bitwise_or))
            steps.then(dve.tensor_tensor(flat(places), flat(places), flat(part_i[0]), ALU.bitwise_or))
            for g, n in enumerate(GROUP_SLOT_TILES):
                steps.did(dve.tensor_tensor(passed[:, FIRST_SLOT[g]:FIRST_SLOT[g + 1], :],
                                            ends[0:1, g, :].unsqueeze(1).to_broadcast([1, n, E]),
                                            slot_f[:, 0:n].unsqueeze(2).to_broadcast([1, n, E]), ALU.is_le))
            steps.settle()
            steps.then(dve.tensor_reduce(owner_f[:, :], passed[:, :, :], AX.X, ALU.add))
            steps.then(dve.tensor_scalar(owner_f[:, :], owner_f[:, :], float(E - 1), None, ALU.min))
            eights = owner_f[:, :].rearrange("a (q k) -> a q k", k=8)
            for k in range(6, -1, -1):
                steps.then(dve.scalar_tensor_tensor(out=eights[:, :, k], in0=eights[:, :, k + 1], scalar=float(E),
                                                    in1=eights[:, :, k], op0=ALU.mult, op1=ALU.add))
            steps.then(dve.tensor_copy(owner[:, :], eights[:, :, 0]))


def run_experts(nc, kind, w_up, w_gate, w_down, up_bias, down_bias, ident, tokens, normed, gates, places,
                owner, sorted_rows, sorted_results, tag):
    row_quads = [x.rearrange("(q p k) c -> q p (k c)", p=P, k=4) for x in sorted_rows]
    result_quads = [x.rearrange("(q p k) c -> q p (k c)", p=P, k=4) for x in sorted_results]
    W, WE = kind.width, kind.even
    chunks = kind.chunks
    whole = sum(width == P for _, width in chunks)
    with ExitStack() as ctx:
        t = Tools(nc, ctx)
        send = [t.sbuf(f"{tag}send{i}", [P, UNIT, C]) for i in range(2)]
        send_at = [t.sbuf(f"{tag}send_at{i}", [P, UNIT, 2], I32) for i in range(2)]
        fetch = [t.sbuf(f"{tag}fetch{i}", [P, UNIT, 2, C]) for i in range(2)]
        fetch_at = [t.sbuf(f"{tag}fetch_at{i}", [P, UNIT, 2], I32) for i in range(2)]
        xq = [t.sbuf(f"{tag}xq{i}", [P, 4, C]) for i in range(2)]
        yq = [t.sbuf(f"{tag}yq{i}", [P, 4, C]) for i in range(2)]
        xT = [t.sbuf(f"{tag}xT_{part}", [P, 4, P], F32R) for part in ("high", "low")]
        silu = None if kind.gelu else [t.sbuf(f"{tag}silu{i}", [P, W]) for i in range(2)]
        hidden = [t.sbuf(f"{tag}hidden{i}", [P, W]) for i in range(2)]
        hT = [t.sbuf(f"{tag}hT{i}", [P, len(chunks), P]) for i in range(2)]
        ones = t.sbuf(f"{tag}ones", [3, P], BF16)
        up = [t.psum(f"{tag}up{i}", [P, HALF]) for i in range(2)]
        gate = None if kind.gelu else [t.psum(f"{tag}gate{i}", [P, HALF]) for i in range(2)]
        hturn = [t.psum(f"{tag}hturn{i}", [P, HALF]) for i in range(2)]
        xturn = t.psum(f"{tag}xturn", [P, P])
        down = t.psum(f"{tag}down", [P, C])

        staged = t.sem(f"{tag}staged")
        indexed = t.sem(f"{tag}indexed")
        sent = [t.sem(f"{tag}sent{i}") for i in range(2)]
        fetched = [t.sem(f"{tag}fetched{i}") for i in range(2)]
        fetch_used = t.sem(f"{tag}fetch_used")
        x_loaded = [t.sem(f"{tag}x_loaded{i}") for i in range(2)]
        y_stored = [t.sem(f"{tag}y_stored{i}") for i in range(2)]
        ones_ready = t.sem(f"{tag}ones_ready")
        x_turned = t.sem(f"{tag}x_turned")
        x_high = t.sem(f"{tag}x_high")
        xT_ready = t.sem(f"{tag}xT_ready")
        up_done = t.sem(f"{tag}up_done")
        silu_ready = None if kind.gelu else t.sem(f"{tag}silu_ready")
        hidden_ready = t.sem(f"{tag}hidden_ready")
        h_turned = t.sem(f"{tag}h_turned")
        hT_ready = t.sem(f"{tag}hT_ready")
        down_done = t.sem(f"{tag}down_done")
        y_ready = t.sem(f"{tag}y_ready")
        added = t.sem(f"{tag}added")
        block = ctx.enter_context(nc.Block())
        last = SLOT_TILES - 1

        def known(s, least):
            return not isinstance(s, int) or s >= least

        @block.gpsimd
        def _(pool):
            pool.memset(ones[:, :], 1.0).then_inc(ones_ready, 1)
            sent_goal = [pool.alloc_register(f"{tag}sent_goal{i}") for i in range(2)]
            used_goal = [pool.alloc_register(f"{tag}used_goal{i}") for i in range(2)]
            staged_goal = pool.alloc_register(f"{tag}staged_goal")
            indexed_goal = pool.alloc_register(f"{tag}indexed_goal")
            for i in range(2):
                pool.reg_mov(sent_goal[i], 2 * UNIT * 16)
                pool.reg_mov(used_goal[i], 1 + i)
            pool.reg_mov(staged_goal, 2)
            pool.reg_mov(indexed_goal, 1)

            def send_unit(g, n, par):
                if known(n, 2):
                    pool.wait_ge(sent[par], sent_goal[par])
                    pool.reg_add(sent_goal[par], sent_goal[par], 2 * UNIT * 16)
                if isinstance(n, int):
                    for i in range(UNIT):
                        for r in range(2):
                            at = n * UNIT + i
                            pool.indirect_dma_start(
                                out=sorted_rows[g], out_offset=bass.IndirectOffsetOnAxis(ap=places[:, at, r:r + 1], axis=0),
                                in_=normed[:, at, :], in_offset=None).then_inc(sent[par], 16)
                    return
                pool.tensor_copy(send[par][:, :, :], normed[:, bass.ds(n * UNIT, UNIT), :]).then_inc(staged, 1)
                pool.tensor_copy(send_at[par][:, :, :], places[:, bass.ds(n * UNIT, UNIT), :]).then_inc(staged, 1)
                pool.wait_ge(staged, staged_goal)
                pool.reg_add(staged_goal, staged_goal, 2)
                for i in range(UNIT):
                    for r in range(2):
                        pool.indirect_dma_start(
                            out=sorted_rows[g], out_offset=bass.IndirectOffsetOnAxis(ap=send_at[par][:, i, r:r + 1], axis=0),
                            in_=send[par][:, i, :], in_offset=None).then_inc(sent[par], 16)

            def fetch_unit(g, n, par):
                if known(n, 2):
                    pool.wait_ge(fetch_used, used_goal[par])
                    pool.reg_add(used_goal[par], used_goal[par], 2)
                pool.tensor_copy(fetch_at[par][:, :, :], places[:, bass.ds(n * UNIT, UNIT), :]).then_inc(indexed, 1)
                pool.wait_ge(indexed, indexed_goal)
                pool.reg_add(indexed_goal, indexed_goal, 1)
                for i in range(UNIT):
                    for r in range(2):
                        pool.indirect_dma_start(
                            out=fetch[par][:, i, r, :], out_offset=None, in_=sorted_results[g],
                            in_offset=bass.IndirectOffsetOnAxis(ap=fetch_at[par][:, i, r:r + 1], axis=0)
                            ).then_inc(fetched[par], 16)

            def over_units(g, unit):
                start, end = FIRST_UNIT[g], FIRST_UNIT[g + 1]
                if g == 0:
                    unit(g, 0, 0)
                    unit(g, 1, 1)
                    start = 2
                if start < end:
                    with pool.Fori(start, end - 1, 2) as n:
                        unit(g, n, 0)
                        unit(g, n + 1, 1)

            def fetch_group(g):
                for par in range(2):
                    pool.wait_ge(y_stored[par], 16 * FIRST_SLOT[g + 1] // 8)
                over_units(g, fetch_unit)

            over_units(0, send_unit)
            for g in range(1, GROUPS):
                over_units(g, send_unit)
                fetch_group(g - 1)
            fetch_group(GROUPS - 1)

        @block.sync
        def _(sp):
            def load(g, q, par):
                if known(q, 2) or g > 0:
                    sp.wait_ge(x_turned, q * 4 + (FIRST_SLOT[g] - 4))
                sp.dma_start(xq[par][:, :, :], row_quads[g][bass.ds(q, 1), :, :].rearrange("a p (k c) -> p (a k) c", k=4)
                             ).then_inc(x_loaded[par], 16)

            def store(g, q, par):
                sp.wait_ge(y_ready, q * 4 + (FIRST_SLOT[g] + 4))
                sp.dma_start(result_quads[g][bass.ds(q, 1), :, :].rearrange("a p (k c) -> p (a k) c", k=4),
                             yq[par][:, :, :]).then_inc(y_stored[par], 16)

            for g in range(GROUPS):
                for par in range(2):
                    sp.wait_ge(sent[par], FIRST_UNIT[g + 1] // 2 * 2 * UNIT * 16)
                for par in range(2):
                    load(g, par, par)
                    if g > 0:
                        store(g - 1, QUADS[g - 1] - 2 + par, par)
                with sp.Fori(2, QUADS[g] - 1, 2) as q:
                    for par in range(2):
                        load(g, q + par, par)
                        store(g, q + par - 2, par)
            for par in range(2):
                store(GROUPS - 1, QUADS[-1] - 2 + par, par)
            for par in range(2):
                sp.wait_ge(y_stored[par], 16 * SLOT_TILES // 8)

        @block.tensor
        def _(pe):
            def owners(q):
                word = pe.value_load(owner[0:1, bass.ds(q, 1)], min_val=0, max_val=E ** 8 - 1)
                return [(word >> 3 * k) & E - 1 for k in range(8)]

            def product(out, left, right, final=True):
                for i, (l, r) in enumerate(((0, 0), (0, 1), (1, 0))):
                    done = pe.matmul(out, left[l], right[r], start=(i == 0), stop=(final and i == 2))
                return done

            def turn_x(s, k, qpar):
                if k == 0:
                    pe.wait_ge(x_loaded[qpar], (s - 4 * qpar) * 2 + 16)
                if known(s, 1):
                    pe.wait_ge(xT_ready, s)
                pe.transpose(xturn[:, :], xq[qpar][:, k, :], ident[:, :]).then_inc(x_turned, 1)

            def go_up(s, k, e):
                par = k % 2
                pe.wait_ge(xT_ready, s + 1)
                if known(s, 2):
                    pe.wait_ge(hidden_ready, s - 1)
                left = [part[:, k, :] for part in xT]
                rows = lambda w: [part[:, bass.ds(e, 1), 0:WE].rearrange("p a h -> p (a h)") for part in w]
                done = product(up[par][:, 0:WE], left, rows(w_up), final=not kind.gelu)
                if kind.gelu:
                    done = pe.matmul(up[par][:, 0:W], ones[:, :],
                                     up_bias[:, bass.ds(e, 1), :].rearrange("p a h -> p (a h)"), start=False, stop=True)
                else:
                    done = product(gate[par][:, 0:WE], left, rows(w_gate))
                done.then_inc(up_done, 1)

            def turn_hidden(s, par):
                pe.wait_ge(hidden_ready, s + 1)
                if known(s, 2):
                    pe.wait_ge(hT_ready, s - 1)
                for i, (at, width) in enumerate(chunks):
                    done = pe.transpose(hturn[par][0:width, P * i:P * i + P], hidden[par][:, at:at + width], ident[:, :])
                done.then_inc(h_turned, 1)

            def go_down(s, par, e):
                pe.wait_ge(hT_ready, s + 1)
                if known(s, 1):
                    pe.wait_ge(y_ready, s)
                for i, (_, width) in enumerate(chunks):
                    done = pe.matmul(down[:, :], hT[par][0:width, i, :],
                                     w_down[0:width, bass.ds(e, 1), i, :].rearrange("p a c -> p (a c)"),
                                     start=(i == 0), stop=(i == len(chunks) - 1 and not kind.gelu))
                if kind.gelu:
                    done = pe.matmul(down[:, :], ones[:, :],
                                     down_bias[:, bass.ds(e, 1), :].rearrange("p a c -> p (a c)"), start=False, stop=True)
                done.then_inc(down_done, 1)

            def step(s, k, qpar, e, e_down, ending=False):
                if not (ending and k == 3):
                    turn_x(s + 1, (k + 1) % 4, qpar if k < 3 else 1 - qpar)
                go_up(s, k, e)
                if known(s, 1):
                    turn_hidden(s - 1, 1 - k % 2)
                if known(s, 2):
                    go_down(s - 2, k % 2, e_down)

            if kind.gelu:
                pe.wait_ge(ones_ready, 1)
            turn_x(0, 0, 0)
            e = owners(0)
            for k in range(8):
                step(k, k % 4, k // 4, e[k], e[k - 2])
            with pe.Fori(1, SLOT_TILES // 8 - 1, 1) as q:
                e = owners(q - 1)[6:] + owners(q)
                for k in range(8):
                    step(q * 8 + k, k % 4, k // 4, e[2 + k], e[k])
            e = owners(SLOT_TILES // 8 - 2)[6:] + owners(SLOT_TILES // 8 - 1)
            for k in range(8):
                step(SLOT_TILES - 8 + k, k % 4, k // 4, e[2 + k], e[k], ending=(k // 4 == 1))
            turn_hidden(last, 1)
            go_down(last - 1, 0, e[8])
            go_down(last, 1, e[9])

        @block.scalar
        def _(act):
            def act_hidden(s, par):
                act.wait_ge(up_done, s + 1)
                if kind.gelu:
                    if known(s, 2):
                        act.wait_ge(h_turned, s - 1)
                    act.activation(hidden[par][:, :], up[par][:, 0:W], ACT.Gelu).then_inc(hidden_ready, 1)
                else:
                    if known(s, 2):
                        act.wait_ge(hidden_ready, s - 1)
                    act.activation(silu[par][:, :], up[par][:, 0:W], ACT.Silu).then_inc(silu_ready, 1)

            def take_hidden(s, par):
                act.wait_ge(h_turned, s + 1)
                if known(s, 2):
                    act.wait_ge(down_done, s - 1)
                done = act.activation(hT[par][:, 0:whole, :],
                                      hturn[par][:, 0:P * whole].rearrange("p (k m) -> p k m", m=P), ACT.Copy)
                if whole < len(chunks):
                    width = chunks[whole][1]
                    done = act.activation(hT[par][0:width, whole, :], hturn[par][0:width, P * whole:P * whole + P],
                                          ACT.Copy)
                done.then_inc(hT_ready, 1)

            def step(s, k):
                act_hidden(s, k % 2)
                if known(s, 1):
                    take_hidden(s - 1, 1 - k % 2)

            for k in range(4):
                step(k, k)
            with act.Fori(4, SLOT_TILES - 3, 4) as s:
                for k in range(4):
                    step(s + k, k)
            take_hidden(last, 1)

        @block.vector
        def _(dve):
            def take_x_high(s, k):
                dve.wait_ge(x_turned, s + 1)
                if known(s, 4):
                    dve.wait_ge(up_done, s - 3)
                dve.tensor_copy(xT[0][:, k, :], xturn[:, :]).then_inc(x_high, 1)

            def take_x_low(s, k):
                dve.wait_ge(x_high, s + 1)
                dve.tensor_tensor(xT[1][:, k, :], xturn[:, :], xT[0][:, k, :].bitcast(F32), ALU.subtract
                                  ).then_inc(xT_ready, 1)

            def gate_hidden(s, par):
                dve.wait_ge(silu_ready, s + 1)
                if known(s, 2):
                    dve.wait_ge(h_turned, s - 1)
                dve.tensor_tensor(hidden[par][:, :], silu[par][:, :], gate[par][:, 0:W], ALU.mult
                                  ).then_inc(hidden_ready, 1)

            def take_down(s, k, qpar):
                if k == 0 and known(s, 8):
                    dve.wait_ge(y_stored[qpar], (s - 4 * qpar) * 2)
                dve.wait_ge(down_done, s + 1)
                dve.tensor_copy(yq[qpar][:, k, :], down[:, :]).then_inc(y_ready, 1)

            def add_result(n, i, par, r):
                if i == 0 and r == 0:
                    dve.wait_ge(fetched[par], (n - par) * (UNIT * 16) + 2 * UNIT * 16)
                if r == 1:
                    dve.wait_ge(added, n * UNIT + (i + 1))
                row = tokens[:, bass.ds(n * UNIT + i, 1), :].rearrange("p a c -> p (a c)")
                done = dve.scalar_tensor_tensor(
                    out=row, in0=fetch[par][:, i, r, :],
                    scalar=gates[:, bass.ds(n * UNIT + i, 1), r:r + 1].rearrange("p a b -> p (a b)"),
                    in1=row, op0=ALU.mult, op1=ALU.add)
                if r == 0:
                    done.then_inc(added, 1)
                elif i == UNIT - 1:
                    done.then_inc(fetch_used, 1)

            def step(s, k, qpar, ending=False, unit=None):
                more = not (ending and k == 3)
                if more:
                    take_x_high(s + 1, (k + 1) % 4)
                if unit:
                    add_result(unit[0], k, unit[1], 0)
                if known(s, 3):
                    take_down(s - 3, (k + 1) % 4, qpar if k == 3 else 1 - qpar)
                if more:
                    take_x_low(s + 1, (k + 1) % 4)
                if not kind.gelu:
                    gate_hidden(s, k % 2)
                if unit:
                    add_result(unit[0], k, unit[1], 1)

            take_x_high(0, 0)
            take_x_low(0, 0)
            for k in range(4):
                step(k, k, 0)
            for k in range(4):
                step(4 + k, k, 1)
            def pairs(start, end):
                if start == end:
                    return
                with dve.Fori(start, end - 7, 8) as s:
                    for k in range(8):
                        step(s + k, k % 4, k // 4)

            def pairs_adding(start, unit, n):
                with dve.Fori(0, 2 * n - 1, 2) as i:
                    for k in range(8):
                        step(i * 4 + (start + k), k % 4, k // 4, unit=(i + (unit + k // 4), k // 4))

            final = SLOT_TILES - 8
            pairs(8, FIRST_SLOT[1])
            waiting = 0
            for g in range(1, GROUPS):
                start, end = FIRST_SLOT[g], min(FIRST_SLOT[g + 1], final)
                pairs(start, start + 8)
                n = min(FIRST_UNIT[g] - waiting - 2 * (g == GROUPS - 1), (end - start - 8) // 4)
                assert n >= 0
                pairs_adding(start + 8, waiting, n // 2)
                waiting += n
                pairs(start + 8 + 4 * n, end)
            for k in range(8):
                step(final + k, k % 4, k // 4, ending=(k // 4 == 1), unit=(waiting + k // 4, k // 4))
            waiting += 2
            take_down(last - 2, 1, 1)
            take_down(last - 1, 2, 1)
            take_down(last, 3, 1)
            with dve.Fori(waiting, FIRST_UNIT[-1] - 1, 2) as n:
                for par in range(2):
                    for r in range(2):
                        for i in range(UNIT):
                            add_result(n + par, i, par, r)


class GeluSetup:

    def __init__(self, t, ins, ident, w_up, w_down, up_bias, down_bias, router, rbias, width):
        self.ins, self.ident, self.w_up, self.w_down = ins, ident, w_up, w_down
        self.placed_bias, self.router, self.rbias = (up_bias, down_bias), router, rbias
        self.chunks = width // P
        self.raw = t.sbuf("g_raw_up", [P, E, width])
        self.full = [t.sbuf(f"g_full{i}", [P, width]) for i in range(2)]
        self.scale = t.sbuf("g_scale", [P, E])
        self.shift = t.sbuf("g_shift", [P, E])
        rows = (E * self.chunks, E)
        self.bias = [t.sbuf(f"g_bias{m}", [rows[m], P]) for m in range(2)]
        self.parts = [[t.sbuf(f"g_part{i}{m}", [rows[m], P], BF16) for i in range(3)] for m in range(2)]
        self.extra = t.sbuf("g_extra", [P, rows[0]])
        self.extraT = t.sbuf("g_extraT", [rows[0], P])
        self.loaded = [t.sem(f"g_loaded{i}") for i in range(3)]
        self.extra_ready = t.sem("g_extra_ready")
        self.extra_taken = t.sem("g_extra_taken")
        self.extra_turned = t.sem("g_extra_turned")
        self.extraT_taken = t.sem("g_extraT_taken")
        self.highs = t.sem("g_highs")
        self.scaled = t.sem("g_scaled")
        self.lows = t.sem("g_lows")
        self.splits = t.sem("g_splits")
        self.parts_ready = t.sem("g_parts_ready")
        self.placed = t.sem("g_placed")

    def sync(self, sp):
        ins, loaded = self.ins, self.loaded
        sp.dma_start(self.router[:, :], ins["L2_ffn_Wr"]).then_inc(loaded[1], 16)
        sp.dma_start(self.shift[:, :], ins["L2_ffn_ln_b"].rearrange("e c -> c e"), allow_slow_non_contiguous=True
                     ).then_inc(loaded[0], 16)
        sp.dma_start(self.scale[:, :], ins["L2_ffn_ln_g"].rearrange("e c -> c e"), allow_slow_non_contiguous=True
                     ).then_inc(loaded[0], 16)
        sp.dma_start(self.raw[:, :, :], ins["L2_ffn_W1"].rearrange("e c h -> c e h")).then_inc(loaded[0], 16)
        sp.dma_start(self.bias[0][:, :], ins["L2_ffn_b1"].rearrange("e (k p) -> (e k) p", p=P)).then_inc(loaded[1], 16)
        sp.dma_start(self.bias[1][:, :], ins["L2_ffn_b2"]).then_inc(loaded[1], 16)
        sp.dma_start(self.rbias[:, :], row_to_all(ins["L2_ffn_br"])).then_inc(loaded[1], 16)
        sp.dma_start(self.w_down[:, :, :, :].rearrange("p e k c -> p (e k) c"),
                     ins["L2_ffn_W2"].rearrange("e (k p) c -> p (e k) c", p=P)).then_inc(loaded[2], 16)
        sp.wait_ge(self.parts_ready, 2)
        for i in range(3):
            for into, parts in zip(self.placed_bias, self.parts):
                sp.dma_start(into[i:i + 1, :, :].rearrange("a e h -> a (e h)"), parts[i][:, :]).then_inc(self.placed, 16)
        sp.wait_ge(self.placed, 6 * 16)
        sp.wait_ge(loaded[2], 16)

    def tensor(self, pe, bank, bankT):
        pe.wait_ge(self.loaded[0], 48)
        for e in range(E):
            for k in range(self.chunks):
                j = e * self.chunks + k
                done = pe.matmul(bank[:, j:j + 1], self.raw[:, e, P * k:P * k + P], self.shift[:, e:e + 1],
                                 start=True, stop=True)
        done.then_inc(self.extra_ready, 1)
        pe.wait_ge(self.extra_taken, 1)
        pe.transpose(bankT[0:E * self.chunks, 0:P], self.extra[:, :], self.ident[:, :]).then_inc(self.extra_turned, 1)
        pe.wait_ge(self.extraT_taken, 1)
        pe.wait_ge(self.loaded[1], 64)

    def scalar(self, act, bank, bankT):
        act.wait_ge(self.loaded[0], 48)
        for e in range(E):
            act.activation(self.w_up[0][:, e, :], self.raw[:, e, :], ACT.Identity, scale=self.scale[:, e:e + 1]
                           ).then_inc(self.highs, 1)
        act.wait_ge(self.extra_ready, 1)
        act.activation(self.extra[:, :], bank[:, 0:E * self.chunks], ACT.Copy).then_inc(self.extra_taken, 1)
        act.wait_ge(self.extra_turned, 1)
        act.activation(self.extraT[:, :], bankT[0:E * self.chunks, 0:P], ACT.Copy).then_inc(self.extraT_taken, 1)

    def gpsimd(self, pool):
        steps = Steps(pool, self.splits)
        for e in range(E):
            full = self.full[e % 2]
            pool.wait_ge(self.highs, e + 1)
            if e >= 2:
                pool.wait_ge(self.lows, e - 1)
            pool.tensor_tensor(full[:, :], self.raw[:, e, :], self.scale[:, e:e + 1].to_broadcast(full.shape), ALU.mult
                               ).then_inc(self.scaled, 1)
            pool.wait_ge(self.scaled, e + 1)
            pool.tensor_tensor(self.w_up[1][:, e, :], full[:, :], self.w_up[0][:, e, :].bitcast(F32), ALU.subtract
                               ).then_inc(self.lows, 1)
        pool.wait_ge(self.loaded[1], 64)
        pool.wait_ge(self.extraT_taken, 1)
        steps.then(pool.tensor_tensor(self.bias[0][:, :], self.bias[0][:, :], self.extraT[:, :], ALU.add))
        for i in range(3):
            for m in range(2):
                done = pool.tensor_copy(self.parts[m][i][:, :], self.bias[m][:, :])
                if i < 2:
                    steps.did(done)
                else:
                    done.then_inc(self.parts_ready, 1)
            if i < 2:
                steps.settle()
                for m in range(2):
                    steps.did(pool.tensor_tensor(self.bias[m][:, :], self.bias[m][:, :], self.parts[m][i][:, :],
                                                 ALU.subtract))
                steps.settle()


def experts_gelu(nc, ins, ident, tokens, sorted_rows, sorted_results):
    kind = Expert("gelu", 512)
    W = kind.width
    with ExitStack() as ctx:
        t = Tools(nc, ctx)
        gates = t.sbuf("g_gates", [P, TT, 2])
        places = t.sbuf("g_places", [P, TT, 2], I32)
        owner = t.sbuf("g_owner", [1, SLOT_TILES // 8], I32)
        w_up = [t.sbuf(f"g_w_up_{part}", [P, E, W], F32R) for part in ("high", "low")]
        w_down = t.sbuf("g_w_down", [P, E, W // P, C])
        up_bias = t.sbuf("g_up_bias", [3, E, W], BF16)
        down_bias = t.sbuf("g_down_bias", [3, E, C], BF16)
        normed = t.sbuf("g_normed", [P, TT, C])
        with ExitStack() as routing:
            t = Tools(nc, routing)
            router = t.sbuf("g_router", [P, E])
            rbias = t.sbuf("g_rbias", [P, E])
            masks = [t.sbuf(f"g_mask{i}", [P, TT, E]) for i in range(2)]
            setup = GeluSetup(t, ins, ident, w_up, w_down, up_bias, down_bias, router, rbias, W)
            route(nc, kind, router, rbias, ident, tokens, normed, masks, gates, places, owner, "gr_", setup)
        run_experts(nc, kind, w_up, None, w_down, up_bias, down_bias, ident, tokens, normed, gates, places,
                    owner, sorted_rows, sorted_results, "gx_")



WINDOW = 32
SHIFT = WINDOW // 2
HEADS3 = 4
HD = C // HEADS3
CW = HALF // WINDOW
MASKED = -1.0e30


def window_attention(nc, ins, ident, tokens):
    with ExitStack() as ctx:
        t = Tools(nc, ctx)
        rows = t.sbuf("w_rows", [P, 4, C])
        wT = t.sbuf("w_wT", [P, 4, C])
        qbias = t.sbuf("w_qbias", [P, 3])
        obias = t.sbuf("w_obias", [P, C])
        toeplitz = t.sbuf("w_toeplitz", [P, WINDOW])
        bias = t.sbuf("w_bias", [P, WINDOW])
        last_bias = t.sbuf("w_last_bias", [P, CW, WINDOW])
        norm = TokenNorm(t, "w_")
        u = t.sbuf("w_u", [P, NT, C])
        uT = [t.sbuf(f"w_uT{i}", [P, N + SHIFT]) for i in range(2)]
        qT = [t.sbuf(f"w_qT{i}", [P, HALF]) for i in range(2)]
        kT = [t.sbuf(f"w_kT{i}", [P, HALF]) for i in range(2)]
        vs = [t.sbuf(f"w_vs{i}", [P, HALF]) for i in range(4)]
        logit = [t.sbuf(f"w_logit{i}", [P, CW, WINDOW]) for i in range(2)]
        top = [t.sbuf(f"w_top{i}", [P, CW]) for i in range(2)]
        prob = [t.sbuf(f"w_prob{i}", [P, CW, WINDOW]) for i in range(2)]
        total = [t.sbuf(f"w_total{i}", [P, CW]) for i in range(2)]
        pT = [t.sbuf(f"w_pT{i}", [P, HALF]) for i in range(2)]
        oT = [t.sbuf(f"w_oT{i}", [P, SHIFT + N]) for i in range(2)]
        turn = [t.psum(f"w_turn{i}", [P, HALF]) for i in range(2)]
        proj = [t.psum(f"w_proj{i}", [P, HALF]) for i in range(3)]
        score = t.psum("w_score", [P, HALF])
        mixed = t.psum("w_mixed", [P, HALF])
        result = t.psum("w_result", [P, HALF])

        loaded = t.sem("w_loaded")
        turned = t.sem("w_turned")
        weights_ready = t.sem("w_weights_ready")
        pool_steps = t.sem("w_pool_steps")
        masks_ready = t.sem("w_masks_ready")
        setup = t.sem("w_setup")
        table_ready = t.sem("w_table_ready")
        u_ready = t.sem("w_u_ready")
        turn_ready = t.sem("w_turn_ready")
        uT_ready = t.sem("w_uT_ready")
        prepared = t.sem("w_prepared")
        result_ready = t.sem("w_result_ready")
        result_taken = t.sem("w_result_taken")
        proj_ready = t.sem("w_proj_ready")
        q_taken = t.sem("w_q_taken")
        k_taken = t.sem("w_k_taken")
        v_taken = t.sem("w_v_taken")
        score_ready = t.sem("w_score_ready")
        score_taken = t.sem("w_score_taken")
        pre_steps = t.sem("w_pre_steps")
        shifted = t.sem("w_shifted")
        exp_done = t.sem("w_exp_done")
        post_steps = t.sem("w_post_steps")
        pT_ready = t.sem("w_pT_ready")
        mixed_ready = t.sem("w_mixed_ready")
        mixed_taken = t.sem("w_mixed_taken")
        block = ctx.enter_context(nc.Block())
        loads = 8 + HEADS3

        def batches(engine, step, turn_first, norm_of=None):
            turn_first()
            for b in range(2):
                for h in range(2):
                    step(b, h, b)
                    pair = 2 * b + h + 1
                    if norm_of and 2 * pair < B:
                        norm_of(2 * pair, 2 * pair + 2)
            with engine.Fori(2, B - 3, 2) as b:
                for par in range(2):
                    for h in range(2):
                        step(b + par, h, par)
            for b in (B - 2, B - 1):
                for h in range(2):
                    step(b, h, b % 2)

        def known(x, least):
            return not isinstance(x, int) or x >= least

        @block.sync
        def _(sp):
            for i in range(3):
                sp.dma_start(rows[:, i, :], ins["L3_attn_w_qkv"][P * i:P * i + P, :]).then_inc(loaded, 16)
                sp.dma_start(qbias[:, i:i + 1], ins["L3_attn_b_qkv"][P * i:P * i + P].rearrange("(c a) -> c a", a=1)
                             ).then_inc(loaded, 16)
            sp.dma_start(rows[:, 3, :], ins["L3_attn_w_out"]).then_inc(loaded, 16)
            sp.dma_start(obias[:, :], row_to_all(ins["L3_attn_b_out"])).then_inc(loaded, 16)
            rel = ins["L3_attn_rel_pos"]
            for h in range(HEADS3):
                windows = bass.AP(tensor=rel.tensor, offset=h * (2 * WINDOW - 1), ap=[[1, WINDOW], [1, WINDOW]])
                sp.dma_start(toeplitz[WINDOW * h:WINDOW * h + WINDOW, :], windows).then_inc(loaded, 16)

        @block.gpsimd
        def _(pool):
            steps = Steps(pool, pool_steps)
            pool.wait_ge(table_ready, 1)
            steps.then(pool.tensor_copy(last_bias[:, :, :], bias[:, :].unsqueeze(1).to_broadcast([P, CW, WINDOW])))
            for h in range(HEADS3):
                part = slice(WINDOW * h, WINDOW * h + WINDOW)
                pool.affine_select(out=last_bias[part, CW - 1, SHIFT:], in_=last_bias[part, CW - 1, SHIFT:],
                                   compare_op=ALU.is_ge, fill=MASKED, base=-SHIFT,
                                   pattern=[[0, WINDOW - SHIFT]], channel_multiplier=1).then_inc(masks_ready, 1)
                pool.affine_select(out=last_bias[part, CW - 1, 0:SHIFT], in_=last_bias[part, CW - 1, 0:SHIFT],
                                   compare_op=ALU.is_ge, fill=MASKED, base=SHIFT - 1,
                                   pattern=[[0, SHIFT]], channel_multiplier=-1).then_inc(masks_ready, 1)

            def prepare(b):
                pool.wait_ge(u_ready, b + 1)
                batch = tokens[:, bass.ds(b * NT, NT), :]
                pool.tensor_tensor(batch, batch, obias[:, :].unsqueeze(1).to_broadcast([P, NT, C]), ALU.add
                                   ).then_inc(prepared, 1)
            pool.wait_ge(loaded, 16 * loads)
            with pool.Fori(0, B) as b:
                prepare(b)

        @block.tensor
        def _(pe):
            pe.wait_ge(loaded, 16 * loads)
            for i in range(4):
                done = pe.transpose(turn[0][:, P * i:P * i + P], rows[:, i, :], ident[:, :])
            done.then_inc(turned, 1)
            pe.wait_ge(weights_ready, 1)

            def turn_batch(b):
                pe.wait_ge(u_ready, b + 1)
                if known(b, 1):
                    pe.wait_ge(uT_ready, b)
                for j in range(NT):
                    done = pe.transpose(turn[j // 4][:, P * (j % 4):P * (j % 4) + P], u[:, j, :], ident[:, :])
                done.then_inc(turn_ready, 1)

            def project(b, h, par):
                pe.wait_ge(uT_ready, b + 1)
                for i, taken in enumerate((q_taken, k_taken, v_taken)):
                    if known(b, 1) or h == 1:
                        pe.wait_ge(taken, b * 2 + h)
                    at = SHIFT + HALF * h
                    pe.matmul(proj[i][:, :], wT[:, i, :], uT[par][:, at:at + HALF], start=True, stop=True
                              ).then_inc(proj_ready, 1)

            score_goal, mix_goal = (pe.alloc_register(f"w_{name}_goal") for name in ("score", "mix"))
            pe.reg_mov(score_goal, 1)
            pe.reg_mov(mix_goal, 1)

            def by_window(out, left, right):
                for w in range(CW):
                    at = slice(WINDOW * w, WINDOW * w + WINDOW)
                    for i in range(HEADS3):
                        part = slice(HD * i, HD * i + HD)
                        done = pe.matmul(out[part, at], left[part, at], right[part, at], start=True, stop=True)
                return done

            def scores(b, h):
                pe.wait_ge(q_taken, b * 2 + h + 1)
                if known(b, 1) or h == 1:
                    pe.wait_ge(score_taken, b * 2 + h)
                pe.wait_ge(k_taken, score_goal)
                pe.reg_add(score_goal, score_goal, 1)
                done = by_window(score, qT[h], kT[h])
                done.then_inc(score_ready, 1)

            def mix(b, h, par):
                pe.wait_ge(v_taken, b * 2 + h + 1)
                if known(b, 1) or h == 1:
                    pe.wait_ge(mixed_taken, b * 2 + h)
                pe.wait_ge(pT_ready, mix_goal)
                pe.reg_add(mix_goal, mix_goal, 1)
                done = by_window(mixed, vs[2 * par + h], pT[h])
                done.then_inc(mixed_ready, 1)

            def give(b, par, half):
                pe.wait_ge(mixed_taken, b * 2 + 2)
                if known(b, 1) or half == 1:
                    pe.wait_ge(result_taken, b * 2 + half)
                for j in range(4):
                    at = P * (4 * half + j)
                    done = pe.matmul(result[:, P * j:P * j + P], oT[par][:, at:at + P], wT[:, 3, :],
                                     start=True, stop=True)
                done.then_inc(result_ready, 1)

            def step(b, h, par):
                project(b, h, par)
                if h == 0 and known(b, 2):
                    give(b - 2, par, 0)
                if h == 1:
                    scores(b, 0)
                elif known(b, 1):
                    scores(b - 1, 1)
                if h == 0 and known(b, 2):
                    give(b - 2, par, 1)
                if known(b, 1):
                    mix(b - 1, h, 1 - par)
                if h == 0 and not (isinstance(b, int) and b == B - 1):
                    turn_batch(b + 1)

            batches(pe, step, lambda: turn_batch(0))
            for half in range(2):
                give(B - 2, 0, half)
            scores(B - 1, 1)
            mix(B - 1, 0, 1)
            mix(B - 1, 1, 1)
            for half in range(2):
                give(B - 1, 1, half)

        @block.scalar
        def _(act):
            norm.root_of(act, 0, 2)
            act.wait_ge(table_ready, 1)

            def take_turned(b, par):
                act.wait_ge(turn_ready, b + 1)
                for h in range(2):
                    act.activation(uT[par][:, HALF * h:HALF * h + HALF], turn[h][:, :], ACT.Copy)
                act.activation(uT[par][:, N:N + SHIFT], turn[0][:, 0:SHIFT], ACT.Copy).then_inc(uT_ready, 1)

            def take_qk(b, h):
                act.wait_ge(proj_ready, (b * 2 + h) * 3 + 1)
                if known(b, 1):
                    act.wait_ge(score_ready, b * 2 + h - 1)
                act.activation(qT[h][:, :], proj[0][:, :], ACT.Identity, bias=qbias[:, 0:1], scale=HD ** -0.5
                               ).then_inc(q_taken, 1)
                act.wait_ge(proj_ready, (b * 2 + h) * 3 + 2)
                act.activation(kT[h][:, :], proj[1][:, :], ACT.Identity, bias=qbias[:, 1:2]).then_inc(k_taken, 1)

            def exponent(b, h):
                act.wait_ge(shifted, b * 2 + h + 1)
                act.activation(prob[h][:, :, :], logit[h][:, :, :], ACT.Exp).then_inc(exp_done, 1)

            def take_mixed(b, h, par):
                act.wait_ge(mixed_ready, b * 2 + h + 1)
                if known(b, 2):
                    act.wait_ge(result_ready, b * 2 - 2)
                at = SHIFT + HALF * h
                done = act.activation(oT[par][:, at:at + HALF], mixed[:, :], ACT.Identity, bias=qbias[:, 2:3])
                if h == 1:
                    done = act.activation(oT[par][:, 0:SHIFT], mixed[:, HALF - SHIFT:], ACT.Identity, bias=qbias[:, 2:3])
                done.then_inc(mixed_taken, 1)

            def step(b, h, par):
                take_qk(b, h)
                if h == 1:
                    exponent(b, 0)
                elif known(b, 1):
                    exponent(b - 1, 1)
                if known(b, 1):
                    take_mixed(b - 1, h, 1 - par)
                if h == 0 and not (isinstance(b, int) and b == B - 1):
                    take_turned(b + 1, 1 - par)

            def start():
                take_turned(0, 0)

            batches(act, step, start, lambda *pair: norm.root_of(act, *pair))
            exponent(B - 1, 1)
            take_mixed(B - 1, 0, 1)
            take_mixed(B - 1, 1, 1)

        @block.vector
        def _(dve):
            norm.run(dve, tokens, 0, 2)
            steps = Steps(dve, setup)
            dve.wait_ge(turned, 1)
            dve.tensor_copy(wT[:, :, :].rearrange("p i c -> p (i c)"), turn[0][:, :]).then_inc(weights_ready, 1)
            dve.wait_ge(loaded, 16 * loads)
            steps.then(dve.tensor_scalar(qbias[:, 0:1], qbias[:, 0:1], HD ** -0.5, None, ALU.mult))
            for q in range(WINDOW):
                done = dve.tensor_copy(bias[:, q:q + 1], toeplitz[:, WINDOW - 1 - q:WINDOW - q])
            done.then_inc(table_ready, 1)
            dve.wait_ge(table_ready, 1)

            pre = Steps(dve, pre_steps)
            post = Steps(dve, post_steps)

            def normalise(b):
                if known(b, 1):
                    dve.wait_ge(turn_ready, b)
                norm.apply(dve, tokens, b, u).then_inc(u_ready, 1)

            def take_v(b, h, par):
                dve.wait_ge(proj_ready, (b * 2 + h) * 3 + 3)
                if known(b, 2):
                    dve.wait_ge(mixed_ready, b * 2 + h - 3)
                dve.transpose(vs[2 * par + h][:, :], proj[2][:, :]).then_inc(v_taken, 1)

            def before_exp(b, h):
                pre.round(b * 2 + h)
                dve.wait_ge(score_ready, b * 2 + h + 1)
                table = last_bias[:, :, :] if h == 1 else bias[:, :].unsqueeze(1).to_broadcast([P, CW, WINDOW])
                dve.tensor_tensor(logit[h][:, :, :], score[:, :].rearrange("p (w q) -> p w q", w=CW), table, ALU.add
                                  ).then_inc(score_taken, 1)
                dve.wait_ge(score_taken, b * 2 + h + 1)
                pre.then(dve.tensor_reduce(top[h][:, :], logit[h][:, :, :], AX.X, ALU.max))
                dve.tensor_tensor(logit[h][:, :, :], logit[h][:, :, :],
                                  top[h][:, :].unsqueeze(2).to_broadcast([P, CW, WINDOW]), ALU.subtract
                                  ).then_inc(shifted, 1)

            def after_exp(b, h):
                post.round(b * 2 + h)
                dve.wait_ge(exp_done, b * 2 + h + 1)
                post.then(dve.tensor_reduce(total[h][:, :], prob[h][:, :, :], AX.X, ALU.add))
                post.then(dve.reciprocal(total[h][:, :], total[h][:, :]))
                post.then(dve.tensor_tensor(prob[h][:, :, :], prob[h][:, :, :],
                                            total[h][:, :].unsqueeze(2).to_broadcast([P, CW, WINDOW]), ALU.mult))
                if known(b, 1):
                    dve.wait_ge(mixed_ready, b * 2 + h - 1)
                dve.transpose(pT[h][:, :], prob[h][:, :, :].rearrange("p w q -> p (w q)")).then_inc(pT_ready, 1)

            def add(b, half):
                dve.wait_ge(prepared, b + 1)
                dve.wait_ge(result_ready, b * 2 + half + 1)
                rows4 = tokens[:, bass.ds(b * NT + 4 * half, 4), :]
                dve.tensor_tensor(rows4, rows4, result[:, :].rearrange("p (a c) -> p a c", a=4), ALU.add
                                  ).then_inc(result_taken, 1)

            def step(b, h, par):
                if known(b, 1):
                    after_exp(b - 1, h)
                take_v(b, h, par)
                if h == 0 and known(b, 2):
                    add(b - 2, 0)
                if h == 1:
                    before_exp(b, 0)
                elif known(b, 1):
                    before_exp(b - 1, 1)
                if h == 0 and known(b, 2):
                    add(b - 2, 1)
                if h == 0 and not (isinstance(b, int) and b == B - 1):
                    normalise(b + 1)

            dve.wait_ge(masks_ready, 2 * HEADS3)
            batches(dve, step, lambda: normalise(0), lambda *pair: norm.run(dve, tokens, *pair))
            for half in range(2):
                add(B - 2, half)
            after_exp(B - 1, 0)
            before_exp(B - 1, 1)
            after_exp(B - 1, 1)
            for half in range(2):
                add(B - 1, half)


class SiluSetup:

    def __init__(self, t, ins, ident, w_up, w_gate, w_down, router, kind):
        self.ins, self.ident, self.kind = ins, ident, kind
        self.split, self.w_down, self.router = (w_up, w_gate), w_down, router
        self.at_last, self.rest = kind.chunks[-1]
        self.K = len(kind.chunks) - 1
        self.raw = [t.sbuf(f"s_raw{i}", [P, E, self.K + 1, C]) for i in range(2)]
        self.raw_down = t.sbuf("s_raw_down", [P, E, kind.width])
        self.raw_router = t.sbuf("s_raw_router", [E, C])
        self.full = [t.sbuf(f"s_full{i}", [P, kind.even]) for i in range(4)]
        self.loaded = [t.sem(f"s_loaded{i}") for i in range(3)]
        self.cleared = t.sem("s_cleared")
        self.turned = t.sem("s_turned")
        self.taken = t.sem("s_taken")
        self.highs = t.sem("s_highs")
        self.lows = t.sem("s_lows")
        self.jobs = [(m, e) for m in range(3) for e in range(E)]

    def sync(self, sp):
        ins, K = self.ins, self.K
        sp.wait_ge(self.cleared, 2)
        for m, name in enumerate(("L3_ffn_w1", "L3_ffn_w3")):
            sp.dma_start(self.raw[m][0:self.rest, :, K, :], ins[name][:, self.at_last:, :].rearrange("e p c -> p e c")
                         ).then_inc(self.loaded[m], 16)
            for k in range(K):
                sp.dma_start(self.raw[m][:, :, k, :], ins[name][:, P * k:P * k + P, :].rearrange("e p c -> p e c")
                             ).then_inc(self.loaded[m], 16)
        sp.dma_start(self.raw_down[:, :, :], ins["L3_ffn_w2"].rearrange("e c h -> c e h")).then_inc(self.loaded[2], 16)
        sp.dma_start(self.raw_router[:, :], ins["L3_ffn_router_w"]).then_inc(self.loaded[2], 16)
        sp.wait_ge(self.loaded[2], 32)

    def tensor(self, pe, *banks):
        K, ident = self.K, self.ident
        for n, (m, e) in enumerate(self.jobs):
            if e == 0:
                pe.wait_ge(self.loaded[m], 32 if m == 2 else 16 * (K + 1))
            if n >= 2:
                pe.wait_ge(self.taken, n - 1)
            bank = banks[n % 2]
            for k in range(K):
                part = self.raw_down[:, e, P * k:P * k + P] if m == 2 else self.raw[m][:, e, k, :]
                pe.transpose(bank[:, P * k:P * k + P], part, ident[:, :])
            if m == 2:
                done = pe.transpose(bank[0:self.rest, P * K:P * K + P], self.raw_down[:, e, self.at_last:], ident[:, :])
            else:
                width = self.kind.even - self.at_last
                done = pe.transpose(bank[:, self.at_last:self.kind.even], self.raw[m][0:width, e, K, :],
                                    ident[0:width, 0:width])
            done.then_inc(self.turned, 1)
        pe.wait_ge(self.taken, len(self.jobs) - 1)
        pe.transpose(banks[len(self.jobs) % 2][:, 0:E], self.raw_router[:, :], ident[0:E, 0:E]).then_inc(self.turned, 1)
        pe.wait_ge(self.taken, len(self.jobs) + 1)

    def scalar(self, act, *banks):
        K = self.K
        for n, (m, e) in enumerate(self.jobs):
            bank = banks[n % 2]
            act.wait_ge(self.turned, n + 1)
            if m == 2:
                act.activation(self.w_down[:, e, 0:K, :], bank[:, 0:P * K].rearrange("p (k c) -> p k c", c=C), ACT.Copy)
                act.activation(self.w_down[0:self.rest, e, K, :], bank[0:self.rest, P * K:P * K + P], ACT.Copy
                               ).then_inc(self.taken, 1)
            else:
                if n >= 4:
                    act.wait_ge(self.lows, n - 3)
                act.activation(self.full[n % 4][:, :], bank[:, 0:self.kind.even], ACT.Copy).then_inc(self.taken, 1)
                act.wait_ge(self.taken, n + 1)
                act.activation(self.split[m][0][:, e, :], self.full[n % 4][:, :], ACT.Copy).then_inc(self.highs, 1)
        act.wait_ge(self.turned, len(self.jobs) + 1)
        act.activation(self.router[:, :], banks[len(self.jobs) % 2][:, 0:E], ACT.Copy).then_inc(self.taken, 1)

    def gpsimd(self, pool):
        low = self.rest // 32 * 32
        for m in range(2):
            pool.memset(self.raw[m][low:low + 32, :, self.K, :], 0.0).then_inc(self.cleared, 1)
        for n, (m, e) in enumerate(self.jobs[0:2 * E]):
            pool.wait_ge(self.highs, n + 1)
            high, into = self.split[m][0], self.split[m][1]
            pool.tensor_tensor(into[:, e, :], self.full[n % 4][:, :], high[:, e, :].bitcast(F32), ALU.subtract
                               ).then_inc(self.lows, 1)


def experts_silu(nc, ins, ident, tokens, sorted_rows, sorted_results):
    kind = Expert("silu", 341)
    with ExitStack() as ctx:
        t = Tools(nc, ctx)
        gates = t.sbuf("s_gates", [P, TT, 2])
        places = t.sbuf("s_places", [P, TT, 2], I32)
        owner = t.sbuf("s_owner", [1, SLOT_TILES // 8], I32)
        w_up, w_gate = ([t.sbuf(f"s_w_{name}_{part}", [P, E, kind.even], F32R) for part in ("high", "low")]
                        for name in ("up", "gate"))
        w_down = t.sbuf("s_w_down", [P, E, len(kind.chunks), C])
        normed = t.sbuf("s_normed", [P, TT, C])
        with ExitStack() as routing:
            t = Tools(nc, routing)
            router = t.sbuf("s_router", [P, E])
            masks = [t.sbuf(f"s_mask{i}", [P, TT, E]) for i in range(2)]
            setup = SiluSetup(t, ins, ident, w_up, w_gate, w_down, router, kind)
            route(nc, kind, router, None, ident, tokens, normed, masks, gates, places, owner, "sr_", setup)
        run_experts(nc, kind, w_up, w_gate, w_down, None, None, ident, tokens, normed, gates, places,
                    owner, sorted_rows, sorted_results, "sx_")


INPUTS = ['x', 'L0_conv_Wq', 'L0_conv_bq', 'L0_conv_Wk', 'L0_conv_bk', 'L0_conv_Wv', 'L0_conv_bv',
          'L0_conv_gamma', 'L1_conv_weight', 'L1_conv_bias', 'L2_attn_kln_weight', 'L2_attn_kln_bias',
          'L2_attn_vln_weight', 'L2_attn_vln_bias', 'L2_ffn_Wr', 'L2_ffn_br', 'L2_ffn_ln_g', 'L2_ffn_ln_b',
          'L2_ffn_W1', 'L2_ffn_b1', 'L2_ffn_W2', 'L2_ffn_b2', 'L3_attn_w_qkv', 'L3_attn_b_qkv',
          'L3_attn_rel_pos', 'L3_attn_w_out', 'L3_attn_b_out', 'L3_ffn_router_w', 'L3_ffn_w1', 'L3_ffn_w2',
          'L3_ffn_w3']


def build(nc, ins, out, sorted_rows, sorted_results):
    with ExitStack() as ctx:
        t = Tools(nc, ctx)
        ident = t.sbuf("ident", [P, P])
        tokens = t.sbuf("tokens", [P, TT, C])
        made = t.sem("made")
        with nc.Block() as block:
            @block.gpsimd
            def _(pool):
                make_identity(pool, Steps(pool, made), ident[:, :])
        with ExitStack() as early:
            t = Tools(nc, early)
            feats = t.sbuf("feats", [P, B, N])
            stats = t.sbuf("stats", [P, 2 * B, 6])
            conv_attention(nc, ins, ident, feats, stats, sorted_rows)
            whiten(nc, ins, ident, feats, stats, tokens)
        linear_attention(nc, ins, ident, tokens)
        experts_gelu(nc, ins, ident, tokens, sorted_rows, sorted_results)
        window_attention(nc, ins, ident, tokens)
        experts_silu(nc, ins, ident, tokens, sorted_rows, sorted_results)
        store_images(nc, ident, tokens, out)


def kernel(**inputs):
    import numpy as np
    import concourse.bacc as bacc
    from concourse.bass_utils import run_bass_kernel_spmd

    nc = bacc.Bacc("TRN2", target_bir_lowering=False, num_devices=1)
    arrays, ins = {}, {}
    for name in INPUTS:
        a = np.ascontiguousarray(inputs[name])
        arrays[f"in_{name}"] = a
        ins[name] = nc.dram_tensor(f"in_{name}", a.shape, mybir.dt.from_np(a.dtype), kind="ExternalInput").ap()
    out = nc.dram_tensor("out", (B, C, 32, 32), F32, kind="ExternalOutput").ap()
    sorted_rows, sorted_results = ([nc.dram_tensor(f"sorted_{what}{g}", (n * P, C), F32, kind="Internal").ap()
                                    for g, n in enumerate(GROUP_SLOT_TILES)] for what in ("rows", "results"))
    build(nc, ins, out, sorted_rows, sorted_results)
    r = run_bass_kernel_spmd(nc, [arrays], core_ids=[0])
    return r.results[0]["out"]
```
